# Optimizing a Trainium2 kernel written in Bass

```python
import numpy as np
import jax
import jax.numpy as jnp

def _softmax(x, axis=-1):
    return jax.nn.softmax(x, axis=axis)

def _gelu(x):
    return jax.nn.gelu(x, approximate=True)

def _silu(x):
    return jax.nn.silu(x)

def _sigmoid(x):
    return jax.nn.sigmoid(x)

def _layernorm(x, axis=-1, eps=1e-05):
    m = jnp.mean(x, axis=axis, keepdims=True)
    v = jnp.var(x, axis=axis, keepdims=True)
    return (x - m) / jnp.sqrt(v + eps)

def _scatter_add(tgt, idx, src, axis=0):
    return tgt.at[idx].add(src)

def _segment_sum(src, seg, n):
    return jax.ops.segment_sum(src, seg, n)
kernel_name = 'mk_gnn_preln_d4_gnn_r8_e9ac5d'

def setup_inputs(seed: int=0):
    np.random.seed(seed)
    _w = jnp.asarray

    def _rec_inputs():
        import jax
        import jax.numpy as jnp
        _gk = jax.random.key(seed)
        x = -0.000202 + 1 * jax.random.normal(jax.random.fold_in(_gk, 1), (12500, 64), jnp.float32)
        _s = jax.random.randint(jax.random.fold_in(_gk, 2), (100000,), 0, 12500, jnp.int32)
        _d = jax.random.randint(jax.random.fold_in(_gk, 3), (100000,), 0, 12500, jnp.int32)
        _loop = jnp.arange(12500, dtype=jnp.int32)
        src = jnp.concatenate([_s, _d, _loop])
        dst = jnp.concatenate([_d, _s, _loop])
        _o = jnp.argsort(dst, stable=True)
        src = src[_o]
        dst = dst[_o]
        edge_attr_16 = -0.00010739 + 0.99994 * jax.random.normal(jax.random.fold_in(_gk, 12), (212500, 16), jnp.float32)
        edge_weight = jax.random.uniform(jax.random.fold_in(_gk, 14), (212500,), jnp.float32, 0.0, 1)
        return (x, src, dst, edge_attr_16, edge_weight)
    x, src, dst, edge_attr_16, edge_weight = _rec_inputs()

    def _L0_gnn_setup():
        import jax, jax.numpy as jnp
        import numpy as np
        NEG_SLOPE = 0.2
        key = jax.random.key(seed)
        ks = jax.random.split(key, 5)
        N, E, Din, Dout = (12500, 200000, 64, 64)
        x = jax.random.normal(ks[0], (N, Din), dtype=jnp.float32)
        edge_index = jax.random.randint(ks[1], (2, E), 0, N, dtype=jnp.int64)
        W_l = jax.random.normal(ks[2], (Din, Dout), dtype=jnp.float32) / np.sqrt(Din)
        W_r = jax.random.normal(ks[3], (Din, Dout), dtype=jnp.float32) / np.sqrt(Din)
        att = jax.random.normal(ks[4], (Dout,), dtype=jnp.float32) / np.sqrt(Dout)
        bias = jnp.zeros((Dout,), dtype=jnp.float32)
        return {'x': x, 'edge_index': edge_index, 'W_l': W_l, 'W_r': W_r, 'att': att, 'bias': bias}
    _L0_gnn_all = _L0_gnn_setup()
    _L0_gnn_in = {k: v for k, v in _L0_gnn_all.items() if k in ('W_l', 'W_r', 'att', 'bias')}
    del _L0_gnn_all

    def _L1_gnn_setup():
        import jax, jax.numpy as jnp
        import numpy as np
        N = 12500
        NNZ = 200000
        D = 64
        key = jax.random.key(seed)
        k1, k2, k3, k4 = jax.random.split(key, 4)
        x = jax.random.normal(k1, (N, D), dtype=jnp.float32)
        row = jax.random.randint(k2, (NNZ,), 0, N, dtype=jnp.int64)
        col = jax.random.randint(k3, (NNZ,), 0, N, dtype=jnp.int64)
        value = jax.random.uniform(k4, (NNZ,), dtype=jnp.float32)
        return {'x': x, 'row': row, 'col': col, 'value': value, 'size': N}
    _L1_gnn_all = _L1_gnn_setup()
    _L1_gnn_in = {k: v for k, v in _L1_gnn_all.items() if k in ()}
    del _L1_gnn_all

    def _L2_gnn_setup():
        import jax, jax.numpy as jnp
        import numpy as np
        N = 6250
        E = 100000
        D = 64
        ED = 16
        H = 64
        CIN = 2 * D + ED

        def _he(key, shape):
            return jax.random.normal(key, shape, jnp.float32) * jnp.sqrt(2.0 / shape[0])

        def _layer_norm(x, g, b, eps=1e-06):
            mu = jnp.mean(x, axis=-1, keepdims=True)
            var = jnp.var(x, axis=-1, keepdims=True)
            return (x - mu) * jax.lax.rsqrt(var + eps) * g + b
        key = jax.random.key(seed)
        ks = jax.random.split(key, 8)
        nodes = jax.random.normal(ks[0], (N, D), jnp.float32)
        edges = jax.random.normal(ks[1], (E, ED), jnp.float32)
        senders = jax.random.randint(ks[2], (E,), 0, N, jnp.int32)
        receivers = jax.random.randint(ks[3], (E,), 0, N, jnp.int32)
        return {'nodes': nodes, 'edges': edges, 'senders': senders, 'receivers': receivers, 'Wq': _he(ks[4], (CIN, H)), 'bq': jnp.zeros((H,), jnp.float32), 'W0': _he(ks[5], (CIN, H)), 'b0': jnp.zeros((H,), jnp.float32), 'g0': jnp.ones((H,), jnp.float32), 'beta0': jnp.zeros((H,), jnp.float32), 'W1': _he(ks[6], (H, H)), 'b1': jnp.zeros((H,), jnp.float32), 'g1': jnp.ones((H,), jnp.float32), 'beta1': jnp.zeros((H,), jnp.float32), 'Wf': _he(ks[7], (H, 1)), 'bf': jnp.zeros((1,), jnp.float32)}
    _L2_gnn_all = _L2_gnn_setup()
    _L2_gnn_in = {k: v for k, v in _L2_gnn_all.items() if k in ('Wq', 'bq', 'W0', 'b0', 'g0', 'beta0', 'W1', 'b1', 'g1', 'beta1', 'Wf', 'bf')}
    del _L2_gnn_all

    def _L3_gnn_setup():
        import jax, jax.numpy as jnp
        import numpy as np
        key = jax.random.key(seed)
        k1, k2, k3, k4, k5 = jax.random.split(key, 5)
        N, E, C_in, C_out = (12500, 200000, 64, 64)
        x = jax.random.normal(k1, (N, C_in), dtype=jnp.float32)
        edge_index = jax.random.randint(k2, (2, E), 0, N, dtype=jnp.int64)
        edge_weight = jax.random.uniform(k3, (E,), dtype=jnp.float32)
        bound = float(np.sqrt(6.0 / (C_in + C_out)))
        W_self = jax.random.uniform(k4, (C_out, C_in), dtype=jnp.float32, minval=-bound, maxval=bound)
        W_neigh = jax.random.uniform(k5, (C_out, C_in), dtype=jnp.float32, minval=-bound, maxval=bound)
        b_self = jnp.zeros((C_out,), dtype=jnp.float32)
        b_neigh = jnp.zeros((C_out,), dtype=jnp.float32)
        return {'x': x, 'edge_index': edge_index, 'edge_weight': edge_weight, 'W_self': W_self, 'b_self': b_self, 'W_neigh': W_neigh, 'b_neigh': b_neigh, 'num_nodes': N}
    _L3_gnn_all = _L3_gnn_setup()
    _L3_gnn_in = {k: v for k, v in _L3_gnn_all.items() if k in ('W_self', 'b_self', 'W_neigh', 'b_neigh')}
    del _L3_gnn_all
    return {'x': x, 'src': src, 'dst': dst, 'edge_attr_16': edge_attr_16, 'edge_weight': edge_weight, 'L0_gnn_W_l': _L0_gnn_in['W_l'], 'L0_gnn_W_r': _L0_gnn_in['W_r'], 'L0_gnn_att': _L0_gnn_in['att'], 'L0_gnn_bias': _L0_gnn_in['bias'], 'L2_gnn_Wq': _L2_gnn_in['Wq'], 'L2_gnn_bq': _L2_gnn_in['bq'], 'L2_gnn_W0': _L2_gnn_in['W0'], 'L2_gnn_b0': _L2_gnn_in['b0'], 'L2_gnn_g0': _L2_gnn_in['g0'], 'L2_gnn_beta0': _L2_gnn_in['beta0'], 'L2_gnn_W1': _L2_gnn_in['W1'], 'L2_gnn_b1': _L2_gnn_in['b1'], 'L2_gnn_g1': _L2_gnn_in['g1'], 'L2_gnn_beta1': _L2_gnn_in['beta1'], 'L2_gnn_Wf': _L2_gnn_in['Wf'], 'L2_gnn_bf': _L2_gnn_in['bf'], 'L3_gnn_W_self': _L3_gnn_in['W_self'], 'L3_gnn_b_self': _L3_gnn_in['b_self'], 'L3_gnn_W_neigh': _L3_gnn_in['W_neigh'], 'L3_gnn_b_neigh': _L3_gnn_in['b_neigh']}

def reference(x, src, dst, edge_attr_16, edge_weight, L0_gnn_W_l, L0_gnn_W_r, L0_gnn_att, L0_gnn_bias, L2_gnn_Wq, L2_gnn_bq, L2_gnn_W0, L2_gnn_b0, L2_gnn_g0, L2_gnn_beta0, L2_gnn_W1, L2_gnn_b1, L2_gnn_g1, L2_gnn_beta1, L2_gnn_Wf, L2_gnn_bf, L3_gnn_W_self, L3_gnn_b_self, L3_gnn_W_neigh, L3_gnn_b_neigh):
    import jax
    import jax.numpy as jnp

    def _L0_gnn_ref(x, edge_index, W_l, W_r, att, bias):
        import jax, jax.numpy as jnp
        import numpy as np
        NEG_SLOPE = 0.2
        N = x.shape[0]
        loop = jnp.arange(N, dtype=edge_index.dtype)
        src = jnp.concatenate([edge_index[0], loop])
        dst = jnp.concatenate([edge_index[1], loop])
        x_l = x @ W_l
        x_r = x @ W_r
        e = jax.nn.leaky_relu(x_l[src] + x_r[dst], NEG_SLOPE) @ att
        e_max = jax.ops.segment_max(e, dst, num_segments=N)
        e_exp = jnp.exp(e - e_max[dst])
        denom = jax.ops.segment_sum(e_exp, dst, num_segments=N)
        alpha = e_exp / denom[dst]
        out = jax.ops.segment_sum(alpha[:, None] * x_l[src], dst, num_segments=N)
        return out + bias

    def _L1_gnn_ref(x, row, col, value, size):
        import jax, jax.numpy as jnp
        import numpy as np
        N = 12500
        NNZ = 200000
        D = 64
        gathered = value[:, None] * x[col]
        y = jax.ops.segment_sum(gathered, row, num_segments=size)
        return y

    def _L2_gnn_ref(nodes, edges, senders, receivers, Wq, bq, W0, b0, g0, beta0, W1, b1, g1, beta1, Wf, bf):
        import jax, jax.numpy as jnp
        import numpy as np
        N = 6250
        E = 100000
        D = 64
        ED = 16
        H = 64
        CIN = 2 * D + ED

        def _he(key, shape):
            return jax.random.normal(key, shape, jnp.float32) * jnp.sqrt(2.0 / shape[0])

        def _layer_norm(x, g, b, eps=1e-06):
            mu = jnp.mean(x, axis=-1, keepdims=True)
            var = jnp.var(x, axis=-1, keepdims=True)
            return (x - mu) * jax.lax.rsqrt(var + eps) * g + b
        n = nodes.shape[0]
        idx = jnp.arange(n, dtype=senders.dtype)
        snd = jnp.concatenate([senders, idx], axis=0)
        rcv = jnp.concatenate([receivers, idx], axis=0)
        edg = jnp.concatenate([edges, jnp.zeros((n, edges.shape[-1]), edges.dtype)], axis=0)
        x = jnp.concatenate([nodes[snd], nodes[rcv], edg], axis=-1)
        q = x @ Wq + bq
        h = _layer_norm(jax.nn.relu(x @ W0 + b0), g0, beta0)
        h = _layer_norm(jax.nn.relu(h @ W1 + b1), g1, beta1)
        logits = jax.nn.relu(h @ Wf + bf)
        m = jax.ops.segment_max(logits, rcv, num_segments=n)
        e = jnp.exp(logits - m[rcv])
        denom = jax.ops.segment_sum(e, rcv, num_segments=n)
        w = e / denom[rcv]
        out = jax.ops.segment_sum(q * w, rcv, num_segments=n)
        return jnp.reshape(jax.nn.leaky_relu(out), (out.shape[0], -1))

    def _L3_gnn_ref(x, edge_index, edge_weight, W_self, b_self, W_neigh, b_neigh, num_nodes):
        import jax, jax.numpy as jnp
        import numpy as np
        row, col = (edge_index[0], edge_index[1])
        message = x[col] * edge_weight[:, None]
        neigh_agg = jax.ops.segment_sum(message, row, num_segments=num_nodes)
        return x @ W_self.T + b_self + neigh_agg @ W_neigh.T + b_neigh
    edge_index = jnp.stack([src, dst])
    h = jnp.maximum(_layernorm(x, axis=-1), 0.0)
    x = x + _L0_gnn_ref(h, edge_index, L0_gnn_W_l, L0_gnn_W_r, L0_gnn_att, L0_gnn_bias)
    h = jnp.maximum(_layernorm(x, axis=-1), 0.0)
    x = x + _L1_gnn_ref(h, src, dst, edge_weight, 12500)
    h = jnp.maximum(_layernorm(x, axis=-1), 0.0)
    x = x + _L2_gnn_ref(h, edge_attr_16, src, dst, L2_gnn_Wq, L2_gnn_bq, L2_gnn_W0, L2_gnn_b0, L2_gnn_g0, L2_gnn_beta0, L2_gnn_W1, L2_gnn_b1, L2_gnn_g1, L2_gnn_beta1, L2_gnn_Wf, L2_gnn_bf)
    h = jnp.maximum(_layernorm(x, axis=-1), 0.0)
    x = x + _L3_gnn_ref(h, edge_index, edge_weight, L3_gnn_W_self, L3_gnn_b_self, L3_gnn_W_neigh, L3_gnn_b_neigh, 12500)
    return x

_drawn_inputs = setup_inputs


def setup_inputs(seed=0):
    import zlib

    import numpy as np

    out = dict(_drawn_inputs(seed))
    spreads = {'L0_gnn_bias': (0.0, 0.1),
     'L2_gnn_bq': (0.0, 0.388),
     'L2_gnn_b0': (0.0, 0.8),
     'L2_gnn_g0': (1.0, 0.6),
     'L2_gnn_beta0': (0.0, 0.8),
     'L2_gnn_b1': (0.0, 2.0),
     'L2_gnn_g1': (1.0, 0.6),
     'L2_gnn_beta1': (0.0, 2.0),
     'L3_gnn_b_self': (0.0, 0.742),
     'L3_gnn_b_neigh': (0.0, 0.701)}
    factors = {'edge_attr_16': 3.616,
     'L0_gnn_W_r': 19.078,
     'L2_gnn_W0': 4.678,
     'L2_gnn_W1': 4.378,
     'L2_gnn_Wf': 4.125}
    for name, (base, spread) in spreads.items():
        noise = np.random.default_rng([zlib.crc32(name.encode()), seed]).standard_normal(out[name].shape)
        drawn = base * np.exp(spread * noise) if base else spread * noise
        out[name] = jnp.asarray(drawn.astype(out[name].dtype))
    for name, factor in factors.items():
        out[name] = (out[name] * factor).astype(out[name].dtype)
    return out
```

```python
from contextlib import ExitStack
from collections import namedtuple

import numpy as np
import concourse.bass as bass
from concourse import mybir

P = 128
D = 64
F32 = mybir.dt.float32
BF16 = mybir.dt.bfloat16
I32 = mybir.dt.int32
U32 = mybir.dt.uint32
U8 = mybir.dt.uint8
ALU = mybir.AluOpType
ACT = mybir.ActivationFunctionType
AX = mybir.AxisListType.X
ds = bass.ds

EA = 16
G = 4
R = 4
CH = 3
SC = 3
RECD = 2 + EA
RECS = 3
NEG = -(2.0 ** 100)
EPS_NODE = 1e-5
EPS_MLP = 1e-6
DST, SRC = 0, 1


class Sizes:
    def __init__(self, n, e):
        self.N, self.E = n, e
        self.NB = -(-n // P)
        self.NBUCK = self.NB + 1
        self.NBK = -(-(self.NB + 1) // G) * G
        self.PADKEY = self.NB * P
        self.C = -(-(e + P) // (P * CH * SC * 2)) * (CH * SC * 2)
        self.EP = self.C * P
        self.STEPS = -(-(e // P + self.NB) // (G * R)) * (G * R)
        self.NG = self.STEPS // G
        self.NIT = self.NG // R
        self.SJ = -(-self.STEPS // P)
        assert self.NIT >= 3


class Place:
    pass


def named(**values):
    return namedtuple("Named", values.keys())(*values.values())


def after(eng, sem, value, alone=False):
    if not (isinstance(value, int) and value <= 0):
        eng.wait_ge(sem, value)
        if alone:
            eng.nop(nofuse=True)


class Links:

    def __init__(self, eng, sem, per):
        self.eng, self.sem, self.per = eng, sem, per

    def run(self, n):
        self.start, self.n = n * self.per, 0

    def __call__(self, ins):
        self.n += 1
        ins.then_inc(self.sem, 1)
        self.eng.wait_ge(self.sem, self.start + self.n)

    def end(self):
        assert self.n == self.per, self.n


def over_nodes(ap):
    return ap.unsqueeze(2).broadcast_to([P, ap.shape[1], P])


def over_features(ap, d=D):
    return ap.unsqueeze(2).broadcast_to([P, ap.shape[1], d])


def rows_of(ap, m):
    return ap.unsqueeze(1).broadcast_to([P, m, ap.shape[1]])


def skewed(eng, z, first, second):
    first(0, 0)
    for j in range(R):
        first(0, j + 1)
        second(0, j)
    with eng.Fori(1, z.NIT - 1) as it:
        for j in range(R):
            first(it, j + 1)
            second(it, j)
    for j in range(R):
        if j + 1 < R:
            first(z.NIT - 1, j + 1)
        second(z.NIT - 1, j)


def unskewed(eng, z, step):
    for j in range(R):
        step(0, j)
    with eng.Fori(1, z.NIT) as it:
        for j in range(R):
            step(it, j)


def counted(eng, n, body):
    body(0)
    with eng.Fori(1, n) as i:
        body(i)


def load_constants(nc, io, z, k):
    loads = [
        (k.attw[:], io.att.partition_broadcast(P)), (k.bias0[:], io.bias.partition_broadcast(P)),
        (k.wlr[:, 0:D], io.W_l), (k.wlr[:, D:2 * D], io.W_r),
        (k.wqa[:, 0:D], io.Wq[0:D, :]), (k.wqa[:, D:2 * D], io.W0[0:D, :]),
        (k.wqb[:, 0:D], io.Wq[D:2 * D, :]), (k.wqb[:, D:2 * D], io.W0[D:2 * D, :]),
        (k.wqe[:, 0:D], io.Wq[2 * D:2 * D + EA, :]), (k.wqe[:, D:2 * D], io.W0[2 * D:2 * D + EA, :]),
        (k.bq0[:, 0:D], io.bq.partition_broadcast(P)), (k.bq0[:, D:2 * D], io.b0.partition_broadcast(P)),
        (k.w1[:], io.W1), (k.g0[:], io.g0), (k.beta0[:], io.beta0),
        (k.w1b[:], io.b1.partition_broadcast(P)), (k.wfg[:], io.g1.partition_broadcast(P)),
        (k.beta1[:], io.beta1.partition_broadcast(P)), (k.wf[:], io.Wf.partition_broadcast(P)),
        (k.wfb[:], io.bf.partition_broadcast(P)),
        (k.w3[:, 0, :], io.W_selfT), (k.w3[:, 1, :], io.W_neighT),
        (k.b3[:], io.b_self.partition_broadcast(P)), (k.b3n[:], io.b_neigh.partition_broadcast(P)),
    ]
    s = k.csem
    with nc.Block() as block:
        @block.sync
        def _(sp):
            for out, src in loads:
                sp.dma_start(out, src).then_inc(s.consts, 16)

        @block.gpsimd
        def _(pool):
            pool.iota(k.iota[:], [[1, P]], base=0, channel_multiplier=0,
                      allow_small_or_imprecise_dtypes=True).then_inc(s.iota, 1)
            pool.iota(k.pidx[:], [[0, 1]], base=0, channel_multiplier=1,
                      allow_small_or_imprecise_dtypes=True).then_inc(s.iota, 1)

        @block.vector
        def _(v):
            link = Links(v, s.clink, 11)
            link.run(0)
            v.wait_ge(s.iota, 2)
            v.tensor_scalar(k.ident[:], k.iota[:], k.pidx[:], None, ALU.is_equal)
            v.tensor_scalar(k.identb[:], k.iota[:], k.pidx[:], None, ALU.is_equal)
            link(v.tensor_scalar(k.before[:], k.iota[:], k.pidx[:], None, ALU.is_gt))
            link(v.memset(k.ones[:], 1.0))
            v.wait_ge(s.consts, 16 * len(loads))
            link(v.tensor_copy(k.beta0w[:], k.beta0[:].broadcast_to([D, P])))
            v.tensor_scalar(k.w1g[:], k.w1[:], k.g0[:], None, ALU.mult).then_inc(s.beta_wide, 1)
            v.wait_ge(s.beta_w1, 1)
            link(v.tensor_tensor(k.w1b[:], k.w1b[:], k.bank[0][:, 0:D], ALU.add))
            link(v.tensor_tensor(k.wfg[:], k.wfg[:], k.wf[:], ALU.mult))
            link(v.tensor_tensor(k.beta1[:], k.beta1[:], k.wf[:], ALU.mult))
            link(v.tensor_reduce(k.pidx2[:], k.beta1[:], AX, ALU.add))
            link(v.tensor_tensor(k.wfb[:], k.wfb[:], k.pidx2[:], ALU.add))
            link(v.tensor_tensor(k.b3[:], k.b3[:], k.b3n[:], ALU.add))
            link(v.memset(k.zero[:], 0.0))
            link(v.memset(k.epsn[:], EPS_NODE))
            link.end()

        @block.tensor
        def _(pe):
            pe.wait_ge(s.beta_wide, 1)
            pe.matmul(k.bank[0][:, 0:D], k.beta0w[:], k.w1[:], start=True, stop=True).then_inc(s.beta_w1, 1)


NORM_LINKS = 8


def norm_vector(v, k, z, link, s, n):
    nb = z.NBK
    link(v.tensor_reduce(k.nstat[:, 0, :], k.x[:], AX, ALU.add))
    link(v.scalar_tensor_tensor(k.hbuf[:], over_features(k.nstat[:, 0, :]), -1.0 / D, k.x[:], ALU.mult, ALU.add))
    link(v.tensor_tensor(k.tab[:, :, 0:D], k.hbuf[:], k.hbuf[:], ALU.mult))
    link(v.tensor_reduce(k.nstat[:, 1, :], k.tab[:, :, 0:D], AX, ALU.add))
    v.tensor_scalar(k.nstat[:, 2, :], k.nstat[:, 1, :], 1.0 / D, EPS_NODE, ALU.mult, ALU.add).then_inc(s.var_done, 1)
    v.wait_ge(s.sqrt_done, n + 1)
    link(v.reciprocal(k.nstat[:, 1, :], k.nstat[:, 0, :]))
    link(v.scalar_tensor_tensor(k.hbuf[:], k.hbuf[:], 0.0, over_features(k.nstat[:, 1, :]), ALU.max, ALU.mult))


def norm_scalar(a, k, s, n):
    a.wait_ge(s.var_done, n + 1)
    a.activation(k.nstat[:, 0, :], k.nstat[:, 2, :], ACT.Sqrt).then_inc(s.sqrt_done, 1)


def rank_edges(v, k, z, key, n):
    s, cc = k.s1, z.C // CH
    link = Links(v, s.rank_link, 13 + 2 * z.SJ + z.NBUCK + CH * 3 * z.NBUCK)
    link.run(n)
    o = k.order[key]
    link(v.tensor_scalar(o.pos_int[:], o.key_int[:], 7, None, ALU.logical_shift_right))
    link(v.tensor_copy(k.hi[:], o.pos_int[:]))
    first = link.start + link.n
    with v.Fori(0, z.NBUCK) as b:
        v.tensor_scalar(k.same[:], k.hi[:], k.iota[:, ds(b, 1)], None, ALU.is_equal, ALU.add,
                        accum_out=k.cnt[:, ds(b, 1)]).then_inc(s.rank_link, 1)
        v.wait_ge(s.rank_link, first + b + 1)
    link.n += z.NBUCK
    v.tensor_copy(k.cnt2[:], k.cnt[:]).then_inc(s.counted, 1)
    v.wait_ge(s.count_sums, n + 1)
    nb = z.NBUCK
    low, tot = k.bank[0][:, 0:nb], k.bank[1][:, 0:nb]
    link(v.tensor_copy(k.tot[:], tot))
    link(v.tensor_tensor_scan(k.goff[:], k.tot[:], k.tot[:], -1.0, ALU.add, ALU.bypass))
    link(v.tensor_tensor(k.goff[:], k.goff[:], k.tot[:], ALU.subtract))
    link(v.tensor_tensor(k.base[:], k.goff[:], low, ALU.add))
    link(v.tensor_scalar(k.nst_int[:], k.tot[:], float(P - 1), None, ALU.add))
    link(v.tensor_scalar(k.nst_int[:], k.nst_int[:], 7, None, ALU.logical_shift_right))
    link(v.tensor_copy(k.nst[:], k.nst_int[:]))
    link(v.tensor_tensor_scan(k.send[:], k.nst[:], k.nst[:], 0.0, ALU.add, ALU.bypass))
    link(v.tensor_tensor(k.lead[:], k.send[:], k.nst[:], ALU.subtract))
    link(v.scalar_tensor_tensor(k.lead[:], k.lead[:], float(-P), k.goff[:], ALU.mult, ALU.add))
    last = z.NB - 1
    link(v.tensor_tensor(k.jump[:, 0:last], k.lead[:, 1:z.NB], k.lead[:, 0:last], ALU.subtract))
    v.wait_ge(s.step_no_done, 1)
    for j in range(z.SJ):
        link(v.tensor_scalar(k.ended[:, 0:last], k.send[:, 0:last], k.step_no[:, j:j + 1], None, ALU.is_le, ALU.add,
                             accum_out=k.blk[:, j:j + 1]))
        link(v.tensor_tensor_reduce(k.ended2[:, 0:last], k.ended[:, 0:last], k.jump[:, 0:last], 1.0, 0.0, ALU.mult,
                                    ALU.add, k.off[:, j:j + 1]))
    v.scalar_tensor_tensor(k.off2[:], k.step_no[:], float(P), k.off[:], ALU.mult, ALU.add).then_inc(s.off_sum, 1)
    v.wait_ge(s.off_sum, n + 1)
    if n:
        v.wait_ge(s.tables_out[DST], 48)
    v.tensor_scalar(k.off_int[:], k.off2[:], float(z.E), None, ALU.min)
    v.tensor_copy(k.blk_int[:], k.blk[:])
    v.tensor_scalar(k.blk128[:], k.blk[:], float(P), None, ALU.mult).then_inc(s.tables_done, 1)
    for part in range(CH):
        cols = slice(part * cc, (part + 1) * cc)
        at = link.start + link.n
        with v.Fori(0, z.NBUCK) as b:
            v.tensor_scalar(k.same[:, 0:cc], k.hi[:, cols], k.iota[:, ds(b, 1)], None, ALU.is_equal).then_inc(s.rank_link, 1)
            v.wait_ge(s.rank_link, at + 3 * b + 1)
            v.tensor_tensor_scan(k.run[:], k.same[:, 0:cc], k.same[:, 0:cc], k.base[:, ds(b, 1)], ALU.add,
                                 ALU.bypass).then_inc(s.rank_link, 1)
            after(v, s.rank_link, at + 3 * b + 2, alone=True)
            v.tensor_copy(k.base[:, ds(b, 1)], k.run[:, cc - 1:cc])
            v.copy_predicated(o.pos_int[:, cols], k.same[:, 0:cc], k.run[:]).then_inc(s.rank_link, 1)
            v.wait_ge(s.rank_link, at + 3 * b + 3)
        link.n += 3 * z.NBUCK
        v.tensor_copy(k.pidx2[:], k.pidx[:]).then_inc(s.ranked[key], 1)
    link.end()


def sort_and_project(nc, io, z, k):
    s, NG25 = k.s1, z.NBK // G
    units = z.C // SC

    with nc.Block() as block:
        @block.sync
        def _(sp):
            sp.dma_start(k.x[:], io.x.rearrange("(b p) d -> p b d", p=P)).then_inc(s.x_loaded, 16)
            sp.dma_start(k.order[DST].key_int[:], io.dst.rearrange("(p c) -> p c", p=P)).then_inc(s.dst_loaded, 16)
            sp.dma_start(k.order[SRC].key_int[:], io.src.rearrange("(p c) -> p c", p=P)).then_inc(s.src_loaded, 16)
            sp.dma_start(k.w[:], io.w.rearrange("(p c) -> p c", p=P)).then_inc(s.w_loaded, 16)

            def tables_to_dram(n, key):
                sp.wait_ge(s.tables_done, n + 1)
                for tile, dram in ((k.off_int, k.off_dram), (k.blk_int, k.blk_dram), (k.blk128, k.b128_dram)):
                    sp.dma_start(dram[key].rearrange("(p j) -> p j", p=P), tile[:]).then_inc(s.tables_out[key], 16)
                sp.wait_ge(s.tables_out[key], 48)
                sp.dma_start(k.b128[key][:], k.b128_dram[key].partition_broadcast(P)).then_inc(s.tables_in, 16)
                sp.dma_start(k.offs[key], k.off_dram[key].partition_broadcast(1)).then_inc(s.tables_in, 16)
                sp.dma_start(k.blks[key], k.blk_dram[key].partition_broadcast(1)).then_inc(s.tables_in, 16)

            tables_to_dram(0, DST)
            sp.wait_ge(s.xl_done, NG25)
            sp.dma_start(k.xl_dram.rearrange("(b p) d -> p b d", p=P), k.acc[:, :, 0:D]).then_inc(s.xl_out, 16)
            attr = io.attr.rearrange("(p c) f -> p c f", p=P)

            def load_attr(it, half):
                u = 2 * it + half
                after(sp, s.staged, u - 1)
                sp.dma_start(k.attr_in[:, half], attr[:, ds(u * SC, SC), :]).then_inc(s.attr_loaded[half], 16)

            for half in range(2):
                load_attr(0, half)
            with sp.Fori(1, units // 2) as it:
                for half in range(2):
                    load_attr(it, half)
            tables_to_dram(1, SRC)
            sp.wait_ge(s.tables_in, 96)
            sp.wait_ge(s.xl_out, 16)

        @block.scalar
        def _(a):
            norm_scalar(a, k, s, 0)
            a.wait_ge(s.norm_done, 1)

            def project(i):
                a.activation(k.hs[:], k.hbuf[:, ds(i * G, G), :], ACT.Copy).then_inc(s.hs_done, 1)
                a.wait_ge(s.hsT_done, i + 1)
                a.activation(k.hT[:], k.bank[6][0:D, :], ACT.Copy).then_inc(s.hT_done, 1)
                a.wait_ge(s.proj_done, i + 1)
                pr = k.bank[0].rearrange("p (g d) -> p g d", g=G)
                a.activation(k.acc[:, ds(i * G, G), 0:D], pr[:, :, 0:D], ACT.Copy)
                a.activation(k.tab[:, ds(i * G, G), 0:D], pr[:, :, D:2 * D], ACT.Copy).then_inc(s.xl_done, 1)

            with a.Fori(0, NG25) as i:
                project(i)

            def stage(key, n, it, half):
                u = 2 * it + half
                cols = ds(u * SC, SC)
                o, other = k.order[key], k.order[1 - key]
                rec = k.rec[:, half]
                after(a, s.scattered[half], 16 * SC * (it + n * (units // 2)))
                if key == DST:
                    a.wait_ge(s.attr_loaded[half], 16 * (it + 1))
                    a.activation(rec[:, :, 2:RECD], k.attr_in[:, half], ACT.Copy)
                else:
                    a.activation(rec[:, :, 2], k.w[:, cols], ACT.Copy)
                a.activation(rec[:, :, 0].bitcast(I32), other.key_int[:, cols], ACT.Copy)
                a.activation(rec[:, :, 1], o.key_int[:, cols], ACT.Copy)
                a.activation(k.pos_st[:, half], o.pos_int[:, cols], ACT.Copy).then_inc(s.staged, 1)

            def stage_all(key, n):
                for half in range(2):
                    stage(key, n, 0, half)
                with a.Fori(1, units // 2) as it:
                    for half in range(2):
                        stage(key, n, it, half)

            a.wait_ge(s.src_loaded, 16)
            a.wait_ge(s.dst_loaded, 16)
            a.wait_ge(s.ranked[DST], CH)
            stage_all(DST, 0)
            a.wait_ge(s.w_loaded, 16)
            a.wait_ge(s.ranked[SRC], CH)
            stage_all(SRC, 1)

        @block.tensor
        def _(pe):
            def project(i):
                after(pe, s.hs_done, i + 1, alone=True)
                for g in range(G):
                    last = pe.transpose(k.bank[6][0:D, g * P:(g + 1) * P], k.hs[:, g, :], k.ident[:])
                last.then_inc(s.hsT_done, 1)
                pe.wait_ge(s.hT_done, i + 1)
                for g in range(G):
                    last = pe.matmul(k.bank[0][:, g * P:(g + 1) * P], k.hT[:, g * P:(g + 1) * P], k.wlr[:],
                                     start=True, stop=True)
                last.then_inc(s.proj_done, 1)

            with pe.Fori(0, NG25) as i:
                project(i)

            def count_sums(n):
                pe.wait_ge(s.counted, n + 1)
                pe.matmul(k.bank[0][:, 0:z.NBUCK], k.before[:], k.cnt2[:], start=True, stop=True)
                pe.matmul(k.bank[1][:, 0:z.NBUCK], k.ones[:], k.cnt2[:], start=True, stop=True).then_inc(s.count_sums, 1)

            pe.wait_ge(s.xl_done, NG25)
            count_sums(0)
            count_sums(1)

        @block.vector
        def _(v):
            link = Links(v, s.nlink, 11)
            link.run(0)
            v.wait_ge(s.x_loaded, 16)
            norm_vector(v, k, z, link, s, 0)
            v.tensor_copy(k.pidx2[:], k.pidx[:]).then_inc(s.norm_done, 1)
            v.wait_ge(s.dst_loaded, 16)
            rank_edges(v, k, z, DST, 0)
            v.wait_ge(s.xl_done, NG25)
            low, tmp = k.hbuf, k.tab[:, :, D:2 * D]
            link(v.tensor_tensor(low[:], k.acc[:, :, 0:D], k.tab[:, :, 0:D], ALU.add))
            link(v.scalar_tensor_tensor(tmp, low[:], 0.2, low[:], ALU.mult, ALU.max))
            link(v.tensor_tensor(low[:], tmp, rows_of(k.attw[:], z.NBK), ALU.mult))
            link(v.tensor_reduce(k.macc[:], low[:], AX, ALU.add))
            link(v.memset(k.acc[:, :, D:D + 1], 1.0))
            link.end()
            v.wait_ge(s.src_loaded, 16)
            rank_edges(v, k, z, SRC, 1)

        @block.gpsimd
        def _(pool):
            pool.iota(k.step_no[:], [[1, z.SJ]], base=0, channel_multiplier=z.SJ,
                      allow_small_or_imprecise_dtypes=True).then_inc(s.step_no_done, 1)

            def scatter(key, it, half, n):
                u = 2 * it + half
                dram, width = (k.recd_dram, RECD) if key == DST else (k.recs_dram, RECS)
                after(pool, s.staged, n * units + u + 1, alone=True)
                for c in range(SC):
                    pool.indirect_dma_start(
                        dram, bass.IndirectOffsetOnAxis(ap=k.pos_st[:, half, c:c + 1].bitcast(U32), axis=0),
                        k.rec[:, half, c, 0:width], None).then_inc(s.scattered[half], 16)

            for n, key in ((0, DST), (1, SRC)):
                with pool.Fori(0, units // 2) as it:
                    for half in range(2):
                        scatter(key, it, half, n)
            for half in range(2):
                pool.wait_ge(s.scattered[half], 16 * SC * units)


def softmax_edges(nc, z, k, base, mlp):
    s = k.s
    table = k.a2_dram if mlp else k.xl_dram
    width = 2 * D if mlp else D
    bank = k.bank
    hotT_p = bank[2].bitcast(BF16).rearrange("p (a g n) -> p a g n", a=2, g=G)[:, 0]
    mx_p = bank[3].rearrange("p (g n) -> p g n", g=G)
    sum_p = bank[4][:, 0:G * (D + 1)].rearrange("p (g d) -> p g d", g=G)
    me_p = bank[5][:, 0:G]
    x_links = LOGIT_LINKS if mlp else 3
    y_links = 3 * G + G
    value = (lambda slot, two: k.val[:, two]) if mlp else (lambda slot, two: k.rows[:, slot, :, 0:D + 1])

    def z_p(two):
        return bank[two][:, 0:G * width].rearrange("p (g d) -> p g d", g=G)

    def at(it, j):
        return base + R * it + j, j % R, j % 2

    with nc.Block() as block:
        @block.sync
        def _(sp):
            def step(it, j):
                n, slot, _ = at(it, j)
                after(sp, s.s_done, n - R + 1)
                for g in range(G):
                    off = sp.value_load(k.offs[DST][0:1, ds((R * it + j) * G + g, 1)], min_val=0, max_val=z.E)
                    sp.dma_start(k.win[:, slot, g, :], k.recd_dram[ds(off, P), :]).then_inc(s.win_loaded[slot], 16)
            unskewed(sp, z, step)

        @block.gpsimd
        def _(pool):
            def step(it, j):
                n, slot, _ = at(it, j)
                after(pool, s.s_done, n - R + 1, alone=True)
                after(pool, s.win_loaded[slot], 16 * G * (base // R + it + 1), alone=True)
                for g in range(G):
                    pool.indirect_dma_start(
                        k.rows[:, slot, g, 0:width], None, table,
                        bass.IndirectOffsetOnAxis(ap=k.win[:, slot, g, 0:1].bitcast(U32), axis=0)
                    ).then_inc(s.gathered[slot], 16)
            unskewed(pool, z, step)

        @block.scalar
        def _(a):
            def first(it, j):
                n, slot, two = at(it, j)
                if mlp:
                    a.wait_ge(s.atT_p_done, R * it + j + 1)
                    a.activation(k.atT[:, two], bank[7][0:EA, :], ACT.Copy).then_inc(s.atT_done, 1)
                after(a, s.hotT_p_done, n + 1)
                a.activation(k.hotT[:, two], hotT_p, ACT.Copy)
                a.activation(k.negT[:, two], hotT_p, ACT.Copy, scale=-NEG, bias=NEG).then_inc(s.hotT_done, 1)
                after(a, s.z_done, n + 1)
                after(a, s.e_done, n)
                if mlp:
                    a.activation(k.val[:, two, :, 0:D], z_p(two)[:, :, 0:D], ACT.Copy)
                    mlp_scalar(a, k, z.NBK // G + R * it + j, z_p(two)[:, :, D:2 * D])
                else:
                    a.activation(k.tmp[:], z_p(two), ACT.Relu, scale=0.8).then_inc(s.relu_done, 1)

            def second(it, j):
                n, slot, two = at(it, j)
                after(a, s.de_done, n + 1)
                a.activation(k.p[:], k.de[:], ACT.Exp).then_inc(s.p_done, 1)
                a.wait_ge(s.p_done, n + 1)
                for g in range(G):
                    last = a.activation(k.ph[:, g, :], k.hot[:, two, g, :], ACT.Copy, scale=k.p[:, g:g + 1])
                last.then_inc(s.ph_done, 1)
                after(a, s.dd_done, n + 1)
                a.activation(k.cc[:], k.dd[:], ACT.Exp).then_inc(s.cc_done, 1)
            skewed(a, z, first, second)

        @block.tensor
        def _(pe):
            def first(it, j):
                n, slot, two = at(it, j)
                if mlp:
                    after(pe, s.win_loaded[slot], 16 * G * (base // R + it + (j // R) + 1), alone=True)
                    after(pe, s.atT_done, R * it + j, alone=True)
                    for g in range(G):
                        last = pe.transpose(bank[7][0:EA, g * P:(g + 1) * P], k.win[:, slot, g, 2:RECD], k.ident[:])
                    last.then_inc(s.atT_p_done, 1)
                after(pe, s.hot_done, n + 1, alone=True)
                after(pe, s.hotT_done, n, alone=True)
                for g in range(G):
                    last = pe.transpose(hotT_p[:, g, :], k.hot[:, two, g, :], k.identb[:])
                last.then_inc(s.hotT_p_done, 1)
                after(pe, s.gathered[slot], 16 * G * (base // R + it + (j // R) + 1), alone=True)
                after(pe, s.e_done, n - 1, alone=True)
                zp = z_p(two)
                for g in range(G):
                    pe.matmul(zp[:, g, :], k.ident[:], k.rows[:, slot, g, 0:width], start=(g == 0), stop=False,
                              skip_group_check=True)
                if mlp:
                    after(pe, s.atT_done, R * it + j + 1, alone=True)
                    for g in range(G):
                        pe.matmul(zp[:, g, :], k.atT[:, two, g, :], k.wqe[:], start=False, stop=False,
                                  skip_group_check=True)
                after(pe, s.hotT_done, n + 1, alone=True)
                for g in range(G):
                    b = pe.value_load(k.blks[DST][0:1, ds((R * it + j) * G + g, 1)], min_val=0, max_val=z.NB - 1)
                    last = pe.matmul(zp[:, g, :], k.hotT[:, two, g, :],
                                     k.tab[:, ds(b, 1), 0:width].rearrange("p a d -> p (a d)"),
                                     start=False, stop=(g == G - 1), skip_group_check=True)
                last.then_inc(s.z_done, 1)
                if mlp:
                    mlp_tensor(pe, k, z.NBK // G + R * it + j)

            def second(it, j):
                n, slot, two = at(it, j)
                after(pe, s.eh_done, n + 1, alone=True)
                pe.matmul(bank[3][:], k.identb[:], k.negT[:, two].rearrange("p g n -> p (g n)"), start=True, stop=False,
                          skip_group_check=True)
                for g in range(G):
                    last = pe.matmul(mx_p[:, g, :], k.eh[:, g, :], k.ident[:], start=False, stop=(g == G - 1),
                                     skip_group_check=True)
                last.then_inc(s.mx_done, 1)
                after(pe, s.ms_done, n + 1, alone=True)
                for g in range(G):
                    last = pe.matmul(me_p[:, g:g + 1], k.hotT[:, two, g, :], k.ms[:, g:g + 1], start=True, stop=True)
                last.then_inc(s.me_done, 1)
                pe.wait_ge(s.ones_set, 1 + mlp)
                after(pe, s.ph_done, n + 1, alone=True)
                after(pe, s.ts_done, n, alone=True)
                for g in range(G):
                    last = pe.matmul(sum_p[:, g, :], k.ph[:, g, :], value(slot, two)[:, g, :], start=True, stop=True)
                last.then_inc(s.s_done, 1)
            skewed(pe, z, first, second)

        @block.vector
        def _(v):
            xl, yl = Links(v, s.x_link[mlp], x_links), Links(v, s.y_link[mlp], y_links)
            ones = k.val[:, :, :, D:D + 1] if mlp else k.rows[:, :, :, D:D + 1]
            v.memset(ones, 1.0).then_inc(s.ones_set, 1)

            def first(it, j):
                n, slot, two = at(it, j)
                g0 = (R * it + j) * G
                xl.run(R * it + j)
                after(v, s.win_loaded[slot], 16 * G * (base // R + it + (j // R) + 1))
                xl(v.tensor_tensor(k.lo[:, two], k.win[:, slot, :, 1], k.b128[DST][:, ds(g0, G)], ALU.subtract))
                after(v, s.ph_done, n - 1)
                v.tensor_tensor(k.hot[:, two], rows_of(k.iota[:], G), over_nodes(k.lo[:, two]),
                                ALU.is_equal).then_inc(s.hot_done, 1)
                if mlp:
                    mlp_vector(v, k, xl, z.NBK // G + R * it + j, k.e[:, two]).then_inc(s.e_done, 1)
                else:
                    after(v, s.relu_done, n + 1)
                    xl(v.scalar_tensor_tensor(k.tmp[:], z_p(two), 0.2, k.tmp[:], ALU.mult, ALU.add))
                    xl(v.tensor_tensor(k.tmp[:], k.tmp[:], rows_of(k.attw[:], G), ALU.mult))
                    v.tensor_reduce(k.e[:, two], k.tmp[:], AX, ALU.add).then_inc(s.e_done, 1)
                xl.end()

            def second(it, j):
                n, slot, two = at(it, j)
                yl.run(R * it + j)
                after(v, s.hot_done, n + 1)
                after(v, s.e_done, n + 1)
                v.tensor_tensor(k.eh[:], k.hot[:, two], over_nodes(k.e[:, two]), ALU.mult).then_inc(s.eh_done, 1)
                after(v, s.mx_done, n + 1)
                v.tensor_reduce(k.ms[:], mx_p, AX, ALU.max).then_inc(s.ms_done, 1)
                after(v, s.me_done, n + 1)
                v.tensor_tensor(k.de[:], k.e[:, two], me_p, ALU.subtract).then_inc(s.de_done, 1)
                blocks = [v.value_load(k.blks[DST][0:1, ds((R * it + j) * G + g, 1)], min_val=0, max_val=z.NB - 1)
                          for g in range(G)]
                after(v, s.ms_done, n + 1)
                for g in range(G):
                    old = k.macc[:, ds(blocks[g], 1)]
                    yl(v.tensor_tensor(k.mn[:, g:g + 1], old, k.ms[:, g:g + 1], ALU.max))
                    yl(v.tensor_tensor(k.dd[:, g, 0:1], old, k.mn[:, g:g + 1], ALU.subtract))
                    yl(v.tensor_scalar(old, k.mn[:, g:g + 1], 0.0, None, ALU.add))
                v.tensor_tensor(k.dd[:, :, 1], k.ms[:], k.mn[:], ALU.subtract).then_inc(s.dd_done, 1)
                after(v, s.cc_done, n + 1)
                after(v, s.s_done, n + 1)
                v.tensor_tensor(k.ts[:], sum_p, over_features(k.cc[:, :, 1], D + 1), ALU.mult).then_inc(s.ts_done, 1)
                after(v, s.ts_done, n + 1)
                for g in range(G):
                    node = k.acc[:, ds(blocks[g], 1), :].rearrange("p a d -> p (a d)")
                    yl(v.scalar_tensor_tensor(node, node, k.cc[:, g, 0:1], k.ts[:, g, :], ALU.mult, ALU.add))
                yl.end()
            skewed(v, z, first, second)


def sum_edges(nc, z, k, base, table):
    s = k.s

    def at(it, j):
        return base + R * it + j, j % R, j % 2

    def loads(it, j):
        return 16 * G * (base // R + it + (j // R) + 1)

    def sum_p(two):
        return k.bank[two][:, 0:G * D].rearrange("p (g d) -> p g d", g=G)

    with nc.Block() as block:
        @block.sync
        def _(sp):
            def step(it, j):
                n, slot, _ = at(it, j)
                after(sp, s.w_sum, n - R + 1)
                for g in range(G):
                    off = sp.value_load(k.offs[SRC][0:1, ds((R * it + j) * G + g, 1)], min_val=0, max_val=z.E)
                    sp.dma_start(k.win[:, slot, g, 0:RECS], k.recs_dram[ds(off, P), :]).then_inc(s.swin_loaded[slot], 16)
            unskewed(sp, z, step)

        @block.gpsimd
        def _(pool):
            def step(it, j):
                n, slot, _ = at(it, j)
                after(pool, s.w_sum, n - R + 1, alone=True)
                after(pool, s.swin_loaded[slot], loads(it, j), alone=True)
                for g in range(G):
                    pool.indirect_dma_start(
                        k.rows[:, slot, g, 0:D], None, table,
                        bass.IndirectOffsetOnAxis(ap=k.win[:, slot, g, 0:1].bitcast(U32), axis=0)
                    ).then_inc(s.sgathered[slot], 16)
            unskewed(pool, z, step)

        @block.tensor
        def _(pe):
            def step(it, j):
                n, slot, two = at(it, j)
                after(pe, s.w_hot, n + 1, alone=True)
                after(pe, s.w_acc, n - 1, alone=True)
                after(pe, s.sgathered[slot], loads(it, j), alone=True)
                wh = (k.eh, k.ph)[two]
                for g in range(G):
                    last = pe.matmul(sum_p(two)[:, g, :], wh[:, g, :], k.rows[:, slot, g, 0:D], start=True, stop=True)
                last.then_inc(s.w_sum, 1)
            unskewed(pe, z, step)

        @block.vector
        def _(v):
            link = Links(v, s.a_link, G)

            def first(it, j):
                n, slot, two = at(it, j)
                g0 = (R * it + j) * G
                wh = (k.eh, k.ph)[two]
                after(v, s.swin_loaded[slot], loads(it, j))
                v.tensor_tensor(k.lo[:, two], k.win[:, slot, :, 1], k.b128[SRC][:, ds(g0, G)],
                                ALU.subtract).then_inc(s.w_lo, 1)
                after(v, s.w_lo, n + 1)
                after(v, s.w_sum, n - 1)
                for g in range(G):
                    last = v.tensor_scalar(wh[:, g, :], k.iota[:], k.lo[:, two, g:g + 1], k.win[:, slot, g, 2:3],
                                           ALU.is_equal, ALU.mult)
                last.then_inc(s.w_hot, 1)

            def second(it, j):
                n, slot, two = at(it, j)
                link.run(n)
                after(v, s.w_sum, n + 1)
                for g in range(G):
                    b = v.value_load(k.blks[SRC][0:1, ds((R * it + j) * G + g, 1)], min_val=0, max_val=z.NB - 1)
                    node = k.acc[:, ds(b, 1), 0:D].rearrange("p a d -> p (a d)")
                    link(v.tensor_tensor(node, node, sum_p(two)[:, g, :], ALU.add))
                v.tensor_copy(k.pidx2[:], k.pidx[:]).then_inc(s.w_acc, 1)
                link.end()
            skewed(v, z, first, second)


def mlp_scalar(a, k, m, h0):
    s = k.s
    a.activation(k.h0[:], h0, ACT.Relu).then_inc(s.h_relu, 1)
    a.wait_ge(s.h_centred, 2 * m + 1)
    a.activation(k.sq[:], k.h0[:], ACT.Square).then_inc(s.h_sq, 1)
    a.wait_ge(s.hcT_p_done, m + 1)
    a.activation(k.hT[:], k.bank[6][0:D, :], ACT.Copy).then_inc(s.hcT_done, 1)
    a.wait_ge(s.v_done, 2 * m + 1)
    a.activation(k.lnv[:], k.var[:], ACT.Ln).then_inc(s.ln_done, 1)
    a.wait_ge(s.ln_done, 2 * m + 1)
    a.activation(k.r0[:], k.lnv[:], ACT.Exp, scale=-0.5).then_inc(s.r_guess, 1)
    a.wait_ge(s.t_done, m + 1)
    a.activation(k.h1[:], k.t1[:], ACT.Relu).then_inc(s.h1_relu, 1)
    a.wait_ge(s.h_centred, 2 * m + 2)
    a.activation(k.sq[:], k.h1[:], ACT.Square).then_inc(s.h_sq, 1)
    a.wait_ge(s.v_done, 2 * m + 2)
    a.activation(k.lnv[:], k.var[:], ACT.Ln).then_inc(s.ln_done, 1)
    a.wait_ge(s.ln_done, 2 * m + 2)
    a.activation(k.r0[:], k.lnv[:], ACT.Exp, scale=-0.5).then_inc(s.r_guess, 1)


def mlp_tensor(pe, k, m):
    s = k.s
    after(pe, s.h_centred, 2 * m + 1, alone=True)
    for g in range(G):
        last = pe.transpose(k.bank[6][0:D, g * P:(g + 1) * P], k.h0[:, g, :], k.ident[:])
    last.then_inc(s.hcT_p_done, 1)
    after(pe, s.hcT_done, m + 1, alone=True)
    for g in range(G):
        last = pe.matmul(k.bank[5][:, 64 + g * D:64 + (g + 1) * D], k.hT[:, g * P:(g + 1) * P], k.w1g[:],
                         start=True, stop=True)
    last.then_inc(s.y_done, 1)


MLP_LINKS = 14
LOGIT_LINKS = 1 + MLP_LINKS


def mlp_vector(v, k, link, m, out):
    s = k.s

    def rstd(m2):
        after(v, s.h_sq, m2)
        link(v.tensor_reduce(k.ss[:], k.sq[:], AX, ALU.add))
        v.tensor_scalar(k.var[:], k.ss[:], 1.0 / D, EPS_MLP, ALU.mult, ALU.add).then_inc(s.v_done, 1)
        after(v, s.r_guess, m2)
        link(v.tensor_tensor(k.ra[:], k.r0[:], k.r0[:], ALU.mult))
        link(v.scalar_tensor_tensor(k.ra[:], k.ra[:], -0.5, k.var[:], ALU.mult, ALU.mult))
        link(v.scalar_tensor_tensor(k.ra[:], k.ra[:], 1.5, k.r0[:], ALU.add, ALU.mult))

    after(v, s.h_relu, m + 1)
    link(v.tensor_reduce(k.ss[:], k.h0[:], AX, ALU.add))
    v.scalar_tensor_tensor(k.h0[:], over_features(k.ss[:]), -1.0 / D, k.h0[:], ALU.mult, ALU.add).then_inc(s.h_centred, 1)
    rstd(2 * m + 1)
    after(v, s.y_done, m + 1)
    y = k.bank[5][:, 64:64 + G * D].rearrange("p (g d) -> p g d", g=G)
    link(v.tensor_tensor(k.t1[:], y, over_features(k.ra[:]), ALU.mult))
    v.tensor_tensor(k.t1[:], k.t1[:], rows_of(k.w1b[:], G), ALU.add).then_inc(s.t_done, 1)
    after(v, s.h1_relu, m + 1)
    link(v.tensor_reduce(k.ss[:], k.h1[:], AX, ALU.add))
    v.scalar_tensor_tensor(k.h1[:], over_features(k.ss[:]), -1.0 / D, k.h1[:], ALU.mult, ALU.add).then_inc(s.h_centred, 1)
    rstd(2 * m + 2)
    link(v.tensor_tensor(k.t1[:], k.h1[:], rows_of(k.wfg[:], G), ALU.mult))
    link(v.tensor_reduce(k.ss[:], k.t1[:], AX, ALU.add))
    link(v.tensor_tensor(k.ss[:], k.ss[:], k.ra[:], ALU.mult))
    return v.tensor_scalar(out, k.ss[:], k.wfb[:], 0.0, ALU.add, ALU.max)


def close_layer(nc, z, k, layer, n, table):
    s = k.s
    with nc.Block() as block:
        @block.vector
        def _(v):
            link = Links(v, s.close_link[layer], {0: 4, 1: 1, 2: 4}[layer] + 6)
            link.run(0)
            sums, tmp = k.acc[:, :, 0:D], k.tab[:, :, 0:D]
            if layer != 1:
                link(v.reciprocal(k.nstat[:, 0, :], k.acc[:, :, D]))
                link(v.tensor_tensor(tmp, sums, over_features(k.nstat[:, 0, :]), ALU.mult))
            if layer == 0:
                link(v.tensor_tensor(k.x[:], k.x[:], tmp, ALU.add))
                link(v.tensor_tensor(k.x[:], k.x[:], rows_of(k.bias0[:], z.NBK), ALU.add))
            if layer == 1:
                link(v.tensor_tensor(k.x[:], k.x[:], sums, ALU.add))
            if layer == 2:
                link(v.scalar_tensor_tensor(tmp, tmp, 0.01, tmp, ALU.mult, ALU.max))
                link(v.tensor_tensor(k.x[:], k.x[:], tmp, ALU.add))
            norm_vector(v, k, z, link, s, n)
            link.end()
            v.memset(k.acc[:], 0.0).then_inc(s.norm_done, 1)

        @block.scalar
        def _(a):
            norm_scalar(a, k, s, n)

        @block.sync
        def _(sp):
            if table is not None:
                sp.wait_ge(s.norm_done, n + 1)
                sp.dma_start(table.rearrange("(b p) d -> p b d", p=P), k.hbuf[:]).then_inc(s.h_out, 16)
                sp.wait_ge(s.h_out, 16 if layer == 0 else 32)


def mlp_nodes(nc, z, k):
    s, groups = k.s, z.NBK // G
    dst = k.a2_dram.rearrange("(b p) d -> p b d", p=P)
    bank = k.bank

    def grouped(b):
        return bank[b].rearrange("p (g d) -> p g d", g=G)

    with nc.Block() as block:
        @block.scalar
        def _(a):
            def group(i):
                a.activation(k.hs[:], k.hbuf[:, ds(i * G, G), :], ACT.Copy).then_inc(s.hs_done, 1)
                a.wait_ge(s.hsT_done, i + 1)
                a.activation(k.hT[:], bank[6][0:D, :], ACT.Copy).then_inc(s.hT_done, 1)
                a.wait_ge(s.ab_done, i + 1)
                after(a, s.a_out, 16 * i)
                a.activation(k.a_st[:], grouped(0), ACT.Copy).then_inc(s.a_done, 1)
                a.wait_ge(s.zs_done, i + 1)
                a.activation(k.acc[:, ds(i * G, G), 0:D], k.zs[:, :, 0:D], ACT.Copy)
                a.activation(k.tab[:, ds(i * G, G), :], k.b_st[:], ACT.Copy).then_inc(s.b_kept, 1)
                mlp_scalar(a, k, i, k.zs[:, :, D:2 * D])
            counted(a, groups, group)

        @block.sync
        def _(sp):
            def group(i):
                sp.wait_ge(s.a_done, i + 1)
                sp.dma_start(dst[:, ds(i * G, G), :], k.a_st[:]).then_inc(s.a_out, 16)
            counted(sp, groups, group)
            sp.wait_ge(s.a_out, 16 * groups)

        @block.tensor
        def _(pe):
            def group(i):
                after(pe, s.hs_done, i + 1, alone=True)
                for g in range(G):
                    last = pe.transpose(bank[6][0:D, g * P:(g + 1) * P], k.hs[:, g, :], k.ident[:])
                last.then_inc(s.hsT_done, 1)
                after(pe, s.hT_done, i + 1, alone=True)
                for b, w in ((0, k.wqa), (1, k.wqb)):
                    for g in range(G):
                        last = pe.matmul(bank[b][:, g * P:(g + 1) * P], k.hT[:, g * P:(g + 1) * P], w[:],
                                         start=True, stop=True)
                last.then_inc(s.ab_done, 1)
                mlp_tensor(pe, k, i)
            counted(pe, groups, group)

        @block.vector
        def _(v):
            link = Links(v, s.m_link, MLP_LINKS + 2)
            v.memset(k.acc[:, :, D:D + 1], 1.0).then_inc(s.one_set, 1)
            def group(i):
                link.run(i)
                v.wait_ge(s.a_done, i + 1)
                after(v, s.b_kept, i)
                link(v.tensor_tensor(k.b_st[:], grouped(1), rows_of(k.bq0[:], G), ALU.add))
                v.tensor_tensor(k.zs[:], k.b_st[:], k.a_st[:], ALU.add).then_inc(s.zs_done, 1)
                link(mlp_vector(v, k, link, i, k.macc[:, ds(i * G, G)]))
                link.end()
            counted(v, groups, group)


def last_nodes(nc, io, z, k):
    s, groups = k.s, z.NBK // G
    full = z.N // P
    with nc.Block() as block:
        @block.scalar
        def _(a):
            def group(i):
                for part, src in ((0, k.hbuf), (1, k.acc)):
                    n = 2 * i + part
                    a.activation(k.hs[:], src[:, ds(i * G, G), 0:D], ACT.Copy).then_inc(s.l_hs, 1)
                    a.wait_ge(s.l_hsT, n + 1)
                    a.activation(k.hT[:], k.bank[6][0:D, :], ACT.Copy).then_inc(s.l_hT, 1)
                    a.wait_ge(s.l_y, n + 1)
            counted(a, groups, group)

        @block.tensor
        def _(pe):
            def group(i):
                for part in range(2):
                    n = 2 * i + part
                    after(pe, s.l_hs, n + 1, alone=True)
                    for g in range(G):
                        last = pe.transpose(k.bank[6][0:D, g * P:(g + 1) * P], k.hs[:, g, :], k.ident[:])
                    last.then_inc(s.l_hsT, 1)
                    after(pe, s.l_hT, n + 1, alone=True)
                    after(pe, s.l_x, i, alone=True)
                    for g in range(G):
                        last = pe.matmul(k.bank[part][:, g * D:(g + 1) * D], k.hT[:, g * P:(g + 1) * P], k.w3[:, part, :],
                                         start=True, stop=True)
                    last.then_inc(s.l_y, 1)
            counted(pe, groups, group)

        @block.vector
        def _(v):
            link = Links(v, s.l_link, 2)
            def group(i):
                link.run(i)
                x = k.x[:, ds(i * G, G), :]
                y = [k.bank[b][:, 0:G * D].rearrange("p (g d) -> p g d", g=G) for b in range(2)]
                v.wait_ge(s.l_y, 2 * i + 2)
                link(v.tensor_tensor(x, x, y[0], ALU.add))
                link(v.tensor_tensor(x, x, y[1], ALU.add))
                v.tensor_tensor(x, x, rows_of(k.b3[:], G), ALU.add).then_inc(s.l_x, 1)
            counted(v, groups, group)

        @block.sync
        def _(sp):
            sp.wait_ge(s.l_x, groups)
            sp.dma_start(io.out[0:full * P, :].rearrange("(b p) d -> p b d", p=P), k.x[:, 0:full, :]).then_inc(s.out_done, 16)
            rest = z.N - full * P
            if rest:
                sp.dma_start(io.out[full * P:z.N, :], k.x[0:rest, full, :]).then_inc(s.out_done, 16)
            sp.wait_ge(s.out_done, 32 if rest else 16)


def build(nc, io, n, e):
    z = Sizes(n, e)
    NBK, NBUCK, C = z.NBK, z.NBUCK, z.C
    with ExitStack() as top:
        k = Place()
        names = []

        def sems(**more):
            out = named()
            return out

        def sem(name):
            return top.enter_context(nc.semaphore(name))

        def sb(name, shape, dt=F32, ctx=top):
            return ctx.enter_context(nc.sbuf_tensor(name, shape, dt))

        def dram(name, shape, dt=F32):
            return nc.dram_tensor(name, shape, dt, kind="Internal").ap()

        k.xl_dram = dram("xl_dram", (NBK * P, D))
        k.h1_dram = dram("h1_dram", (NBK * P, D))
        k.h3_dram = dram("h3_dram", (NBK * P, D))
        k.a2_dram = dram("a2_dram", (NBK * P, 2 * D))
        k.recd_dram = dram("recd_dram", (z.EP, RECD))
        k.recs_dram = dram("recs_dram", (z.EP, RECS))
        k.off_dram = [dram(f"off{o}_dram", (P * z.SJ,), I32) for o in "ds"]
        k.blk_dram = [dram(f"blk{o}_dram", (P * z.SJ,), I32) for o in "ds"]
        k.b128_dram = [dram(f"b128{o}_dram", (P * z.SJ,)) for o in "ds"]

        k.x = sb("x", [P, NBK, D])
        k.tab = sb("tab", [P, NBK, 2 * D])
        k.acc = sb("acc", [P, NBK, D + 1])
        k.macc = sb("macc", [P, NBK])
        k.hbuf = sb("hbuf", [P, NBK, D])
        k.nstat = sb("nstat", [P, 3, NBK])
        k.b128 = [sb(f"b128_{o}", [P, P * z.SJ]) for o in "ds"]
        k.steps = sb("steps", [4, P * z.SJ], I32)
        k.offs = [k.steps[2 * o:2 * o + 1, :] for o in (DST, SRC)]
        k.blks = [k.steps[2 * o + 1:2 * o + 2, :] for o in (DST, SRC)]
        k.ident = sb("ident", [P, P])
        k.identb = sb("identb", [P, P], BF16)
        k.iota = sb("iota", [P, P])
        k.pidx = sb("pidx", [P, 1])
        k.pidx2 = sb("pidx2", [P, 1])
        k.attw = sb("attw", [P, D])
        k.bias0 = sb("bias0", [P, D])
        k.wlr = sb("wlr", [D, 2 * D])
        k.wqa = sb("wqa", [D, 2 * D])
        k.wqb = sb("wqb", [D, 2 * D])
        k.wqe = sb("wqe", [EA, 2 * D])
        k.bq0 = sb("bq0", [P, 2 * D])
        k.w1g = sb("w1g", [D, D])
        k.w1b = sb("w1b", [P, D])
        k.wfg = sb("wfg", [P, D])
        k.wfb = sb("wfb", [P, 1])
        k.w3 = sb("w3", [D, 2, D])
        k.b3 = sb("b3", [P, D])
        k.zero = sb("zero", [P, 1])
        k.epsn = sb("epsn", [P, 1])
        k.hs = sb("hs", [P, G, D])
        k.hT = sb("hT", [D, G * P])
        k.bank = [top.enter_context(nc.psum_tensor(f"bank{i}", [P, 512], F32)) for i in range(8)]

        with ExitStack() as early:
            k.w1 = sb("w1", [D, D], ctx=early)
            k.g0 = sb("g0", [D, 1], ctx=early)
            k.beta0 = sb("beta0", [D, 1], ctx=early)
            k.beta0w = sb("beta0w", [D, P], ctx=early)
            k.beta1 = sb("beta1", [P, D], ctx=early)
            k.wf = sb("wf", [P, D], ctx=early)
            k.b3n = sb("b3n", [P, D], ctx=early)
            k.before = sb("before", [P, P], ctx=early)
            k.ones = sb("ones", [P, P], ctx=early)
            k.csem = named(**{m: sem(m) for m in ("consts", "iota", "clink", "beta_wide", "beta_w1")})
            load_constants(nc, io, z, k)

            k.order = [named(
                key_int=sb(f"key_int{o}", [P, C], I32, early),
                pos_int=sb(f"pos_int{o}", [P, C], I32, early)) for o in "ds"]
            k.w = sb("w", [P, C], ctx=early)
            k.hi = sb("hi", [P, C], BF16, early)
            k.same = sb("same", [P, C], U8, early)
            k.run = sb("run", [P, C // CH], I32, early)
            (k.cnt, k.cnt2, k.tot, k.goff, k.base, k.nst, k.send, k.lead, k.jump, k.ended, k.ended2) = [
                sb(t, [P, NBUCK], ctx=early)
                for t in ("cnt", "cnt2", "tot", "goff", "base", "nst", "send", "lead", "jump", "ended", "ended2")]
            k.nst_int = sb("nst_int", [P, NBUCK], I32, early)
            k.step_no, k.blk, k.off, k.off2, k.blk128 = [
                sb(t, [P, z.SJ], ctx=early) for t in ("step_no", "blk", "off", "off2", "blk128")]
            k.off_int = sb("off_int", [P, z.SJ], I32, early)
            k.blk_int = sb("blk_int", [P, z.SJ], I32, early)
            k.attr_in = sb("attr_in", [P, 2, SC, EA], ctx=early)
            k.rec = sb("rec", [P, 2, SC, RECD], ctx=early)
            k.pos_st = sb("pos_st", [P, 2, SC], I32, early)
            k.s1 = named(
                ranked=[sem("ranked_dst"), sem("ranked_src")], tables_out=[sem("tables_out_dst"), sem("tables_out_src")],
                attr_loaded=[sem("attr_loaded0"), sem("attr_loaded1")], scattered=[sem("scattered0"), sem("scattered1")],
                **{m: sem("first_" + m) for m in (
                    "rank_link", "counted", "count_sums", "off_sum", "tables_done", "tables_in", "x_loaded", "dst_loaded",
                    "src_loaded", "w_loaded", "xl_done", "xl_out", "staged", "norm_done", "hs_done", "hsT_done", "hT_done",
                    "proj_done", "nlink", "var_done", "sqrt_done", "step_no_done")})
            sort_and_project(nc, io, z, k)

        k.win = sb("win", [P, R, G, RECD])
        k.rows = sb("rows", [P, R, G, 2 * D])
        k.lo = sb("lo", [P, 2, G])
        k.hot = sb("hot", [P, 2, G, P], BF16)
        k.hotT = sb("hotT", [P, 2, G, P])
        k.negT = sb("negT", [P, 2, G, P], BF16)
        k.atT = sb("atT", [EA, 2, G, P])
        k.val = sb("val", [P, 2, G, D + 1])
        small = {}
        for t, shape in {
            "tmp": (G, D), "h0": (G, D), "h1": (G, D), "sq": (G, D), "t1": (G, D), "e": (2, G), "eh": (G, P),
            "ph": (G, P), "ms": (G,), "mn": (G,), "dd": (G, 2), "cc": (G, 2), "ts": (G, D + 1), "de": (G,), "p": (G,),
            "ss": (G,), "var": (G,), "lnv": (G,), "r0": (G,), "ra": (G,), "a_st": (G, 2 * D),
            "b_st": (G, 2 * D), "zs": (G, 2 * D),
        }.items():
            small[t] = sb(t, [P, *shape])
        k.s = named(
            win_loaded=[sem(f"win_loaded{r}") for r in range(R)], gathered=[sem(f"gathered{r}") for r in range(R)],
            swin_loaded=[sem(f"swin_loaded{r}") for r in range(R)], sgathered=[sem(f"sgathered{r}") for r in range(R)],
            x_link=[sem("x_link0"), sem("x_link1")], y_link=[sem("y_link0"), sem("y_link1")],
            close_link=[sem(f"close_link{i}") for i in range(3)],
            **{m: sem(m) for m in (
                "s_done", "atT_p_done", "atT_done", "hotT_p_done", "hotT_done", "z_done", "relu_done", "de_done", "p_done",
                "ph_done", "dd_done", "cc_done", "hot_done", "eh_done", "mx_done", "ms_done", "me_done", "ts_done",
                "ones_set", "e_done", "w_sum", "w_hot", "w_acc", "w_lo", "a_link", "h_relu", "h_centred", "h_sq",
                "hcT_p_done", "hcT_done", "v_done", "ln_done", "r_guess", "t_done", "h1_relu", "y_done", "h_out",
                "hsT_done", "hT_done", "hs_done", "ab_done", "a_out", "a_done", "zs_done", "b_kept", "m_link",
                "one_set", "l_hs", "l_hsT", "l_hT", "l_y", "l_x", "l_link", "out_done", "var_done", "sqrt_done",
                "norm_done")})

        k.tmp, k.h0, k.h1, k.sq, k.t1, k.e, k.eh, k.ph, k.ms, k.mn, k.dd, k.cc, k.ts, k.de, k.p = [small[t] for t in (
            "tmp", "h0", "h1", "sq", "t1", "e", "eh", "ph", "ms", "mn", "dd", "cc", "ts", "de", "p")]
        k.ss, k.var, k.lnv, k.r0, k.ra, k.a_st, k.b_st, k.zs = [small[t] for t in (
            "ss", "var", "lnv", "r0", "ra", "a_st", "b_st", "zs")]
        softmax_edges(nc, z, k, 0, False)
        close_layer(nc, z, k, 0, 0, k.h1_dram)
        sum_edges(nc, z, k, 0, k.h1_dram)
        close_layer(nc, z, k, 1, 1, None)
        mlp_nodes(nc, z, k)
        softmax_edges(nc, z, k, z.NG, True)
        close_layer(nc, z, k, 2, 2, k.h3_dram)
        sum_edges(nc, z, k, z.NG, k.h3_dram)
        last_nodes(nc, io, z, k)


def kernel(**inputs):
    import numpy as _np
    import concourse.bacc as _bacc
    from concourse.bass_utils import run_bass_kernel_spmd as _run

    a = {name: _np.asarray(value) for name, value in inputs.items()}
    n, e = a["x"].shape[0], a["src"].shape[0]
    z = Sizes(n, e)
    nodes = (0, z.NBK * P - n)
    edges = (0, z.EP - e)
    laid = {
        "x": _np.pad(a["x"], (nodes, (0, 0))),
        "src": _np.pad(a["src"], edges, constant_values=z.PADKEY),
        "dst": _np.pad(a["dst"], edges, constant_values=z.PADKEY),
        "w": _np.pad(a["edge_weight"], edges),
        "attr": _np.pad(a["edge_attr_16"], (edges, (0, 0))),
        "W_l": a["L0_gnn_W_l"], "W_r": a["L0_gnn_W_r"], "att": a["L0_gnn_att"], "bias": a["L0_gnn_bias"],
        "Wq": a["L2_gnn_Wq"], "bq": a["L2_gnn_bq"], "W0": a["L2_gnn_W0"], "b0": a["L2_gnn_b0"],
        "g0": a["L2_gnn_g0"].reshape(D, 1), "beta0": a["L2_gnn_beta0"].reshape(D, 1),
        "W1": a["L2_gnn_W1"], "b1": a["L2_gnn_b1"], "g1": a["L2_gnn_g1"], "beta1": a["L2_gnn_beta1"],
        "Wf": a["L2_gnn_Wf"].reshape(D), "bf": a["L2_gnn_bf"],
        "W_selfT": a["L3_gnn_W_self"].T, "W_neighT": a["L3_gnn_W_neigh"].T,
        "b_self": a["L3_gnn_b_self"], "b_neigh": a["L3_gnn_b_neigh"],
    }
    nc = _bacc.Bacc("TRN2", target_bir_lowering=False, num_devices=1)
    arrays, tensors = {}, {}
    for name, value in laid.items():
        value = _np.ascontiguousarray(value)
        arrays[f"in_{name}"] = value
        t = nc.dram_tensor(f"in_{name}", value.shape, mybir.dt.from_np(value.dtype), kind="ExternalInput").ap()
        tensors[name] = t
    tensors["out"] = nc.dram_tensor("out", (n, D), F32, kind="ExternalOutput").ap()
    io = named(**tensors)
    build(nc, io, n, e)
    r = _run(nc, [arrays], core_ids=[0])
    return r.results[0]["out"]
```

```python
from contextlib import ExitStack
from collections import namedtuple

import numpy as np
import concourse.bass as bass
from concourse import mybir

P = 128
D = 64
F32 = mybir.dt.float32
BF16 = mybir.dt.bfloat16
I32 = mybir.dt.int32
U32 = mybir.dt.uint32
U8 = mybir.dt.uint8
ALU = mybir.AluOpType
ACT = mybir.ActivationFunctionType
AX = mybir.AxisListType.X
ds = bass.ds

EA = 16
G = 4
R = 8
CH = 3
SC = 3
RECD = 2 + EA
RECS = 3
NEG = -(2.0 ** 100)
EPS_NODE = 1e-5
EPS_MLP = 1e-6
DST, SRC = 0, 1


class Sizes:
    def __init__(self, n, e):
        self.N, self.E = n, e
        self.NB = -(-n // P)
        self.NBUCK = self.NB + 1
        self.NBK = -(-(self.NB + 1) // G) * G
        self.PADKEY = self.NB * P
        self.C = -(-(e + P) // (P * CH * SC * 2)) * (CH * SC * 2)
        self.EP = self.C * P
        self.STEPS = -(-(e // P + self.NB) // (G * R)) * (G * R)
        self.NG = self.STEPS // G
        self.NIT = self.NG // R
        self.SJ = -(-self.STEPS // P)
        assert self.NIT >= 3 and self.STEPS >= self.C


class Place:
    pass


def named(**values):
    return namedtuple("Named", values.keys())(*values.values())


def after(eng, sem, value, alone=False):
    if not (isinstance(value, int) and value <= 0):
        eng.wait_ge(sem, value)
        if alone:
            eng.nop(nofuse=True)


class Links:

    def __init__(self, eng, sem, per):
        self.eng, self.sem, self.per = eng, sem, per

    def run(self, n):
        self.start, self.n = n * self.per, 0

    def __call__(self, ins):
        self.n += 1
        ins.then_inc(self.sem, 1)
        self.eng.wait_ge(self.sem, self.start + self.n)

    def end(self):
        assert self.n == self.per, self.n


def over_nodes(ap):
    return ap.unsqueeze(2).broadcast_to([P, ap.shape[1], P])


def over_features(ap, d=D):
    return ap.unsqueeze(2).broadcast_to([P, ap.shape[1], d])


def rows_of(ap, m):
    return ap.unsqueeze(1).broadcast_to([P, m, ap.shape[1]])


class Group:

    def __init__(self, n, c, at, use):
        self.n, self.c, self.at, self.two, self.use = n, c, at, at % 2, use


def pipelined(eng, z, layer, stages):
    lag_max = max(lag for lag, _ in stages)
    lead = max(-(-lag_max // R), 1)

    def turn(it, j):
        for lag, what in stages:
            n = R * it + (j - lag)
            if isinstance(n, int) and not 0 <= n < z.NG:
                continue
            what(Group(n, (layer // 2) * z.NG + n, (j - lag) % R, layer * z.NIT + it + (j - lag) // R + 1))

    for t in range(lead * R):
        turn(t // R, t % R)
    with eng.Fori(lead, z.NIT) as it:
        for j in range(R):
            turn(it, j)
    for t in range(z.NG, z.NG + lag_max):
        turn(t // R, t % R)



def counted(eng, n, body):
    body(0)
    with eng.Fori(1, n) as i:
        body(i)


def load_constants(nc, io, z, k):
    loads = [
        (k.attw[:], io.att.partition_broadcast(P)), (k.bias0[:], io.bias.partition_broadcast(P)),
        (k.wlr[:, 0:D], io.W_l), (k.wlr[:, D:2 * D], io.W_r),
        (k.wqa[:, 0:D], io.Wq[0:D, :]), (k.wqa[:, D:2 * D], io.W0[0:D, :]),
        (k.wqb[:, 0:D], io.Wq[D:2 * D, :]), (k.wqb[:, D:2 * D], io.W0[D:2 * D, :]),
        (k.bq0[:, 0:D], io.bq.partition_broadcast(P)), (k.bq0[:, D:2 * D], io.b0.partition_broadcast(P)),
        (k.w1[:], io.W1), (k.g0[:], io.g0), (k.beta0[:], io.beta0),
        (k.w1b[:], io.b1.partition_broadcast(P)), (k.g1[:], io.g1.rearrange("(p a) -> p a", a=1)),
        (k.wfcol[:], io.Wf.rearrange("(p a) -> p a", a=1)),
        (k.beta1[:], io.beta1.partition_broadcast(P)), (k.wf[:], io.Wf.partition_broadcast(P)),
        (k.wfb[:], io.bf.partition_broadcast(P)),
        (k.w3[:, 0, :], io.W_selfT), (k.w3[:, 1, :], io.W_neighT),
        (k.b3[:], io.b_self.partition_broadcast(P)), (k.b3n[:], io.b_neigh.partition_broadcast(P)),
    ]
    s = k.csem
    with nc.Block() as block:
        @block.sync
        def _(sp):
            for out, src in loads:
                sp.dma_start(out, src).then_inc(s.consts, 16)
            sp.wait_ge(s.wqe_clear, 1)
            for g in range(G):
                at = slice(g * RECD + 2, (g + 1) * RECD)
                sp.dma_start(k.wqe4[at, g, 0:D], io.Wq[2 * D:2 * D + EA, :]).then_inc(s.wqe_in, 16)
                sp.dma_start(k.wqe4[at, g, D:2 * D], io.W0[2 * D:2 * D + EA, :]).then_inc(s.wqe_in, 16)
            sp.wait_ge(s.wqe_in, 32 * G)

        @block.gpsimd
        def _(pool):
            pool.iota(k.iota[:], [[1, P]], base=0, channel_multiplier=0,
                      allow_small_or_imprecise_dtypes=True).then_inc(s.iota, 1)
            pool.iota(k.pidx[:], [[0, 1]], base=0, channel_multiplier=1,
                      allow_small_or_imprecise_dtypes=True).then_inc(s.iota, 1)

        @block.vector
        def _(v):
            link = Links(v, s.clink, 13)
            link.run(0)
            v.memset(k.wqe4[:], 0.0).then_inc(s.wqe_clear, 1)
            v.wait_ge(s.iota, 2)
            v.tensor_copy(k.iotab[:], k.iota[:])
            v.tensor_scalar(k.identb[:], k.iota[:], k.pidx[:], None, ALU.is_equal)
            v.memset(k.steps[:, 0:1], 0)
            link(v.tensor_scalar(k.ident[:], k.iota[:], k.pidx[:], None, ALU.is_equal))
            link(v.tensor_scalar(k.centre[:], k.ident[0:D, 0:D], -1.0 / D, None, ALU.add))
            link(v.tensor_scalar(k.before[:], k.iota[:], k.pidx[:], None, ALU.is_gt))
            link(v.memset(k.ones[:], 1.0))
            v.wait_ge(s.consts, 16 * len(loads))
            link(v.tensor_copy(k.beta0w[:], k.beta0[:].broadcast_to([D, P])))
            link(v.tensor_scalar(k.wfcol[:], k.wfcol[:], k.g1[:], None, ALU.mult))
            v.tensor_scalar(k.w1g[:], k.w1[:], k.g0[:], None, ALU.mult).then_inc(s.weights_scaled, 1)
            v.wait_ge(s.products, 1)
            link(v.tensor_tensor(k.w1b[:], k.w1b[:], k.bank[0][:, 0:D], ALU.add))
            v.tensor_copy(k.w1c[:, 0:D], k.bank[1][0:D, 0:D])
            v.tensor_copy(k.w1c[:, D:2 * D], k.centre[:])
            v.tensor_copy(k.w2c[:, 0:D], k.centre[:])
            v.tensor_copy(k.w2c[:, D:D + 1], k.bank[2][0:D, 0:1])
            link(v.tensor_tensor(k.beta1[:], k.beta1[:], k.wf[:], ALU.mult))
            link(v.tensor_reduce(k.pidx2[:], k.beta1[:], AX, ALU.add))
            link(v.tensor_tensor(k.wfb[:], k.wfb[:], k.pidx2[:], ALU.add))
            link(v.tensor_tensor(k.b3[:], k.b3[:], k.b3n[:], ALU.add))
            link(v.memset(k.nstat[:], 0.0))
            link(v.memset(k.pidx2[:], 0.0))
            link.end()

        @block.tensor
        def _(pe):
            pe.wait_ge(s.weights_scaled, 1)
            pe.matmul(k.bank[0][:, 0:D], k.beta0w[:], k.w1[:], start=True, stop=True)
            pe.matmul(k.bank[1][0:D, 0:D], k.centre[:], k.w1g[:], start=True, stop=True)
            pe.matmul(k.bank[2][0:D, 0:1], k.centre[:], k.wfcol[:], start=True, stop=True).then_inc(s.products, 1)


def norm_vector(v, k, z, link, s, n):
    nb = z.NBK
    link(v.tensor_reduce(k.nstat[:, 0, :], k.x[:], AX, ALU.add))
    link(v.scalar_tensor_tensor(k.hbuf, over_features(k.nstat[:, 0, :]), -1.0 / D, k.x[:], ALU.mult, ALU.add))
    link(v.tensor_tensor(k.tab[:, :, 0:D], k.hbuf, k.hbuf, ALU.mult))
    link(v.tensor_reduce(k.nstat[:, 1, :], k.tab[:, :, 0:D], AX, ALU.add))
    v.tensor_scalar(k.nstat[:, 2, :], k.nstat[:, 1, :], 1.0 / D, EPS_NODE, ALU.mult, ALU.add).then_inc(s.nvar_done, 1)
    v.wait_ge(s.nsqrt_done, n + 1)
    link(v.reciprocal(k.nstat[:, 1, :], k.nstat[:, 0, :]))
    link(v.scalar_tensor_tensor(k.hbuf, k.hbuf, 0.0, over_features(k.nstat[:, 1, :]), ALU.max, ALU.mult))


def norm_scalar(a, k, s, n):
    a.wait_ge(s.nvar_done, n + 1)
    a.activation(k.nstat[:, 0, :], k.nstat[:, 2, :], ACT.Sqrt).then_inc(s.nsqrt_done, 1)


def rank_edges(v, k, z, key, n):
    s, cc = k.s1, z.C // CH
    rank_link = s.rank_link[key]
    link = Links(v, rank_link, 13 + (2 if key == DST else 0) + 2 * z.SJ + z.NBUCK + CH * 3 * z.NBUCK)
    link.run(0)
    o = k.order[key]
    link(v.tensor_scalar(o.pos_int[:], o.key_int[:], 7, None, ALU.logical_shift_right))
    link(v.tensor_copy(k.hi[:], o.pos_int[:]))
    first = link.start + link.n
    with v.Fori(0, z.NBUCK) as b:
        v.tensor_scalar(k.same[:], k.hi[:], k.iota[:, ds(b, 1)], None, ALU.is_equal, ALU.add,
                        accum_out=k.cnt[:, ds(b, 1)]).then_inc(rank_link, 1)
        v.wait_ge(rank_link, first + b + 1)
    link.n += z.NBUCK
    v.tensor_copy(k.cnt2[:], k.cnt[:]).then_inc(s.counted, 1)
    v.wait_ge(s.count_sums, n + 1)
    nb = z.NBUCK
    low, tot = k.bank[0][:, 0:nb], k.bank[1][:, 0:nb]
    link(v.tensor_copy(k.tot[:], tot))
    link(v.tensor_tensor_scan(k.goff[:], k.tot[:], k.tot[:], -1.0, ALU.add, ALU.bypass))
    link(v.tensor_tensor(k.goff[:], k.goff[:], k.tot[:], ALU.subtract))
    link(v.tensor_tensor(k.base[:], k.goff[:], low, ALU.add))
    link(v.tensor_scalar(k.nst_int[:], k.tot[:], float(P - 1), None, ALU.add))
    link(v.tensor_scalar(k.nst_int[:], k.nst_int[:], 7, None, ALU.logical_shift_right))
    link(v.tensor_copy(k.nst[:], k.nst_int[:]))
    link(v.tensor_tensor_scan(k.send[:], k.nst[:], k.nst[:], 0.0, ALU.add, ALU.bypass))
    if key == DST:
        link(v.tensor_scalar(k.lead[:], k.nst[:], 1.0, None, ALU.min))
        link(v.tensor_tensor(k.lasts[:], k.lead[0:1, :], k.send[0:1, :], ALU.mult))
    link(v.tensor_tensor(k.lead[:], k.send[:], k.nst[:], ALU.subtract))
    link(v.scalar_tensor_tensor(k.lead[:], k.lead[:], float(-P), k.goff[:], ALU.mult, ALU.add))
    last = z.NB - 1
    link(v.tensor_tensor(k.jump[:, 0:last], k.lead[:, 1:z.NB], k.lead[:, 0:last], ALU.subtract))
    v.wait_ge(s.step_no_done, 1)
    for j in range(z.SJ):
        link(v.tensor_scalar(k.ended[:, 0:last], k.send[:, 0:last], k.step_no[:, j:j + 1], None, ALU.is_le, ALU.add,
                             accum_out=k.blk[:, j:j + 1]))
        link(v.tensor_tensor_reduce(k.ended2[:, 0:last], k.ended[:, 0:last], k.jump[:, 0:last], 1.0, 0.0, ALU.mult,
                                    ALU.add, k.off[:, j:j + 1]))
    v.scalar_tensor_tensor(k.off2[:], k.step_no[:], float(P), k.off[:], ALU.mult, ALU.add).then_inc(s.off_sum, 1)
    v.wait_ge(s.off_sum, n + 1)
    if n:
        v.wait_ge(s.tables_out[DST], 48)
    v.tensor_scalar(k.off_int[:], k.off2[:], float(z.E), None, ALU.min)
    v.tensor_copy(k.blk_int[:], k.blk[:])
    v.tensor_scalar(k.blk128[:], k.blk[:], float(P), None, ALU.mult).then_inc(s.tables_done, 1)
    for part in range(CH):
        cols = slice(part * cc, (part + 1) * cc)
        at = link.start + link.n
        with v.Fori(0, z.NBUCK) as b:
            v.tensor_scalar(k.same[:, 0:cc], k.hi[:, cols], k.iota[:, ds(b, 1)], None, ALU.is_equal).then_inc(rank_link, 1)
            v.wait_ge(rank_link, at + 3 * b + 1)
            v.tensor_tensor_scan(k.run[:], k.same[:, 0:cc], k.same[:, 0:cc], k.base[:, ds(b, 1)], ALU.add,
                                 ALU.bypass).then_inc(rank_link, 1)
            after(v, rank_link, at + 3 * b + 2, alone=True)
            v.tensor_copy(k.base[:, ds(b, 1)], k.run[:, cc - 1:cc])
            v.copy_predicated(o.pos_int[:, cols], k.same[:, 0:cc], k.run[:]).then_inc(rank_link, 1)
            v.wait_ge(rank_link, at + 3 * b + 3)
        link.n += 3 * z.NBUCK
        v.tensor_copy(k.pidx2[:], k.pidx[:]).then_inc(s.ranked[key], 1)
    link.end()


def sort_and_project(nc, io, z, k):
    s, NG25 = k.s1, z.NBK // G
    units = z.C // SC

    with nc.Block() as block:
        @block.sync
        def _(sp):
            sp.dma_start(k.x[:], io.x.rearrange("(b p) d -> p b d", p=P)).then_inc(s.x_loaded, 16)
            sp.dma_start(k.order[DST].key_int[:], io.dst.rearrange("(p c) -> p c", p=P)).then_inc(s.dst_loaded, 16)
            sp.dma_start(k.order[SRC].key_int[:], io.src.rearrange("(p c) -> p c", p=P)).then_inc(s.src_loaded, 16)
            sp.dma_start(k.w, io.w.rearrange("(p c) -> p c", p=P)).then_inc(s.w_loaded, 16)

            def tables_to_dram(n, key):
                sp.wait_ge(s.tables_done, n + 1)
                for tile, dram in ((k.off_int, k.off_dram), (k.blk_int, k.blk_dram), (k.blk128, k.b128_dram)):
                    sp.dma_start(dram[key].rearrange("(p j) -> p j", p=P), tile[:]).then_inc(s.tables_out[key], 16)
                sp.wait_ge(s.tables_out[key], 48)
                sp.dma_start(k.offs[key], k.off_dram[key].partition_broadcast(1)).then_inc(s.tables_in, 16)
                sp.dma_start(k.blks[key][:, 1:P * z.SJ + 1], k.blk_dram[key].partition_broadcast(1)).then_inc(s.tables_in, 16)

            tables_to_dram(0, DST)
            sp.wait_ge(s.xl_done, NG25)
            sp.dma_start(k.xl_dram.rearrange("(b p) d -> p b d", p=P), k.hbuf).then_inc(s.xl_out, 16)
            attr = io.attr.rearrange("(p c) f -> p c f", p=P)

            def load_attr(it, half):
                u = 2 * it + half
                after(sp, s.staged, u - 1)
                sp.dma_start(k.attr_in[:, half], attr[:, ds(u * SC, SC), :]).then_inc(s.attr_loaded[half], 16)

            for half in range(2):
                load_attr(0, half)
            with sp.Fori(1, units // 2) as it:
                for half in range(2):
                    load_attr(it, half)
            tables_to_dram(1, SRC)
            sp.wait_ge(s.tables_in, 64)
            sp.wait_ge(s.xl_out, 16)

        @block.scalar
        def _(a):
            norm_scalar(a, k, s, 0)
            a.wait_ge(s.norm_done, 1)

            def project(i):
                a.activation(k.hs[:], k.hbuf[:, ds(i * G, G), :], ACT.Copy).then_inc(s.hs_done, 1)
                a.wait_ge(s.hsT_done, i + 1)
                a.activation(k.hTn[:], k.bank[6][0:D, :], ACT.Copy).then_inc(s.hT_done, 1)
                after(a, s.proj_done, i + 1, alone=True)
                pr = k.bank[0].rearrange("p (g d) -> p g d", g=G)
                a.activation(k.hbuf[:, ds(i * G, G), :], pr[:, :, 0:D], ACT.Copy)
                a.activation(k.tab[:, ds(i * G, G), 0:D], pr[:, :, D:2 * D], ACT.Copy).then_inc(s.xl_done, 1)

            with a.Fori(0, NG25) as i:
                project(i)

            def stage(key, n, it, half):
                u = 2 * it + half
                cols = ds(u * SC, SC)
                o, other = k.order[key], k.order[1 - key]
                rec = k.rec[:, half]
                after(a, s.scattered[half], 16 * SC * (it + n * (units // 2)))
                if key == DST:
                    a.wait_ge(s.attr_loaded[half], 16 * (it + 1))
                    a.activation(rec[:, :, 2:RECD], k.attr_in[:, half], ACT.Copy)
                else:
                    a.activation(rec[:, :, 2], k.w[:, cols], ACT.Copy)
                a.activation(rec[:, :, 0].bitcast(I32), other.key_int[:, cols], ACT.Copy)
                a.activation(rec[:, :, 1], o.key_int[:, cols], ACT.Copy)
                a.activation(k.pos_st[:, half], o.pos_int[:, cols], ACT.Copy).then_inc(s.staged, 1)

            def stage_all(key, n):
                for half in range(2):
                    stage(key, n, 0, half)
                with a.Fori(1, units // 2) as it:
                    for half in range(2):
                        stage(key, n, it, half)

            a.wait_ge(s.src_loaded, 16)
            a.wait_ge(s.dst_loaded, 16)
            a.wait_ge(s.ranked[DST], CH)
            stage_all(DST, 0)
            a.wait_ge(s.w_loaded, 16)
            a.wait_ge(s.ranked[SRC], CH)
            stage_all(SRC, 1)

        @block.tensor
        def _(pe):
            def project(i):
                after(pe, s.hs_done, i + 1, alone=True)
                for g in range(G):
                    last = pe.transpose(k.bank[6][0:D, g * P:(g + 1) * P], k.hs[:, g, :], k.ident[:])
                last.then_inc(s.hsT_done, 1)
                pe.wait_ge(s.hT_done, i + 1)
                for g in range(G):
                    last = pe.matmul(k.bank[0][:, g * P:(g + 1) * P], k.hTn[:, g * P:(g + 1) * P], k.wlr[:],
                                     start=True, stop=True)
                last.then_inc(s.proj_done, 1)

            with pe.Fori(0, NG25) as i:
                project(i)

            def count_sums(n):
                pe.wait_ge(s.counted, n + 1)
                pe.matmul(k.bank[0][:, 0:z.NBUCK], k.before[:], k.cnt2[:], start=True, stop=True)
                pe.matmul(k.bank[1][:, 0:z.NBUCK], k.ones[:], k.cnt2[:], start=True, stop=True).then_inc(s.count_sums, 1)

            pe.wait_ge(s.xl_done, NG25)
            count_sums(0)
            count_sums(1)

        @block.vector
        def _(v):
            link = Links(v, s.nlink, 11)
            link.run(0)
            v.wait_ge(s.x_loaded, 16)
            norm_vector(v, k, z, link, s, 0)
            v.tensor_copy(k.pidx2[:], k.pidx[:]).then_inc(s.norm_done, 1)
            v.wait_ge(s.dst_loaded, 16)
            rank_edges(v, k, z, DST, 0)
            v.wait_ge(s.xl_done, NG25)
            low, tmp = k.acc[:, :, 0:D], k.tab[:, :, D:2 * D]
            link(v.tensor_tensor(low, k.hbuf, k.tab[:, :, 0:D], ALU.add))
            link(v.scalar_tensor_tensor(tmp, low, 0.2, low, ALU.mult, ALU.max))
            link(v.tensor_tensor(low, tmp, rows_of(k.attw[:], z.NBK), ALU.mult))
            link(v.tensor_reduce(k.eself[:], low, AX, ALU.add))
            link(v.memset(k.acc[:], 0.0))
            link.end()
            v.wait_ge(s.src_loaded, 16)
            rank_edges(v, k, z, SRC, 1)

        @block.gpsimd
        def _(pool):
            pool.iota(k.step_no[:], [[1, z.SJ]], base=0, channel_multiplier=z.SJ,
                      allow_small_or_imprecise_dtypes=True).then_inc(s.step_no_done, 1)

            def scatter(key, it, half, n):
                u = 2 * it + half
                dram, width = (k.recd_dram, RECD) if key == DST else (k.recs_dram, RECS)
                after(pool, s.staged, n * units + u + 1, alone=True)
                for c in range(SC):
                    pool.indirect_dma_start(
                        dram, bass.IndirectOffsetOnAxis(ap=k.pos_st[:, half, c:c + 1].bitcast(U32), axis=0),
                        k.rec[:, half, c, 0:width], None).then_inc(s.scattered[half], 16)

            for n, key in ((0, DST), (1, SRC)):
                with pool.Fori(0, units // 2) as it:
                    for half in range(2):
                        scatter(key, it, half, n)
            for half in range(2):
                pool.wait_ge(s.scattered[half], 16 * SC * units)


def softmax_edges(nc, z, k, layer):
    s, bank, mlp = k.s, k.bank, layer == 2
    first = z.NBK // G
    e_done, e0 = (s.logit_done, first) if mlp else (s.e_done, 0)
    table, width = (k.a2_dram, 2 * D) if mlp else (k.xl_dram, D)
    late = 4 if mlp else 2
    value = k.val if mlp else k.rows
    negT_p = bank[1].bitcast(BF16)[:, 0:G * P].rearrange("p (g n) -> p g n", g=G)
    atT_p = bank[1][0:G * RECD, 3 * P:4 * P]
    mx_p = bank[2].rearrange("p (g n) -> p g n", g=G)
    sum_p = bank[3][:, 0:G * (D + 1)].rearrange("p (g d) -> p g d", g=G)
    me_p = bank[3][:, 2 * P + 64:2 * P + 64 + G]

    def z_p(two):
        return bank[0][:, 0:G * width] if mlp else bank[0][:, two * G * D:(two + 1) * G * D]

    def loaded(g):
        return 16 * G * g.use

    with nc.Block() as block:
        @block.sync
        def _(sp):
            sp.dma_start(k.b128[:], k.b128_dram[DST].partition_broadcast(P)).then_inc(s.table_in, 16)

            def load_windows(g):
                after(sp, s.s_done, g.c - R + 1)
                for i in range(G):
                    off = sp.value_load(k.offs[DST][0:1, ds(g.n * G + i, 1)], min_val=0, max_val=z.E)
                    sp.dma_start(k.win[:, g.at, i, :], k.recd_dram[ds(off, P), :]).then_inc(s.win_loaded[g.at], 16)
            pipelined(sp, z, layer, [(0, load_windows)])

        @block.gpsimd
        def _(pool):
            def gather(g):
                after(pool, s.s_done, g.c - R + 1, alone=True)
                after(pool, s.win_loaded[g.at], loaded(g), alone=True)
                for i in range(G):
                    pool.indirect_dma_start(
                        k.rows[:, g.at, i, 0:width], None, table,
                        bass.IndirectOffsetOnAxis(ap=k.win[:, g.at, i, 0:1].bitcast(U32), axis=0)
                    ).then_inc(s.gathered[g.at], 16)
            pipelined(pool, z, layer, [(0, gather)])

        @block.scalar
        def _(a):
            def mask_logits(g):
                after(a, e_done, e0 + g.n + 1)
                after(a, s.ehT_done, g.c - 1)
                for i in range(G):
                    last = a.activation(k.eh[:, g.two, i, :], k.neg[:, g.at, i, :], ACT.Identity,
                                        bias=k.e[:, g.at, i:i + 1])
                last.then_inc(s.eh_done, 1)

            def copy_one_hots(g):
                after(a, s.negT_done, g.c + 1)
                if mlp:
                    a.activation(k.atT[:], atT_p, ACT.Copy)
                a.activation(k.hotT[:, g.at % 4], negT_p, ACT.Copy, scale=-1.0 / NEG, bias=1.0).then_inc(s.hotT_done, 1)

            def relu(g):
                after(a, s.z_done, g.c + 1)
                after(a, s.e_done, g.c)
                a.activation(k.tmp[:], z_p(g.two), ACT.Relu, scale=0.8).then_inc(s.relu_done, 1)

            def take_z(g):
                after(a, s.z_done, g.c + 1)
                q = z_p(0).rearrange("p (g d) -> p g d", g=G)
                a.activation(k.val[:, g.at, :, 0:D], q[:, :, 0:D], ACT.Copy)
                mlp_h0(a, k, q[:, :, D:2 * D], g.two, first + g.n)

            def exp_peaks(g):
                after(a, s.dd_done, g.c + 1)
                a.activation(k.cc[:, g.two], k.dd[:, g.two], ACT.Exp).then_inc(s.cc_done, 1)

            def exp_logits(g):
                after(a, s.nme_done, g.c + 1)
                after(a, s.s_done, g.c - 1)
                after(a, s.eh_done, g.c + 1)
                for i in range(G):
                    last = a.activation(k.ph[:, g.two, i, :], k.eh[:, g.two, i, :], ACT.Exp,
                                        bias=k.nme[:, g.two, i:i + 1])
                last.then_inc(s.ph_done, 1)

            if mlp:
                pipelined(a, z, layer, [
                    (2, lambda g: mlp_rstd_guess(a, k, 0, first + g.n)), (late, mask_logits), (3, lambda g: mlp_square1(a, k, first + g.n)),
                    (1, copy_one_hots), (2, lambda g: mlp_h1(a, k, first + g.n)), (1, take_z), (2, lambda g: mlp_copy1(a, k, first + g.n)),
                    (1, lambda g: mlp_copy0(a, k, first + g.n)), (3, lambda g: mlp_rstd_guess(a, k, 1, first + g.n)),
                    (late, exp_peaks), (late, exp_logits), (1, lambda g: mlp_square0(a, k, first + g.n))])
            else:
                pipelined(a, z, layer, [(late, mask_logits), (1, copy_one_hots), (1, relu), (late, exp_peaks), (late, exp_logits)])

        @block.tensor
        def _(pe):
            def sums(g):
                pe.wait_ge(s.ones_set, layer // 2 + 1)
                after(pe, s.ph_done, g.c + 1, alone=True)
                after(pe, s.ts_done, g.c, alone=True)
                for i in range(G):
                    last = pe.matmul(sum_p[:, i, :], k.ph[:, g.two, i, :], value[:, g.at, i, 0:D + 1], start=True, stop=True)
                last.then_inc(s.s_done, 1)

            def turn_one_hots(g):
                after(pe, s.neg_done, g.c + 1, alone=True)
                after(pe, s.hotT_done, g.c, alone=True)
                for i in range(G):
                    last = pe.transpose(negT_p[:, i, :], k.neg[:, g.at, i, :], k.identb[:])
                if mlp:
                    after(pe, s.z_done, g.c, alone=True)
                    last = pe.transpose(atT_p, k.win[:, g.at].rearrange("p g c -> p (g c)"), k.ident[:])
                last.then_inc(s.negT_done, 1)

            def turn_logits(g):
                after(pe, s.eh_done, g.c + 1, alone=True)
                after(pe, s.ms_done, g.c, alone=True)
                for i in range(G):
                    last = pe.transpose(mx_p[:, i, :], k.eh[:, g.two, i, :], k.ident[:])
                last.then_inc(s.ehT_done, 1)

            def add_rows(g):
                after(pe, s.gathered[g.at], loaded(g), alone=True)
                if mlp:
                    after(pe, s.h0_done, first + g.n, alone=True)
                else:
                    after(pe, s.e_done, g.c - 1, alone=True)
                zp = z_p(g.two).rearrange("p (g d) -> p g d", g=G)
                rows = k.rows[:, g.at, :, 0:width] if mlp else k.rows[:, g.at, :, 0:D]
                pe.matmul(zp, k.ident[:], rows, start=True, stop=False, skip_group_check=True)
                after(pe, s.hotT_done, g.c + 1, alone=True)
                if mlp:
                    pe.matmul(z_p(0), k.atT[:], k.wqe4[:], start=False, stop=False, skip_group_check=True)
                for i in range(G):
                    b = pe.value_load(k.blks[DST][0:1, ds(g.n * G + i + 1, 1)], min_val=0, max_val=z.NB - 1)
                    last = pe.matmul(zp[:, i, :], k.hotT[:, g.at % 4, i, :],
                                     k.tab[:, ds(b, 1), 0:width].rearrange("p a d -> p (a d)"),
                                     start=False, stop=(i == G - 1), skip_group_check=True)
                last.then_inc(s.z_done, 1)

            def peaks_of_edges(g):
                after(pe, s.ms_done, g.c + 1, alone=True)
                for i in range(G):
                    last = pe.matmul(me_p[:, i:i + 1], k.hotT[:, g.at % 4, i, :], k.ms[:, g.two, i:i + 1],
                                     start=True, stop=True)
                last.then_inc(s.me_done, 1)

            if mlp:
                pipelined(pe, z, layer, [
                    (late + 1, sums), (1, turn_one_hots), (late, turn_logits), (1, add_rows),
                    (2, lambda g: mlp_turn1(pe, k, first + g.n)), (late, peaks_of_edges), (1, lambda g: mlp_turn0(pe, k, g.two, first + g.n)),
                    (2, lambda g: mlp_second(pe, k, first + g.n)), (1, lambda g: mlp_first(pe, k, first + g.n))])
            else:
                pipelined(pe, z, layer, [(late + 1, sums), (1, turn_one_hots), (late, turn_logits), (1, add_rows),
                                  (late, peaks_of_edges)])

        @block.vector
        def _(v):
            start = Links(v, s.start_link, 4)
            start.run(layer // 2)
            v.memset(value[:, :, :, D:D + 1], 1.0).then_inc(s.ones_set, 1)
            link = Links(v, s.peak_link, 2)
            v.wait_ge(s.table_in, 16 * (layer + 1))
            start(v.tensor_tensor(k.fresh[:, 1:z.STEPS], k.b128[:, 1:z.STEPS], k.b128[:, 0:z.STEPS - 1], ALU.not_equal))
            start(v.tensor_scalar(k.fresh[:, 1:z.STEPS], k.fresh[:, 1:z.STEPS], NEG, None, ALU.mult))
            start(v.memset(k.fresh[:, 0:1], NEG))
            start(v.memset(k.peak[:, 0:1], NEG))

            def one_hots(g):
                after(v, s.win_loaded[g.at], loaded(g))
                v.tensor_tensor(k.lo[:, g.two], k.win[:, g.at, :, 1], k.b128[:, ds(g.n * G, G)],
                                ALU.subtract).then_inc(s.lo_done, 1)
                after(v, s.lo_done, g.c + 1)
                after(v, s.eh_done, g.c - R + 1)
                for i in range(G):
                    last = v.tensor_scalar(k.neg[:, g.at, i, :], k.iotab[:], k.lo[:, g.two, i:i + 1], NEG,
                                           ALU.not_equal, ALU.mult)
                last.then_inc(s.neg_done, 1)

            def logits(g):
                after(v, s.relu_done, g.c + 1)
                v.scalar_tensor_tensor(k.tmp[:], z_p(g.two), 0.2, k.tmp[:], ALU.mult, ALU.add).then_inc(s.lr_done, 1)
                after(v, s.lr_done, g.c + 1)
                t = k.tmp[:].rearrange("p (g d) -> p g d", g=G)
                v.tensor_tensor(t, t, rows_of(k.attw[:], G), ALU.mult).then_inc(s.att_done, 1)
                after(v, s.att_done, g.c + 1)
                v.tensor_reduce(k.e[:, g.at], t, AX, ALU.add).then_inc(s.e_done, 1)

            def step_peaks(g):
                after(v, s.ehT_done, g.c + 1)
                v.tensor_reduce(k.ms[:, g.two], mx_p, AX, ALU.max).then_inc(s.ms_done, 1)

            def running_peaks(g):
                link.run(g.c)
                after(v, s.ms_done, g.c + 1)
                before, now = k.peak[:, ds(g.n * G, G)], k.peak[:, ds(g.n * G + 1, G)]
                fresh = k.fresh[:, ds(g.n * G, G)]
                link(v.tensor_tensor_scan(now, fresh, k.ms[:, g.two], k.peak[:, ds(g.n * G, 1)], ALU.add, ALU.max))
                link(v.tensor_tensor(k.dp[:], before, fresh, ALU.add))
                v.tensor_tensor(k.dd[:, g.two, 0], k.dp[:], now, ALU.subtract)
                v.tensor_tensor(k.dd[:, g.two, 1], k.ms[:, g.two], now, ALU.subtract).then_inc(s.dd_done, 1)

            def minus_peaks_of_edges(g):
                after(v, s.me_done, g.c + 1)
                v.tensor_scalar(k.nme[:, g.two], me_p, -1.0, None, ALU.mult).then_inc(s.nme_done, 1)

            def add_sums(g):
                after(v, s.cc_done, g.c + 1)
                after(v, s.s_done, g.c + 1)
                v.tensor_tensor(k.ts[:], sum_p, over_features(k.cc[:, g.two, 1], D + 1), ALU.mult).then_inc(s.ts_done, 1)
                b = [v.value_load(k.blks[DST][0:1, ds(g.n * G + i, 1)], min_val=0, max_val=z.NB - 1) for i in range(G + 1)]
                nodes = [k.acc[:, ds(x, 1), :].rearrange("p a d -> p (a d)") for x in b]
                after(v, s.ts_done, g.c + 1)
                for i in range(G):
                    v.scalar_tensor_tensor(nodes[i + 1], nodes[i], k.cc[:, g.two, 0, i:i + 1], k.ts[:, i, :],
                                           ALU.mult, ALU.add).then_inc(s.sum_link, 1)
                    v.wait_ge(s.sum_link, g.c * G + i + 1)

            if mlp:
                pipelined(v, z, layer, [
                    (0, one_hots), (2, lambda g: mlp_t(v, k, first + g.n)), (late, step_peaks), (late, running_peaks),
                    (late, minus_peaks_of_edges), (3, lambda g: mlp_var(v, k, 1, first + g.n)), (late + 1, add_sums),
                    (3, lambda g: mlp_logit(v, k, k.e[:, g.at], first + g.n)), (1, lambda g: mlp_var(v, k, 0, first + g.n))])
            else:
                pipelined(v, z, layer, [
                    (0, one_hots), (late, step_peaks), (late, running_peaks), (late, minus_peaks_of_edges),
                    (1, logits), (late + 1, add_sums)])


def sum_edges(nc, z, k, layer, table):
    s = k.s

    def loaded(g):
        return 16 * G * g.use

    def sum_p(g):
        return k.bank[g.two][:, 0:G * D].rearrange("p (g d) -> p g d", g=G)

    weighted = (k.eh, k.ph)

    with nc.Block() as block:
        @block.sync
        def _(sp):
            sp.dma_start(k.b128[:], k.b128_dram[SRC].partition_broadcast(P)).then_inc(s.table_in, 16)

            def load_windows(g):
                after(sp, s.w_sum, g.c - R + 1)
                for i in range(G):
                    off = sp.value_load(k.offs[SRC][0:1, ds(g.n * G + i, 1)], min_val=0, max_val=z.E)
                    sp.dma_start(k.win[:, g.at, i, 0:RECS], k.recs_dram[ds(off, P), :]).then_inc(s.win_loaded[g.at], 16)
            pipelined(sp, z, layer, [(0, load_windows)])

        @block.gpsimd
        def _(pool):
            def gather(g):
                after(pool, s.w_sum, g.c - R + 1, alone=True)
                after(pool, s.win_loaded[g.at], loaded(g), alone=True)
                for i in range(G):
                    pool.indirect_dma_start(
                        k.rows[:, g.at, i, 0:D], None, table,
                        bass.IndirectOffsetOnAxis(ap=k.win[:, g.at, i, 0:1].bitcast(U32), axis=0)
                    ).then_inc(s.gathered[g.at], 16)
            pipelined(pool, z, layer, [(0, gather)])

        @block.tensor
        def _(pe):
            def sums(g):
                after(pe, s.w_hot, g.c + 1, alone=True)
                after(pe, s.w_acc, g.c - 1, alone=True)
                after(pe, s.gathered[g.at], loaded(g), alone=True)
                for i in range(G):
                    last = pe.matmul(sum_p(g)[:, i, :], weighted[0][:, g.two, i, :], k.rows[:, g.at, i, 0:D],
                                     start=True, stop=True)
                last.then_inc(s.w_sum, 1)
            pipelined(pe, z, layer, [(1, sums)])

        @block.vector
        def _(v):
            v.wait_ge(s.table_in, 16 * (layer + 1))

            def weigh(g):
                after(v, s.win_loaded[g.at], loaded(g))
                v.tensor_tensor(k.lo[:, g.two], k.win[:, g.at, :, 1], k.b128[:, ds(g.n * G, G)],
                                ALU.subtract).then_inc(s.w_lo, 1)
                after(v, s.w_lo, g.c + 1)
                after(v, s.w_sum, g.c - 1)
                for i in range(G):
                    last = v.tensor_scalar(weighted[0][:, g.two, i, :], k.iota[:], k.lo[:, g.two, i:i + 1],
                                           k.win[:, g.at, i, 2:3], ALU.is_equal, ALU.mult)
                last.then_inc(s.w_hot, 1)

            def add_sums(g):
                after(v, s.w_sum, g.c + 1)
                for i in range(G):
                    b = v.value_load(k.blks[SRC][0:1, ds(g.n * G + i + 1, 1)], min_val=0, max_val=z.NB - 1)
                    node = k.acc[:, ds(b, 1), 0:D].rearrange("p a d -> p (a d)")
                    v.tensor_tensor(node, node, sum_p(g)[:, i, :], ALU.add).then_inc(s.w_acc1, 1)
                    v.wait_ge(s.w_acc1, g.c * G + i + 1)
                v.memset(k.pidx2[:], 0.0).then_inc(s.w_acc, 1)
            pipelined(v, z, layer, [(0, weigh), (2, add_sums)])


def mlp_h0(a, k, z, two, m):
    s = k.s
    a.activation(k.h0[:, two], z, ACT.Relu).then_inc(s.h0_done, 1)


def mlp_turn0(pe, k, two, m):
    s = k.s
    after(pe, s.h0_done, m + 1, alone=True)
    after(pe, s.hT_done[0], m, alone=True)
    for g in range(G):
        last = pe.transpose(k.bank[4][0:D, g * P:(g + 1) * P], k.h0[:, two, g, :], k.ident[:])
    last.then_inc(s.hT_p_done[0], 1)


def mlp_copy0(a, k, m):
    s = k.s
    after(a, s.hT_p_done[0], m + 1)
    a.activation(k.hT[:, 0], k.bank[4][0:D, :], ACT.Copy).then_inc(s.hT_done[0], 1)


def mlp_first(pe, k, m):
    s = k.s
    after(pe, s.hT_done[0], m + 1, alone=True)
    after(pe, s.t_done, m, alone=True)
    for g in range(G):
        last = pe.matmul(k.bank[5][:, g * P:(g + 1) * P], k.hT[:, 0, g * P:(g + 1) * P], k.w1c[:], start=True, stop=True)
    last.then_inc(s.first_done, 1)


def mlp_square0(a, k, m):
    s = k.s
    after(a, s.first_done, m + 1)
    after(a, s.var_done[0], m)
    hc = k.bank[5].rearrange("p (g d) -> p g d", g=G)[:, :, D:2 * D]
    a.activation(k.sq[:, 0], hc, ACT.Square).then_inc(s.sq_done[0], 1)


def mlp_var(v, k, norm, m):
    s = k.s
    after(v, s.sq_done[norm], m + 1)
    v.tensor_reduce(k.ss[:, norm], k.sq[:, norm], AX, ALU.add).then_inc(s.ss_done[norm], 1)
    after(v, s.ss_done[norm], m + 1)
    v.tensor_scalar(k.var[:, norm], k.ss[:, norm], 1.0 / D, EPS_MLP, ALU.mult, ALU.add).then_inc(s.var_done[norm], 1)


def mlp_rstd_guess(a, k, norm, m):
    s = k.s
    after(a, s.var_done[norm], m + 1)
    a.activation(k.lnv[:, norm], k.var[:, norm], ACT.Ln).then_inc(s.ln_done[norm], 1)
    after(a, s.ln_done[norm], m + 1)
    a.activation(k.guess[:, norm], k.lnv[:, norm], ACT.Exp, scale=-0.5).then_inc(s.guess_done[norm], 1)


def newton(v, k, norm, m):
    s = k.s
    link = Links(v, s.newton_link[norm], 3)
    link.run(m)
    after(v, s.guess_done[norm], m + 1)
    r, out = k.guess[:, norm], k.rstd[:, norm]
    link(v.tensor_tensor(out, r, r, ALU.mult))
    link(v.scalar_tensor_tensor(out, out, -0.5, k.var[:, norm], ALU.mult, ALU.mult))
    link(v.scalar_tensor_tensor(out, out, 1.5, r, ALU.add, ALU.mult))


def mlp_t(v, k, m):
    s = k.s
    newton(v, k, 0, m)
    after(v, s.first_done, m + 1)
    after(v, s.h1_done, m)
    for g in range(G):
        last = v.scalar_tensor_tensor(k.t1[:, g, :], k.bank[5][:, g * P:g * P + D], k.rstd[:, 0, g:g + 1], k.w1b[:],
                                      ALU.mult, ALU.add)
    last.then_inc(s.t_done, 1)


def mlp_h1(a, k, m):
    s = k.s
    after(a, s.t_done, m + 1)
    after(a, s.hT_p_done[1], m)
    a.activation(k.h1[:], k.t1[:], ACT.Relu).then_inc(s.h1_done, 1)


def mlp_turn1(pe, k, m):
    s = k.s
    after(pe, s.h1_done, m + 1, alone=True)
    after(pe, s.hT_done[1], m, alone=True)
    for g in range(G):
        last = pe.transpose(k.bank[6][0:D, g * P:(g + 1) * P], k.h1[:, g, :], k.ident[:])
    last.then_inc(s.hT_p_done[1], 1)


def mlp_copy1(a, k, m):
    s = k.s
    after(a, s.hT_p_done[1], m + 1)
    after(a, s.second_done, m)
    a.activation(k.hT[:, 1], k.bank[6][0:D, :], ACT.Copy).then_inc(s.hT_done[1], 1)


def mlp_second(pe, k, m):
    s = k.s
    after(pe, s.hT_done[1], m + 1, alone=True)
    after(pe, s.logit_done, m, alone=True)
    for g in range(G):
        last = pe.matmul(k.bank[7][:, g * (D + 1):(g + 1) * (D + 1)], k.hT[:, 1, g * P:(g + 1) * P], k.w2c[:],
                         start=True, stop=True)
    last.then_inc(s.second_done, 1)


def second_p(k):
    return k.bank[7][:, 0:G * (D + 1)].rearrange("p (g d) -> p g d", g=G)


def mlp_square1(a, k, m):
    s = k.s
    after(a, s.second_done, m + 1)
    after(a, s.var_done[1], m)
    a.activation(k.sq[:, 1], second_p(k)[:, :, 0:D], ACT.Square).then_inc(s.sq_done[1], 1)


def mlp_logit(v, k, out, m):
    s = k.s
    newton(v, k, 1, m)
    after(v, s.second_done, m + 1)
    v.tensor_tensor(k.dot[:], second_p(k)[:, :, D], k.rstd[:, 1], ALU.mult).then_inc(s.dot_done, 1)
    after(v, s.dot_done, m + 1)
    v.tensor_scalar(out, k.dot[:], k.wfb[:], 0.0, ALU.add, ALU.max).then_inc(s.logit_done, 1)


def close_layer(nc, z, k, layer, table):
    s, n = k.s, layer
    with nc.Block() as block:
        @block.vector
        def _(v):
            link = Links(v, s.close_link[layer], {0: 10, 1: 1, 2: 10}[layer] + 6)
            link.run(0)
            if layer != 1:
                v.memset(k.top[:], NEG).then_inc(s.top_set, 1)
                v.wait_ge(s.top_set, layer // 2 + 1)
                with v.Fori(0, z.NB) as b:
                    at = v.value_load(k.lasts[0:1, ds(b, 1)], min_val=0, max_val=z.STEPS)
                    v.tensor_scalar(k.top[:, ds(b, 1)], k.peak[:, ds(at, 1)], 0.0, None, ALU.add).then_inc(s.top_done, 1)
                v.wait_ge(s.top_done, z.NB * (layer // 2 + 1))
                link(v.tensor_tensor(k.nstat[:, 2, :], k.top[:], k.eself[:], ALU.max))
                v.tensor_tensor(k.nstat[:, 0, :], k.top[:], k.nstat[:, 2, :], ALU.subtract)
                v.tensor_tensor(k.nstat[:, 1, :], k.eself[:], k.nstat[:, 2, :], ALU.subtract).then_inc(s.self_diff, 1)
                v.wait_ge(s.self_exp, layer // 2 + 1)
                c0, c1 = k.nstat[:, 0, :], k.nstat[:, 1, :]
                tmp, sums = k.tab[:, :, 0:D], k.acc[:, :, 0:D]
                link(v.tensor_tensor(k.acc[:], k.acc[:], over_features(c0, D + 1), ALU.mult))
                link(v.tensor_tensor(k.acc[:, :, D], k.acc[:, :, D], c1, ALU.add))
                v.wait_ge(s.own_in, 16 * (layer // 2 + 1))
                link(v.tensor_tensor(tmp, k.hbuf, over_features(c1), ALU.mult))
                link(v.tensor_tensor(sums, sums, tmp, ALU.add))
                link(v.reciprocal(k.nstat[:, 0, :], k.acc[:, :, D]))
                link(v.tensor_tensor(tmp, sums, over_features(k.nstat[:, 0, :]), ALU.mult))
            if layer == 0:
                link(v.tensor_tensor(k.x[:], k.x[:], tmp, ALU.add))
                link(v.tensor_tensor(k.x[:], k.x[:], rows_of(k.bias0[:], z.NBK), ALU.add))
            if layer == 1:
                link(v.tensor_tensor(k.x[:], k.x[:], k.acc[:, :, 0:D], ALU.add))
            if layer == 2:
                link(v.scalar_tensor_tensor(tmp, tmp, 0.01, tmp, ALU.mult, ALU.max))
                link(v.tensor_tensor(k.x[:], k.x[:], tmp, ALU.add))
            norm_vector(v, k, z, link, s, n)
            v.memset(k.acc[:], 0.0).then_inc(s.norm_done, 1)

        @block.scalar
        def _(a):
            if layer != 1:
                a.wait_ge(s.self_diff, layer // 2 + 1)
                a.activation(k.nstat[:, 0:2, :], k.nstat[:, 0:2, :], ACT.Exp).then_inc(s.self_exp, 1)
            norm_scalar(a, k, s, n)

        @block.sync
        def _(sp):
            if layer != 1:
                own = k.xl_dram if layer == 0 else k.q_dram
                sp.dma_start(k.hbuf, own.rearrange("(b p) d -> p b d", p=P)).then_inc(s.own_in, 16)
            if table is not None:
                sp.wait_ge(s.norm_done, n + 1)
                sp.dma_start(table.rearrange("(b p) d -> p b d", p=P), k.hbuf).then_inc(s.h_out, 16)
                sp.wait_ge(s.h_out, 16 if layer == 0 else 32)


def mlp_nodes(nc, z, k):
    s, groups, bank = k.s, z.NBK // G, k.bank
    dst = k.a2_dram.rearrange("(b p) d -> p b d", p=P)
    own = k.q_dram.rearrange("(b p) d -> p b d", p=P)
    a_st, b_st, zs = k.rows[:, 0], k.rows[:, 1], k.rows[:, 2]

    def grouped(b):
        return bank[b].rearrange("p (g d) -> p g d", g=G)

    with nc.Block() as block:
        @block.scalar
        def _(a):
            def group(i):
                a.activation(k.hs[:], k.hbuf[:, ds(i * G, G), :], ACT.Copy).then_inc(s.hs_done, 1)
                a.wait_ge(s.hsT_done, i + 1)
                a.activation(k.hTn[:], bank[3][0:D, :], ACT.Copy).then_inc(s.hTn_done, 1)
                a.wait_ge(s.ab_done, i + 1)
                after(a, s.a_out, 16 * i)
                a.activation(a_st, grouped(0), ACT.Copy).then_inc(s.a_done, 1)
                after(a, s.zs_done, i + 1, alone=True)
                a.activation(k.tab[:, ds(i * G, G), :], b_st, ACT.Copy).then_inc(s.b_kept, 1)
                mlp_h0(a, k, zs[:, :, D:2 * D], 0, i)
                mlp_copy0(a, k, i)
                mlp_square0(a, k, i)
                mlp_rstd_guess(a, k, 0, i)
                mlp_h1(a, k, i)
                mlp_copy1(a, k, i)
                mlp_square1(a, k, i)
                mlp_rstd_guess(a, k, 1, i)
            counted(a, groups, group)

        @block.sync
        def _(sp):
            def group(i):
                sp.wait_ge(s.a_done, i + 1)
                sp.dma_start(dst[:, ds(i * G, G), :], a_st).then_inc(s.a_out, 16)
                sp.wait_ge(s.zs_done, i + 1)
                sp.dma_start(own[:, ds(i * G, G), :], zs[:, :, 0:D]).then_inc(s.q_out, 16)
            counted(sp, groups, group)
            sp.wait_ge(s.q_out, 16 * groups)
            sp.wait_ge(s.a_out, 16 * groups)

        @block.tensor
        def _(pe):
            def group(i):
                after(pe, s.hs_done, i + 1, alone=True)
                for g in range(G):
                    last = pe.transpose(bank[3][0:D, g * P:(g + 1) * P], k.hs[:, g, :], k.ident[:])
                last.then_inc(s.hsT_done, 1)
                after(pe, s.hTn_done, i + 1, alone=True)
                for b, w in ((0, k.wqa), (1, k.wqb)):
                    for g in range(G):
                        last = pe.matmul(bank[b][:, g * P:(g + 1) * P], k.hTn[:, g * P:(g + 1) * P], w[:],
                                         start=True, stop=True)
                last.then_inc(s.ab_done, 1)
                mlp_turn0(pe, k, 0, i)
                mlp_first(pe, k, i)
                mlp_turn1(pe, k, i)
                mlp_second(pe, k, i)
            counted(pe, groups, group)

        @block.vector
        def _(v):
            def group(i):
                v.wait_ge(s.a_done, i + 1)
                after(v, s.b_kept, i)
                v.tensor_tensor(b_st, grouped(1), rows_of(k.bq0[:], G), ALU.add).then_inc(s.b_done, 1)
                v.wait_ge(s.b_done, i + 1)
                after(v, s.q_out, 16 * i)
                v.tensor_tensor(zs, b_st, a_st, ALU.add).then_inc(s.zs_done, 1)
                mlp_var(v, k, 0, i)
                mlp_t(v, k, i)
                mlp_var(v, k, 1, i)
                mlp_logit(v, k, k.eself[:, ds(i * G, G)], i)
            counted(v, groups, group)


def last_nodes(nc, io, z, k):
    s, groups = k.s, z.NBK // G
    full = z.N // P
    with nc.Block() as block:
        @block.scalar
        def _(a):
            a.wait_ge(s.own_in, 48)
            def group(i):
                for part, src in ((0, k.hbuf), (1, k.acc)):
                    n = 2 * i + part
                    a.activation(k.hs[:], src[:, ds(i * G, G), 0:D], ACT.Copy).then_inc(s.l_hs, 1)
                    a.wait_ge(s.l_hsT, n + 1)
                    a.activation(k.hTn[:], k.bank[6][0:D, :], ACT.Copy).then_inc(s.l_hT, 1)
                    a.wait_ge(s.l_y, n + 1)
            counted(a, groups, group)

        @block.tensor
        def _(pe):
            def group(i):
                for part in range(2):
                    n = 2 * i + part
                    after(pe, s.l_hs, n + 1, alone=True)
                    for g in range(G):
                        last = pe.transpose(k.bank[6][0:D, g * P:(g + 1) * P], k.hs[:, g, :], k.ident[:])
                    last.then_inc(s.l_hsT, 1)
                    after(pe, s.l_hT, n + 1, alone=True)
                    after(pe, s.l_x, i, alone=True)
                    for g in range(G):
                        last = pe.matmul(k.bank[part][:, g * D:(g + 1) * D], k.hTn[:, g * P:(g + 1) * P], k.w3[:, part, :],
                                         start=True, stop=True)
                    last.then_inc(s.l_y, 1)
            counted(pe, groups, group)

        @block.vector
        def _(v):
            link = Links(v, s.l_link, 2)
            def group(i):
                link.run(i)
                x = k.x[:, ds(i * G, G), :]
                y = [k.bank[b][:, 0:G * D].rearrange("p (g d) -> p g d", g=G) for b in range(2)]
                v.wait_ge(s.l_y, 2 * i + 2)
                link(v.tensor_tensor(x, x, y[0], ALU.add))
                link(v.tensor_tensor(x, x, y[1], ALU.add))
                v.tensor_tensor(x, x, rows_of(k.b3[:], G), ALU.add).then_inc(s.l_x, 1)
            counted(v, groups, group)

        @block.sync
        def _(sp):
            sp.dma_start(k.hbuf, k.h3_dram.rearrange("(b p) d -> p b d", p=P)).then_inc(s.own_in, 16)
            sp.wait_ge(s.l_x, groups)
            sp.dma_start(io.out[0:full * P, :].rearrange("(b p) d -> p b d", p=P), k.x[:, 0:full, :]).then_inc(s.out_done, 16)
            rest = z.N - full * P
            if rest:
                sp.dma_start(io.out[full * P:z.N, :], k.x[0:rest, full, :]).then_inc(s.out_done, 16)
            sp.wait_ge(s.out_done, 32 if rest else 16)


def build(nc, io, n, e):
    z = Sizes(n, e)
    NBK, NBUCK, C = z.NBK, z.NBUCK, z.C
    with ExitStack() as top:
        k = Place()
        names = []

        def sems(**more):
            out = named()
            return out

        def sem(name):
            return top.enter_context(nc.semaphore(name))

        def sb(name, shape, dt=F32, ctx=top):
            return ctx.enter_context(nc.sbuf_tensor(name, shape, dt))

        def dram(name, shape, dt=F32):
            return nc.dram_tensor(name, shape, dt, kind="Internal").ap()

        k.xl_dram = dram("xl_dram", (NBK * P, D))
        k.h1_dram = dram("h1_dram", (NBK * P, D))
        k.q_dram = dram("q_dram", (NBK * P, D))
        k.h3_dram = dram("h3_dram", (NBK * P, D))
        k.a2_dram = dram("a2_dram", (NBK * P, 2 * D))
        k.recd_dram = dram("recd_dram", (z.EP, RECD))
        k.recs_dram = dram("recs_dram", (z.EP, RECS))
        k.off_dram = [dram(f"off{o}_dram", (P * z.SJ,), I32) for o in "ds"]
        k.blk_dram = [dram(f"blk{o}_dram", (P * z.SJ,), I32) for o in "ds"]
        k.b128_dram = [dram(f"b128{o}_dram", (P * z.SJ,), BF16) for o in "ds"]

        k.x = sb("x", [P, NBK, D])
        k.tab = sb("tab", [P, NBK, 2 * D])
        k.acc = sb("acc", [P, NBK, D + 1])
        k.top = sb("top", [P, NBK])
        k.eself = sb("eself", [P, NBK])
        half = R * G * P // 2
        shared = sb("shared", [P, max(NBK * D, 2 * half)])
        k.hbuf = shared[:, 0:NBK * D].rearrange("p (b d) -> p b d", d=D)
        k.neg = shared[:, 0:half].bitcast(BF16).rearrange("p (r g n) -> p r g n", r=R, g=G)
        k.hotT = shared[:, half:2 * half].rearrange("p (r g n) -> p r g n", r=4, g=G)
        k.nstat = sb("nstat", [P, 3, NBK])
        k.b128 = sb("b128", [P, P * z.SJ], BF16)
        k.fresh = sb("fresh", [P, z.STEPS], BF16)
        k.peak = sb("peak", [P, z.STEPS + 1])
        k.lasts = sb("lasts", [1, NBUCK], I32)
        k.steps = sb("steps", [4, P * z.SJ + 1], I32)
        k.offs = [k.steps[2 * o:2 * o + 1, 0:P * z.SJ] for o in (DST, SRC)]
        k.blks = [k.steps[2 * o + 1:2 * o + 2, :] for o in (DST, SRC)]
        k.ident = sb("ident", [P, P])
        k.identb = sb("identb", [P, P], BF16)
        k.iota = sb("iota", [P, P])
        k.pidx = sb("pidx", [P, 1])
        k.pidx2 = sb("pidx2", [P, 1])
        k.attw = sb("attw", [P, D])
        k.bias0 = sb("bias0", [P, D])
        k.wlr = sb("wlr", [D, 2 * D])
        k.wqa = sb("wqa", [D, 2 * D])
        k.wqb = sb("wqb", [D, 2 * D])
        k.wqe4 = sb("wqe4", [G * RECD, G, 2 * D])
        k.iotab = sb("iotab", [P, P], BF16)
        k.bq0 = sb("bq0", [P, 2 * D])
        k.w1c = sb("w1c", [D, 2 * D])
        k.w2c = sb("w2c", [D, D + 1])
        k.w1b = sb("w1b", [P, D])
        k.wfb = sb("wfb", [P, 1])
        k.w3 = sb("w3", [D, 2, D])
        k.b3 = sb("b3", [P, D])
        k.hs = sb("hs", [P, G, D])
        k.hTn = sb("hTn", [D, G * P])
        k.bank = [top.enter_context(nc.psum_tensor(f"bank{i}", [P, 512], F32)) for i in range(8)]

        with ExitStack() as early:
            k.w1 = sb("w1", [D, D], ctx=early)
            k.w1g = sb("w1g", [D, D], ctx=early)
            k.centre = sb("centre", [D, D], ctx=early)
            k.g1 = sb("g1", [D, 1], ctx=early)
            k.wfcol = sb("wfcol", [D, 1], ctx=early)
            k.g0 = sb("g0", [D, 1], ctx=early)
            k.beta0 = sb("beta0", [D, 1], ctx=early)
            k.beta0w = sb("beta0w", [D, P], ctx=early)
            k.beta1 = sb("beta1", [P, D], ctx=early)
            k.wf = sb("wf", [P, D], ctx=early)
            k.b3n = sb("b3n", [P, D], ctx=early)
            k.before = sb("before", [P, P], ctx=early)
            k.ones = sb("ones", [P, P], ctx=early)
            k.csem = named(**{m: sem(m) for m in ("consts", "iota", "clink", "weights_scaled", "products", "wqe_clear", "wqe_in")})
            load_constants(nc, io, z, k)

            k.order = [named(
                key_int=sb(f"key_int{o}", [P, C], I32, early),
                pos_int=sb(f"pos_int{o}", [P, C], I32, early)) for o in "ds"]
            k.w = k.peak[:, 0:C]
            k.hi = sb("hi", [P, C], BF16, early)
            k.same = sb("same", [P, C], U8, early)
            k.run = sb("run", [P, C // CH], I32, early)
            (k.cnt, k.cnt2, k.tot, k.goff, k.base, k.nst, k.send, k.lead, k.jump, k.ended, k.ended2) = [
                sb(t, [P, NBUCK], ctx=early)
                for t in ("cnt", "cnt2", "tot", "goff", "base", "nst", "send", "lead", "jump", "ended", "ended2")]
            k.nst_int = sb("nst_int", [P, NBUCK], I32, early)
            k.step_no, k.blk, k.off, k.off2 = [
                sb(t, [P, z.SJ], ctx=early) for t in ("step_no", "blk", "off", "off2")]
            k.blk128 = sb("blk128", [P, z.SJ], BF16, early)
            k.off_int = sb("off_int", [P, z.SJ], I32, early)
            k.blk_int = sb("blk_int", [P, z.SJ], I32, early)
            k.attr_in = sb("attr_in", [P, 2, SC, EA], ctx=early)
            k.rec = sb("rec", [P, 2, SC, RECD], ctx=early)
            k.pos_st = sb("pos_st", [P, 2, SC], I32, early)
            k.s1 = named(
                rank_link=[sem("rank_link_dst"), sem("rank_link_src")],
                ranked=[sem("ranked_dst"), sem("ranked_src")], tables_out=[sem("tables_out_dst"), sem("tables_out_src")],
                attr_loaded=[sem("attr_loaded0"), sem("attr_loaded1")], scattered=[sem("scattered0"), sem("scattered1")],
                **{m: sem("first_" + m) for m in (
                    "counted", "count_sums", "off_sum", "tables_done", "tables_in", "x_loaded", "dst_loaded",
                    "src_loaded", "w_loaded", "xl_done", "xl_out", "staged", "norm_done", "hs_done", "hsT_done", "hT_done",
                    "proj_done", "nlink", "nvar_done", "nsqrt_done", "step_no_done")})
            sort_and_project(nc, io, z, k)

        k.win = sb("win", [P, R, G, RECD])
        k.rows = sb("rows", [P, R, G, 2 * D])
        k.val = sb("val", [P, R, G, D + 1])
        k.eh = sb("eh", [P, 2, G, P])
        k.ph = sb("ph", [P, 2, G, P])
        k.e = sb("e", [P, R, G])
        k.lo = sb("lo", [P, 2, G])
        k.tmp = sb("tmp", [P, G * D])
        k.ms = sb("ms", [P, 2, G])
        k.nme = sb("nme", [P, 2, G])
        k.dp = sb("dp", [P, G])
        k.dd = sb("dd", [P, 2, 2, G])
        k.cc = sb("cc", [P, 2, 2, G])
        k.ts = sb("ts", [P, G, D + 1])
        k.atT = sb("atT", [G * RECD, P])
        k.h0 = sb("h0", [P, 2, G, D])
        k.hT = sb("hT", [D, 2, G * P])
        k.sq = sb("sq", [P, 2, G, D])
        k.t1 = sb("t1", [P, G, D])
        k.h1 = sb("h1", [P, G, D])
        k.dot = sb("dot", [P, G])
        k.ss, k.var, k.lnv, k.guess, k.rstd = [sb(t, [P, 2, G]) for t in ("ss", "var", "lnv", "guess", "rstd")]
        k.s = named(
            win_loaded=[sem(f"win_loaded{r}") for r in range(R)], gathered=[sem(f"gathered{r}") for r in range(R)],
            close_link=[sem(f"close_link{i}") for i in range(3)],
            **{m: [sem(m + "0"), sem(m + "1")] for m in (
                "hT_done", "hT_p_done", "sq_done", "ss_done", "var_done", "ln_done", "guess_done", "newton_link")},
            **{m: sem(m) for m in (
                "table_in", "s_done", "eh_done", "ehT_done", "negT_done", "hotT_done", "z_done", "e_done", "relu_done",
                "dd_done", "cc_done", "nme_done", "ph_done", "ts_done", "neg_done", "me_done", "ms_done", "ones_set",
                "start_link", "peak_link", "lo_done", "lr_done", "att_done", "sum_link",
                "w_sum", "w_hot", "w_acc", "w_acc1", "w_lo",
                "h0_done", "first_done", "t_done", "h1_done", "second_done", "dot_done", "logit_done",
                "own_in", "q_out", "top_set", "top_done", "self_diff", "self_exp", "nvar_done", "nsqrt_done", "norm_done", "h_out",
                "hs_done", "hsT_done", "hTn_done", "ab_done", "a_out", "a_done", "b_done", "zs_done", "b_kept",
                "l_hs", "l_hsT", "l_hT", "l_y", "l_x", "l_link", "out_done")})

        softmax_edges(nc, z, k, 0)
        close_layer(nc, z, k, 0, k.h1_dram)
        sum_edges(nc, z, k, 1, k.h1_dram)
        close_layer(nc, z, k, 1, None)
        mlp_nodes(nc, z, k)
        softmax_edges(nc, z, k, 2)
        close_layer(nc, z, k, 2, k.h3_dram)
        sum_edges(nc, z, k, 3, k.h3_dram)
        last_nodes(nc, io, z, k)


def kernel(**inputs):
    import numpy as _np
    import concourse.bacc as _bacc
    from concourse.bass_utils import run_bass_kernel_spmd as _run

    a = {name: _np.asarray(value) for name, value in inputs.items()}
    n, e = a["x"].shape[0], a["src"].shape[0]
    z = Sizes(n, e)
    nodes = (0, z.NBK * P - n)
    edges = (0, z.EP - e)
    laid = {
        "x": _np.pad(a["x"], (nodes, (0, 0))),
        "src": _np.pad(a["src"], edges, constant_values=z.PADKEY),
        "dst": _np.pad(a["dst"], edges, constant_values=z.PADKEY),
        "w": _np.pad(a["edge_weight"], edges),
        "attr": _np.pad(a["edge_attr_16"], (edges, (0, 0))),
        "W_l": a["L0_gnn_W_l"], "W_r": a["L0_gnn_W_r"], "att": a["L0_gnn_att"], "bias": a["L0_gnn_bias"],
        "Wq": a["L2_gnn_Wq"], "bq": a["L2_gnn_bq"], "W0": a["L2_gnn_W0"], "b0": a["L2_gnn_b0"],
        "g0": a["L2_gnn_g0"].reshape(D, 1), "beta0": a["L2_gnn_beta0"].reshape(D, 1),
        "W1": a["L2_gnn_W1"], "b1": a["L2_gnn_b1"], "g1": a["L2_gnn_g1"], "beta1": a["L2_gnn_beta1"],
        "Wf": a["L2_gnn_Wf"].reshape(D), "bf": a["L2_gnn_bf"],
        "W_selfT": a["L3_gnn_W_self"].T, "W_neighT": a["L3_gnn_W_neigh"].T,
        "b_self": a["L3_gnn_b_self"], "b_neigh": a["L3_gnn_b_neigh"],
    }
    nc = _bacc.Bacc("TRN2", target_bir_lowering=False, num_devices=1)
    arrays, tensors = {}, {}
    for name, value in laid.items():
        value = _np.ascontiguousarray(value)
        arrays[f"in_{name}"] = value
        t = nc.dram_tensor(f"in_{name}", value.shape, mybir.dt.from_np(value.dtype), kind="ExternalInput").ap()
        tensors[name] = t
    tensors["out"] = nc.dram_tensor("out", (n, D), F32, kind="ExternalOutput").ap()
    io = named(**tensors)
    build(nc, io, n, e)
    r = _run(nc, [arrays], core_ids=[0])
    return r.results[0]["out"]
```

```python
from contextlib import ExitStack
from collections import namedtuple

import numpy as np
import concourse.bass as bass
from concourse import mybir

P = 128
D = 64
F32 = mybir.dt.float32
BF16 = mybir.dt.bfloat16
I32 = mybir.dt.int32
U32 = mybir.dt.uint32
U8 = mybir.dt.uint8
ALU = mybir.AluOpType
ACT = mybir.ActivationFunctionType
AX = mybir.AxisListType.X
ds = bass.ds

EA = 16
G = 4
R = 8
CH = 3
SC = 3
RECD = 2 + EA
RECS = 3
NEG = -(2.0 ** 100)
EPS_NODE = 1e-5
EPS_MLP = 1e-6
DST, SRC = 0, 1


class Sizes:
    def __init__(self, n, e):
        self.N, self.E = n, e
        self.NB = -(-n // P)
        self.NBUCK = self.NB + 1
        self.NBK = -(-(self.NB + 1) // G) * G
        self.PADKEY = self.NB * P
        self.C = -(-(e + P) // (P * CH * SC * 2)) * (CH * SC * 2)
        self.EP = self.C * P
        self.STEPS = -(-(e // P + self.NB) // (G * R)) * (G * R)
        self.NG = self.STEPS // G
        self.NIT = self.NG // R
        self.SJ = -(-self.STEPS // P)
        assert self.NIT >= 4 and self.C >= 4 * CH * SC and self.STEPS >= self.C


class Place:
    pass


def named(**values):
    return namedtuple("Named", values.keys())(*values.values())


def after(eng, sem, value, alone=False):
    if not (isinstance(value, int) and value <= 0):
        eng.wait_ge(sem, value)
        if alone:
            eng.nop(nofuse=True)


def table_values(nc, eng, table, first, count, most):
    return nc.values_load_multi_w_load_instructions(table[0:1, ds(first, count)], engines=[eng], min_val=0, max_val=most)[1]


class Links:

    def __init__(self, eng, sem, per):
        self.eng, self.sem, self.per = eng, sem, per

    def run(self, n):
        self.start, self.n = n * self.per, 0

    def __call__(self, ins):
        self.n += 1
        ins.then_inc(self.sem, 1)
        self.eng.wait_ge(self.sem, self.start + self.n)

    def end(self):
        assert self.n == self.per, self.n


def over_nodes(ap):
    return ap.unsqueeze(2).broadcast_to([P, ap.shape[1], P])


def over_features(ap, d=D):
    return ap.unsqueeze(2).broadcast_to([P, ap.shape[1], d])


def rows_of(ap, m):
    return ap.unsqueeze(1).broadcast_to([P, m, ap.shape[1]])


class Group:

    def __init__(self, n, c, at, use):
        self.n, self.c, self.at, self.two, self.use = n, c, at, at % 2, use


def pipelined(eng, z, layer, stages):
    lag_max = max(lag for lags, *_ in stages for lag in lags)
    lead = 1 + -(-lag_max // R)

    def turn(it, j):
        for lags, what, *more in stages:
            groups = []
            for lag in lags:
                n = R * it + (j - lag)
                there = not isinstance(n, int) or 0 <= n < z.NG + sum(more)
                groups.append(Group(n, (layer // 2) * z.NG + n, (j - lag) % R,
                                    layer * z.NIT + it + (j - lag) // R + 1) if there else None)
            if any(groups):
                what(*groups)

    for t in range(lead * R):
        turn(t // R, t % R)
    with eng.Fori(lead, z.NIT) as it:
        for j in range(R):
            turn(it, j)
    for t in range(z.NG, z.NG + lag_max):
        turn(t // R, t % R)


def counted(eng, n, body):
    body(0)
    with eng.Fori(1, n) as i:
        body(i)


def twice_counted(eng, n, body):
    body(0)
    body(1)
    with eng.Fori(2, n) as i:
        body(i)


def load_constants(nc, io, z, k):
    loads = [
        (k.attw[:], io.att.partition_broadcast(P)), (k.bias0[:], io.bias.partition_broadcast(P)),
        (k.wlr[:, 0:D], io.W_l), (k.wlr[:, D:2 * D], io.W_r),
        (k.wqa[:, 0:D], io.W0[0:D, :]), (k.wqa[:, D:2 * D], io.Wq[0:D, :]),
        (k.wqb[:, 0:D], io.W0[D:2 * D, :]), (k.wqb[:, D:2 * D], io.Wq[D:2 * D, :]),
        (k.bq0[:, 0:D], io.b0.partition_broadcast(P)), (k.bq0[:, D:2 * D], io.bq.partition_broadcast(P)),
        (k.w1[:], io.W1), (k.g0[:], io.g0), (k.beta0[:], io.beta0),
        (k.w1b[:], io.b1.partition_broadcast(P)), (k.g1[:], io.g1.rearrange("(p a) -> p a", a=1)),
        (k.wfcol[:], io.Wf.rearrange("(p a) -> p a", a=1)),
        (k.beta1[:], io.beta1.partition_broadcast(P)), (k.wf[:], io.Wf.partition_broadcast(P)),
        (k.wfb[:], io.bf.partition_broadcast(P)),
        (k.w3[:, 0, :], io.W_selfT), (k.w3[:, 1, :], io.W_neighT),
        (k.b3[:], io.b_self.partition_broadcast(P)), (k.b3n[:], io.b_neigh.partition_broadcast(P)),
    ]
    s = k.csem
    with nc.Block() as block:
        @block.sync
        def _(sp):
            for out, src in loads:
                sp.dma_start(out, src).then_inc(s.consts, 16)
            sp.wait_ge(s.wqe_clear, 1)
            for g in range(G):
                at = slice(g * RECD + 2, (g + 1) * RECD)
                sp.dma_start(k.wqe4[at, g, D:2 * D], io.Wq[2 * D:2 * D + EA, :]).then_inc(s.wqe_in, 16)
                sp.dma_start(k.wqe4[at, g, 0:D], io.W0[2 * D:2 * D + EA, :]).then_inc(s.wqe_in, 16)
            sp.wait_ge(s.wqe_in, 32 * G)

        @block.gpsimd
        def _(pool):
            pool.iota(k.iota[:], [[1, P]], base=0, channel_multiplier=0,
                      allow_small_or_imprecise_dtypes=True).then_inc(s.iota, 1)
            pool.iota(k.pidx[:], [[0, 1]], base=0, channel_multiplier=1,
                      allow_small_or_imprecise_dtypes=True).then_inc(s.iota, 1)

        @block.vector
        def _(v):
            link = Links(v, s.clink, 14)
            link.run(0)
            v.memset(k.wqe4[:], 0.0).then_inc(s.wqe_clear, 1)
            v.wait_ge(s.iota, 2)
            v.tensor_copy(k.iotab[:], k.iota[:])
            v.tensor_scalar(k.identb[:], k.iota[:], k.pidx[:], None, ALU.is_equal)
            v.memset(k.steps[:, 0:1], 0)
            link(v.tensor_scalar(k.ident[:], k.iota[:], k.pidx[:], None, ALU.is_equal))
            link(v.tensor_scalar(k.centre[:], k.ident[0:D, 0:D].unsqueeze(1).broadcast_to([D, 2, D]), -1.0 / D, None,
                                 ALU.add))
            link(v.tensor_scalar(k.before[:], k.iota[:], k.pidx[:], None, ALU.is_gt))
            link(v.memset(k.ones[:], 1.0))
            v.wait_ge(s.consts, 16 * len(loads))
            link(v.tensor_copy(k.beta0w[:], k.beta0[:].broadcast_to([D, P])))
            link(v.tensor_scalar(k.wfcol[:], k.wfcol[:], k.g1[:], None, ALU.mult))
            v.tensor_scalar(k.w1g[:], k.w1[:], k.g0[:], None, ALU.mult).then_inc(s.weights_scaled, 1)
            v.wait_ge(s.products, 1)
            link(v.tensor_tensor(k.w1b[:], k.w1b[:], k.bank[0][:, 0:D], ALU.add))
            v.memset(k.w1c[:], 0.0)
            link(v.memset(k.w2c[:], 0.0))
            for half in range(2):
                at = slice(half * D, (half + 1) * D)
                v.tensor_copy(k.w1c[at, half, 0:D], k.bank[1][at, 0:D])
                v.tensor_copy(k.w1c[at, half, D:2 * D], k.bank[3][at, 0:D])
                v.tensor_copy(k.w2c[at, half, 0:D], k.bank[3][at, 0:D])
                v.tensor_copy(k.w2c[at, half, D:D + 1], k.bank[2][at, 0:1])
            link(v.tensor_tensor(k.beta1[:], k.beta1[:], k.wf[:], ALU.mult))
            link(v.tensor_reduce(k.pidx2[:], k.beta1[:], AX, ALU.add))
            link(v.tensor_tensor(k.wfb[:], k.wfb[:], k.pidx2[:], ALU.add))
            link(v.tensor_tensor(k.b3[:], k.b3[:], k.b3n[:], ALU.add))
            link(v.memset(k.nstat[:], 0.0))
            link(v.memset(k.pidx2[:], 0.0))
            link.end()

        @block.tensor
        def _(pe):
            pe.wait_ge(s.weights_scaled, 1)
            pe.matmul(k.bank[0][:, 0:D], k.beta0w[:], k.w1[:], start=True, stop=True)
            centre = k.centre[:].rearrange("p a d -> p (a d)")
            pe.matmul(k.bank[1][:, 0:D], centre, k.w1g[:], start=True, stop=True)
            pe.matmul(k.bank[3][:, 0:D], centre, k.ident[0:D, 0:D], start=True, stop=True)
            pe.matmul(k.bank[2][:, 0:1], centre, k.wfcol[:], start=True, stop=True).then_inc(s.products, 1)


def norm_vector(v, k, z, link, s, n):
    nb = z.NBK
    link(v.tensor_reduce(k.nstat[:, 0, :], k.x[:], AX, ALU.add))
    link(v.scalar_tensor_tensor(k.hbuf, over_features(k.nstat[:, 0, :]), -1.0 / D, k.x[:], ALU.mult, ALU.add))
    link(v.tensor_tensor(k.tab[:, :, 0:D], k.hbuf, k.hbuf, ALU.mult))
    link(v.tensor_reduce(k.nstat[:, 1, :], k.tab[:, :, 0:D], AX, ALU.add))
    v.tensor_scalar(k.nstat[:, 2, :], k.nstat[:, 1, :], 1.0 / D, EPS_NODE, ALU.mult, ALU.add).then_inc(s.nvar_done, 1)
    v.wait_ge(s.nsqrt_done, n + 1)
    link(v.reciprocal(k.nstat[:, 1, :], k.nstat[:, 0, :]))
    link(v.scalar_tensor_tensor(k.hbuf, k.hbuf, 0.0, over_features(k.nstat[:, 1, :]), ALU.max, ALU.mult))


def norm_scalar(a, k, s, n):
    a.wait_ge(s.nvar_done, n + 1)
    a.activation(k.nstat[:, 0, :], k.nstat[:, 2, :], ACT.Sqrt).then_inc(s.nsqrt_done, 1)


def rank_edges(v, k, z, key, n):
    s, cc = k.s1, z.C // CH
    rank_link = s.rank_link[key]
    link = Links(v, rank_link, 13 + (2 if key == DST else 0) + 2 * z.SJ + z.NBUCK + CH * 3 * z.NBUCK)
    link.run(0)
    o = k.order[key]
    link(v.tensor_scalar(o.pos_int[:], o.key_int[:], 7, None, ALU.logical_shift_right))
    link(v.tensor_copy(k.hi[:], o.pos_int[:]))
    first = link.start + link.n
    with v.Fori(0, z.NBUCK) as b:
        v.tensor_scalar(k.same[:], k.hi[:], k.iota[:, ds(b, 1)], None, ALU.is_equal, ALU.add,
                        accum_out=k.cnt[:, ds(b, 1)]).then_inc(rank_link, 1)
        v.wait_ge(rank_link, first + b + 1)
    link.n += z.NBUCK
    v.tensor_copy(k.cnt2[:], k.cnt[:]).then_inc(s.counted, 1)
    v.wait_ge(s.count_sums, n + 1)
    nb = z.NBUCK
    low, tot = k.bank[0][:, 0:nb], k.bank[1][:, 0:nb]
    link(v.tensor_copy(k.tot[:], tot))
    link(v.tensor_tensor_scan(k.goff[:], k.tot[:], k.tot[:], -1.0, ALU.add, ALU.bypass))
    link(v.tensor_tensor(k.goff[:], k.goff[:], k.tot[:], ALU.subtract))
    link(v.tensor_tensor(k.base[:], k.goff[:], low, ALU.add))
    link(v.tensor_scalar(k.nst_int[:], k.tot[:], float(P - 1), None, ALU.add))
    link(v.tensor_scalar(k.nst_int[:], k.nst_int[:], 7, None, ALU.logical_shift_right))
    link(v.tensor_copy(k.nst[:], k.nst_int[:]))
    link(v.tensor_tensor_scan(k.send[:], k.nst[:], k.nst[:], 0.0, ALU.add, ALU.bypass))
    if key == DST:
        link(v.tensor_scalar(k.lead[:], k.nst[:], 1.0, None, ALU.min))
        link(v.tensor_tensor(k.lasts[:], k.lead[0:1, :], k.send[0:1, :], ALU.mult))
    link(v.tensor_tensor(k.lead[:], k.send[:], k.nst[:], ALU.subtract))
    link(v.scalar_tensor_tensor(k.lead[:], k.lead[:], float(-P), k.goff[:], ALU.mult, ALU.add))
    last = z.NB - 1
    link(v.tensor_tensor(k.jump[:, 0:last], k.lead[:, 1:z.NB], k.lead[:, 0:last], ALU.subtract))
    v.wait_ge(s.step_no_done, 1)
    for j in range(z.SJ):
        link(v.tensor_scalar(k.ended[:, 0:last], k.send[:, 0:last], k.step_no[:, j:j + 1], None, ALU.is_le, ALU.add,
                             accum_out=k.blk[:, j:j + 1]))
        link(v.tensor_tensor_reduce(k.ended2[:, 0:last], k.ended[:, 0:last], k.jump[:, 0:last], 1.0, 0.0, ALU.mult,
                                    ALU.add, k.off[:, j:j + 1]))
    v.scalar_tensor_tensor(k.off2[:], k.step_no[:], float(P), k.off[:], ALU.mult, ALU.add).then_inc(s.off_sum, 1)
    v.wait_ge(s.off_sum, n + 1)
    if n:
        v.wait_ge(s.tables_out[DST], 48)
    v.tensor_scalar(k.off_int[:], k.off2[:], float(z.E), None, ALU.min)
    v.tensor_copy(k.blk_int[:], k.blk[:])
    v.tensor_scalar(k.blk128[:], k.blk[:], float(P), None, ALU.mult).then_inc(s.tables_done, 1)
    for part in range(CH):
        cols = slice(part * cc, (part + 1) * cc)
        at = link.start + link.n
        with v.Fori(0, z.NBUCK) as b:
            v.tensor_scalar(k.same[:, 0:cc], k.hi[:, cols], k.iota[:, ds(b, 1)], None, ALU.is_equal).then_inc(rank_link, 1)
            v.wait_ge(rank_link, at + 3 * b + 1)
            v.tensor_tensor_scan(k.run[:], k.same[:, 0:cc], k.same[:, 0:cc], k.base[:, ds(b, 1)], ALU.add,
                                 ALU.bypass).then_inc(rank_link, 1)
            after(v, rank_link, at + 3 * b + 2, alone=True)
            v.tensor_copy(k.base[:, ds(b, 1)], k.run[:, cc - 1:cc])
            v.copy_predicated(o.pos_int[:, cols], k.same[:, 0:cc], k.run[:]).then_inc(rank_link, 1)
            v.wait_ge(rank_link, at + 3 * b + 3)
        link.n += 3 * z.NBUCK
        v.tensor_copy(k.pidx2[:], k.pidx[:]).then_inc(s.ranked[key], 1)
    link.end()


def sort_and_project(nc, io, z, k):
    s, NG25 = k.s1, z.NBK // G
    units = z.C // SC

    with nc.Block() as block:
        @block.sync
        def _(sp):
            sp.dma_start(k.x[:], io.x.rearrange("(b p) d -> p b d", p=P)).then_inc(s.x_loaded, 16)
            sp.dma_start(k.order[DST].key_int[:], io.dst.rearrange("(p c) -> p c", p=P)).then_inc(s.dst_loaded, 16)
            sp.dma_start(k.order[SRC].key_int[:], io.src.rearrange("(p c) -> p c", p=P)).then_inc(s.src_loaded, 16)
            sp.dma_start(k.w, io.w.rearrange("(p c) -> p c", p=P)).then_inc(s.w_loaded, 16)

            def tables_to_dram(n, key):
                sp.wait_ge(s.tables_done, n + 1)
                for tile, dram in ((k.off_int, k.off_dram), (k.blk_int, k.blk_dram), (k.blk128, k.b128_dram)):
                    sp.dma_start(dram[key].rearrange("(p j) -> p j", p=P), tile[:]).then_inc(s.tables_out[key], 16)
                sp.wait_ge(s.tables_out[key], 48)
                sp.dma_start(k.offs[key], k.off_dram[key].partition_broadcast(1)).then_inc(s.tables_in, 16)
                sp.dma_start(k.blks[key][:, 1:P * z.SJ + 1], k.blk_dram[key].partition_broadcast(1)).then_inc(s.tables_in, 16)

            tables_to_dram(0, DST)
            sp.wait_ge(s.xl_done, NG25)
            sp.dma_start(k.xl_dram.rearrange("(b p) d -> p b d", p=P), k.hbuf).then_inc(s.xl_out, 16)
            attr = io.attr.rearrange("(p c) f -> p c f", p=P)

            def load_attr(it, half):
                u = 2 * it + half
                after(sp, s.staged, u - 1)
                sp.dma_start(k.attr_in[:, half], attr[:, ds(u * SC, SC), :]).then_inc(s.attr_loaded[half], 16)

            for half in range(2):
                load_attr(0, half)
            with sp.Fori(1, units // 2) as it:
                for half in range(2):
                    load_attr(it, half)
            tables_to_dram(1, SRC)
            sp.wait_ge(s.tables_in, 64)
            sp.wait_ge(s.xl_out, 16)

        @block.scalar
        def _(a):
            norm_scalar(a, k, s, 0)
            a.wait_ge(s.norm_done, 1)

            def project(i):
                a.activation(k.hs[:], k.hbuf[:, ds(i * G, G), :], ACT.Copy).then_inc(s.hs_done, 1)
                a.wait_ge(s.hsT_done, i + 1)
                a.activation(k.hTn[:], k.bank[6][0:D, :], ACT.Copy).then_inc(s.hT_done, 1)
                after(a, s.proj_done, i + 1, alone=True)
                pr = k.bank[0].rearrange("p (g d) -> p g d", g=G)
                a.activation(k.hbuf[:, ds(i * G, G), :], pr[:, :, 0:D], ACT.Copy)
                a.activation(k.tab[:, ds(i * G, G), 0:D], pr[:, :, D:2 * D], ACT.Copy).then_inc(s.xl_done, 1)

            with a.Fori(0, NG25) as i:
                project(i)

            def stage(key, n, it, half):
                u = 2 * it + half
                cols = ds(u * SC, SC)
                o, other = k.order[key], k.order[1 - key]
                rec = k.rec[:, half]
                after(a, s.scattered[half], 16 * SC * (it + n * (units // 2)))
                if key == DST:
                    a.wait_ge(s.attr_loaded[half], 16 * (it + 1))
                    a.activation(rec[:, :, 2:RECD], k.attr_in[:, half], ACT.Copy)
                else:
                    a.activation(rec[:, :, 2], k.w[:, cols], ACT.Copy)
                a.activation(rec[:, :, 0].bitcast(I32), other.key_int[:, cols], ACT.Copy)
                a.activation(rec[:, :, 1], o.key_int[:, cols], ACT.Copy)
                a.activation(k.pos_st[:, half], o.pos_int[:, cols], ACT.Copy).then_inc(s.staged, 1)

            def stage_all(key, n):
                per = units // 2 // CH
                for part in range(CH):
                    a.wait_ge(s.ranked[key], part + 1)
                    if part == 0:
                        for half in range(2):
                            stage(key, n, 0, half)
                    with a.Fori(max(part * per, 1), (part + 1) * per) as it:
                        for half in range(2):
                            stage(key, n, it, half)

            a.wait_ge(s.src_loaded, 16)
            a.wait_ge(s.dst_loaded, 16)
            stage_all(DST, 0)
            a.wait_ge(s.w_loaded, 16)
            stage_all(SRC, 1)

        @block.tensor
        def _(pe):
            def project(i):
                after(pe, s.hs_done, i + 1, alone=True)
                for g in range(G):
                    last = pe.transpose(k.bank[6][0:D, g * P:(g + 1) * P], k.hs[:, g, :], k.ident[:])
                last.then_inc(s.hsT_done, 1)
                pe.wait_ge(s.hT_done, i + 1)
                for g in range(G):
                    last = pe.matmul(k.bank[0][:, g * P:(g + 1) * P], k.hTn[:, g * P:(g + 1) * P], k.wlr[:],
                                     start=True, stop=True)
                last.then_inc(s.proj_done, 1)

            with pe.Fori(0, NG25) as i:
                project(i)

            def count_sums(n):
                pe.wait_ge(s.counted, n + 1)
                pe.matmul(k.bank[0][:, 0:z.NBUCK], k.before[:], k.cnt2[:], start=True, stop=True)
                pe.matmul(k.bank[1][:, 0:z.NBUCK], k.ones[:], k.cnt2[:], start=True, stop=True).then_inc(s.count_sums, 1)

            pe.wait_ge(s.xl_done, NG25)
            count_sums(0)
            count_sums(1)

        @block.vector
        def _(v):
            link = Links(v, s.nlink, 11)
            link.run(0)
            v.wait_ge(s.x_loaded, 16)
            norm_vector(v, k, z, link, s, 0)
            v.tensor_copy(k.pidx2[:], k.pidx[:]).then_inc(s.norm_done, 1)
            v.wait_ge(s.dst_loaded, 16)
            rank_edges(v, k, z, DST, 0)
            v.wait_ge(s.xl_done, NG25)
            low, tmp = k.acc[:, :, 0:D], k.tab[:, :, D:2 * D]
            link(v.tensor_tensor(low, k.hbuf, k.tab[:, :, 0:D], ALU.add))
            link(v.scalar_tensor_tensor(tmp, low, 0.2, low, ALU.mult, ALU.max))
            link(v.tensor_tensor(low, tmp, rows_of(k.attw[:], z.NBK), ALU.mult))
            link(v.tensor_reduce(k.eself[:], low, AX, ALU.add))
            link(v.memset(k.acc[:], 0.0))
            link.end()
            v.wait_ge(s.src_loaded, 16)
            rank_edges(v, k, z, SRC, 1)

        @block.gpsimd
        def _(pool):
            pool.iota(k.step_no[:], [[1, z.SJ]], base=0, channel_multiplier=z.SJ,
                      allow_small_or_imprecise_dtypes=True).then_inc(s.step_no_done, 1)

            def scatter(key, it, half, n):
                u = 2 * it + half
                dram, width = (k.recd_dram, RECD) if key == DST else (k.recs_dram, RECS)
                after(pool, s.staged, n * units + u + 1, alone=True)
                for c in range(SC):
                    pool.indirect_dma_start(
                        dram, bass.IndirectOffsetOnAxis(ap=k.pos_st[:, half, c:c + 1].bitcast(U32), axis=0),
                        k.rec[:, half, c, 0:width], None).then_inc(s.scattered[half], 16)

            for n, key in ((0, DST), (1, SRC)):
                with pool.Fori(0, units // 2) as it:
                    for half in range(2):
                        scatter(key, it, half, n)
            for half in range(2):
                pool.wait_ge(s.scattered[half], 16 * SC * units)


def softmax_edges(nc, z, k, layer):
    s, bank, mlp = k.s, k.bank, layer == 2
    first = k.first
    e_done, e0 = (s.logit_done, first) if mlp else (s.e_done, 0)
    table, width = (k.a2_dram, 2 * D) if mlp else (k.xl_dram, D)
    columns = slice(2 * D - width, 2 * D)
    negT_p = bank[1].bitcast(BF16)[:, 0:G * P].rearrange("p (g n) -> p g n", g=G)
    atT_p = bank[1][0:G * RECD, 3 * P:4 * P]
    mx_p = bank[2].rearrange("p (g n) -> p g n", g=G)
    sum_p = bank[3][:, 0:G * (D + 1)].rearrange("p (g d) -> p g d", g=G)
    me_p = (bank[3] if mlp else bank[4])[:, 3 * P:3 * P + G]

    def z_p(two):
        return bank[0 if mlp else 5 + two][:, 0:G * width]

    def loaded(g):
        return 16 * G * g.use

    with nc.Block() as block:
        @block.sync
        def _(sp):
            sp.dma_start(k.b128[:], k.b128_dram[DST].partition_broadcast(P)).then_inc(s.table_in, 16)

            def load_windows(g):
                after(sp, s.s_done, g.c - R + 1)
                at = table_values(nc, mybir.EngineType.SP, k.offs[DST], g.n * G, G, z.E)
                for i, off in enumerate(at):
                    sp.dma_start(k.win[:, g.at, i, :], k.recd_dram[ds(off, P), :]).then_inc(s.win_loaded[g.at], 16)
            pipelined(sp, z, layer, [((0,), load_windows)])

        @block.gpsimd
        def _(pool):
            def gather(g):
                after(pool, s.s_done, g.c - R + 1, alone=True)
                after(pool, s.win_loaded[g.at], loaded(g), alone=True)
                for i in range(G):
                    pool.indirect_dma_start(
                        k.rows[:, g.at, i, columns], None, table,
                        bass.IndirectOffsetOnAxis(ap=k.win[:, g.at, i, 0:1].bitcast(U32), axis=0)
                    ).then_inc(s.gathered[g.at], 16)
            pipelined(pool, z, layer, [((0,), gather)])

        @block.scalar
        def _(a):
            def mask_logits(g):
                after(a, e_done, e0 + g.n + 1)
                after(a, s.ehT_done, g.c - 3)
                after(a, s.ph_done, g.c - 3)
                for i in range(G):
                    last = a.activation(k.eh[:, g.at % 4, i, :], k.neg[:, g.at, i, :], ACT.Identity,
                                        bias=k.e[:, g.at, i:i + 1])
                last.then_inc(s.eh_done, 1)

            def copy_one_hots(g):
                after(a, s.negT_done, g.c + 1)
                after(a, s.me_done, g.c - R + 1)
                if mlp:
                    after(a, s.z_done, g.c)
                    a.activation(k.atT[:], atT_p, ACT.Copy)
                a.activation(k.hotT[:, g.at], negT_p, ACT.Copy, scale=-1.0 / NEG, bias=1.0).then_inc(s.hotT_done, 1)

            def exp_peaks(g):
                after(a, s.dd_done, g.c + 1)
                after(a, s.sum_link, G * (g.c - 1))
                a.activation(k.cc[:, g.two], k.dd[:, g.two], ACT.Exp).then_inc(s.cc_done, 1)

            def exp_logits(g):
                after(a, s.nme_done, g.c + 1)
                after(a, s.s_done, g.c - 1)
                after(a, s.eh_done, g.c + 1)
                for i in range(G):
                    last = a.activation(k.ph[:, g.two, i, :], k.eh[:, g.at % 4, i, :], ACT.Exp,
                                        bias=k.nme[:, g.two, i:i + 1])
                last.then_inc(s.ph_done, 1)

            if mlp:
                pipelined(a, z, layer, [
                    ((1,), lambda g: mlp_h0(a, k, k.rows[:, g.at, :, 0:D], g.two, first + g.n, z_kept=True)),
                    ((2,), lambda g: mlp_h1(a, k, first + g.n)), ((1,), lambda g: mlp_copy(a, k, 0, first + g.n)),
                    ((2,), lambda g: mlp_copy(a, k, 1, first + g.n)), ((1,), lambda g: mlp_square0(a, k, first + g.n)),
                    ((2,), lambda g: mlp_square1(a, k, first + g.n)), ((0,), copy_one_hots), ((3,), exp_logits),
                    ((2,), mask_logits), ((3,), exp_peaks)])
            else:
                pipelined(a, z, layer, [((6,), exp_peaks), ((5,), exp_logits), ((0,), copy_one_hots), ((2,), mask_logits)])

        @block.tensor
        def _(pe):
            def sums(g):
                pe.wait_ge(s.ones_set, 1)
                after(pe, s.ph_done, g.c + 1, alone=True)
                after(pe, s.ts_done, g.c, alone=True)
                for i in range(G):
                    last = pe.matmul(sum_p[:, i, :], k.ph[:, g.two, i, :], k.rows[:, g.at, i, D:2 * D + 1], start=True, stop=True)
                last.then_inc(s.s_done, 1)

            def turn_one_hots(g):
                after(pe, s.neg_done, g.c + 1, alone=True)
                after(pe, s.hotT_done, g.c, alone=True)
                for i in range(G):
                    last = pe.transpose(negT_p[:, i, :], k.neg[:, g.at, i, :], k.identb[:])
                if mlp:
                    last = pe.transpose(atT_p, k.win[:, g.at].rearrange("p g c -> p (g c)"), k.ident[:])
                last.then_inc(s.negT_done, 1)

            def turn_logits(g):
                after(pe, s.eh_done, g.c + 1, alone=True)
                after(pe, s.ms_done, g.c, alone=True)
                for i in range(G):
                    last = pe.transpose(mx_p[:, i, :], k.eh[:, g.at % 4, i, :], k.ident[:])
                last.then_inc(s.ehT_done, 1)

            blocks = []

            def load_blocks(g):
                blocks[:] = table_values(nc, mybir.EngineType.PE, k.blks[DST], g.n * G + 1, G, z.NB - 1)

            def add_rows(g):
                zp = z_p(g.two).rearrange("p (g d) -> p g d", g=G)
                if mlp:
                    after(pe, s.z_kept, g.c - z.NG, alone=True)
                else:
                    after(pe, s.z_added, g.c - 1, alone=True)
                after(pe, s.hotT_done, g.c + 1, alone=True)
                if mlp:
                    pe.matmul(z_p(0), k.atT[:], k.wqe4[:], start=True, stop=False, skip_group_check=True)
                for i, b in enumerate(blocks):
                    last = pe.matmul(zp[:, i, :], k.hotT[:, g.at, i, :],
                                     k.tab[:, ds(b, 1), 0:width].rearrange("p a d -> p (a d)"),
                                     start=not mlp, stop=(not mlp or i == G - 1), skip_group_check=True)
                last.then_inc(s.z_done, 1)

            def peaks_of_edges(g):
                after(pe, s.ms_done, g.c + 1, alone=True)
                after(pe, s.nme_done, g.c, alone=True)
                if mlp:
                    after(pe, s.ts_done, g.c, alone=True)
                for i in range(G):
                    last = pe.matmul(me_p[:, i:i + 1], k.hotT[:, g.at, i, :], k.ms[:, g.two, i:i + 1],
                                     start=True, stop=True)
                last.then_inc(s.me_done, 1)

            if mlp:
                pipelined(pe, z, layer, [
                    ((4,), sums), ((3,), turn_logits), ((1,), lambda g: mlp_turn0(pe, k, g.two, first + g.n)),
                    ((2,), lambda g: mlp_turn1(pe, k, first + g.n)), ((1,), lambda g: mlp_first(pe, k, first + g.n)),
                    ((0,), load_blocks), ((2,), lambda g: mlp_second(pe, k, first + g.n)), ((0,), turn_one_hots),
                    ((3,), peaks_of_edges), ((0,), add_rows)])
            else:
                pipelined(pe, z, layer, [
                    ((0,), turn_one_hots), ((6,), sums), ((1,), load_blocks), ((3,), turn_logits), ((1,), add_rows),
                    ((4,), peaks_of_edges)])

        @block.vector
        def _(v):
            start = Links(v, s.start_link, 4)
            start.run(layer // 2)
            if layer == 0:
                v.memset(k.rows[:, :, :, 2 * D:2 * D + 1], 1.0).then_inc(s.ones_set, 1)
            link = Links(v, s.peak_link, 2)
            v.wait_ge(s.table_in, 16 * (layer + 1))
            start(v.tensor_tensor(k.fresh[:, 1:z.STEPS], k.b128[:, 1:z.STEPS], k.b128[:, 0:z.STEPS - 1], ALU.not_equal))
            start(v.tensor_scalar(k.fresh[:, 1:z.STEPS], k.fresh[:, 1:z.STEPS], NEG, None, ALU.mult))
            start(v.memset(k.fresh[:, 0:1], NEG))
            start(v.memset(k.peak[:, 0:1], NEG))

            blocks = []

            def load_blocks(g):
                blocks[:] = table_values(nc, mybir.EngineType.DVE, k.blks[DST], g.n * G, G + 1, z.NB - 1)

            def add_sums_and_one_hots(old, new):
                if new:
                    after(v, s.win_loaded[new.at], loaded(new))
                    v.tensor_tensor(k.lo[:, new.two], k.win[:, new.at, :, 1], k.b128[:, ds(new.n * G, G)],
                                    ALU.subtract).then_inc(s.lo_done, 1)
                if old:
                    nodes = [k.acc[:, ds(b, 1), :].rearrange("p a d -> p (a d)") for b in blocks]
                    after(v, s.cc_done, old.c + 1)
                    after(v, s.s_done, old.c + 1)
                    after(v, s.sum_link, old.c * G)
                    v.tensor_tensor(k.ts[:], sum_p, over_features(k.cc[:, old.two, 1], D + 1), ALU.mult).then_inc(s.ts_done, 1)
                if new:
                    after(v, s.lo_done, new.c + 1)
                    after(v, s.eh_done, new.c - R + 1)
                if old:
                    after(v, s.ts_done, old.c + 1)
                for i in range(G):
                    if old:
                        if i:
                            after(v, s.sum_link, old.c * G + i)
                        v.scalar_tensor_tensor(nodes[i + 1], nodes[i], k.cc[:, old.two, 0, i:i + 1], k.ts[:, i, :],
                                               ALU.mult, ALU.add).then_inc(s.sum_link, 1)
                    if new:
                        mask = v.tensor_scalar(k.neg[:, new.at, i, :], k.iotab[:], k.lo[:, new.two, i:i + 1], NEG,
                                               ALU.not_equal, ALU.mult)
                if new:
                    mask.then_inc(s.neg_done, 1)

            def logits(g):
                after(v, s.gathered[g.at], loaded(g))
                after(v, s.z_done, g.c + 1)
                t = k.tmp[:].rearrange("p (g d) -> p g d", g=G)
                v.tensor_tensor(t, z_p(g.two).rearrange("p (g d) -> p g d", g=G), k.rows[:, g.at, :, columns],
                                ALU.add).then_inc(s.z_added, 1)
                after(v, s.z_added, g.c + 1)
                v.scalar_tensor_tensor(k.lr[:], k.tmp[:], 0.2, k.tmp[:], ALU.mult, ALU.max).then_inc(s.lr_done, 1)
                after(v, s.lr_done, g.c + 1)
                v.tensor_tensor(t, k.lr[:].rearrange("p (g d) -> p g d", g=G), rows_of(k.attw[:], G),
                                ALU.mult).then_inc(s.att_done, 1)
                after(v, s.att_done, g.c + 1)
                v.tensor_reduce(k.e[:, g.at], t, AX, ALU.add).then_inc(s.e_done, 1)

            def peaks(g):
                link.run(g.c)
                after(v, s.ehT_done, g.c + 1)
                after(v, s.me_done, g.c - 1)
                v.tensor_reduce(k.ms[:, g.two], mx_p, AX, ALU.max).then_inc(s.ms_done, 1)
                after(v, s.cc_done, g.c - 1)
                after(v, s.ms_done, g.c + 1)
                before, now = k.peak[:, ds(g.n * G, G)], k.peak[:, ds(g.n * G + 1, G)]
                fresh = k.fresh[:, ds(g.n * G, G)]
                link(v.tensor_tensor_scan(now, fresh, k.ms[:, g.two], k.peak[:, ds(g.n * G, 1)], ALU.add, ALU.max))
                link(v.tensor_tensor(k.dp[:], before, fresh, ALU.add))
                v.tensor_tensor(k.dd[:, g.two, 0], k.dp[:], now, ALU.subtract)
                v.tensor_tensor(k.dd[:, g.two, 1], k.ms[:, g.two], now, ALU.subtract).then_inc(s.dd_done, 1)

            def minus_peaks_of_edges(g):
                after(v, s.me_done, g.c + 1)
                after(v, s.ph_done, g.c - 1)
                v.tensor_scalar(k.nme[:, g.two], me_p, -1.0, None, ALU.mult).then_inc(s.nme_done, 1)

            def add_gathered(g):
                after(v, s.gathered[g.at], loaded(g))
                after(v, s.z_done, g.c + 1)
                v.tensor_tensor(k.rows[:, g.at, :, 0:2 * D], bank[0].rearrange("p (g d) -> p g d", g=G),
                                k.rows[:, g.at, :, 0:2 * D], ALU.add).then_inc(s.z_kept, 1)

            def rstds(g):
                past = isinstance(g.n, int) and g.n == z.NG
                mlp_rstd(v, k, 2 * first + g.n, (first + g.n + (0 if past else 1), first + g.n))

            if mlp:
                pipelined(v, z, layer, [
                    ((2,), lambda g: mlp_t(v, k, first + g.n)), ((1,), add_gathered), ((4,), load_blocks), ((4, 0), add_sums_and_one_hots),
                    ((3,), peaks), ((2,), lambda g: mlp_sums(v, k, 1, first + g.n)),
                    ((1,), lambda g: mlp_sums(v, k, 0, first + g.n)), ((3,), minus_peaks_of_edges),
                    ((1,), rstds, 1), ((2,), lambda g: mlp_logit(v, k, k.e[:, g.at], first + g.n))])
            else:
                pipelined(v, z, layer, [
                    ((7,), load_blocks), ((7, 0), add_sums_and_one_hots), ((4,), peaks), ((5,), minus_peaks_of_edges),
                    ((2,), logits)])


def sum_edges(nc, z, k, layer, table):
    s = k.s

    def loaded(g):
        return 16 * G * g.use

    def sum_p(g):
        return k.bank[g.two][:, 0:G * D].rearrange("p (g d) -> p g d", g=G)

    weighted = k.ph

    with nc.Block() as block:
        @block.sync
        def _(sp):
            sp.dma_start(k.b128[:], k.b128_dram[SRC].partition_broadcast(P)).then_inc(s.table_in, 16)

            def load_windows(g):
                after(sp, s.w_sum, g.c - R + 1)
                at = table_values(nc, mybir.EngineType.SP, k.offs[SRC], g.n * G, G, z.E)
                for i, off in enumerate(at):
                    sp.dma_start(k.win[:, g.at, i, 0:RECS], k.recs_dram[ds(off, P), :]).then_inc(s.win_loaded[g.at], 16)
            pipelined(sp, z, layer, [((0,), load_windows)])

        @block.gpsimd
        def _(pool):
            def gather(g):
                after(pool, s.w_sum, g.c - R + 1, alone=True)
                after(pool, s.win_loaded[g.at], loaded(g), alone=True)
                for i in range(G):
                    pool.indirect_dma_start(
                        k.rows[:, g.at, i, 0:D], None, table,
                        bass.IndirectOffsetOnAxis(ap=k.win[:, g.at, i, 0:1].bitcast(U32), axis=0)
                    ).then_inc(s.gathered[g.at], 16)
            pipelined(pool, z, layer, [((0,), gather)])

        @block.tensor
        def _(pe):
            def sums(g):
                after(pe, s.w_hot, g.c + 1, alone=True)
                after(pe, s.w_acc, g.c - 1, alone=True)
                after(pe, s.gathered[g.at], loaded(g), alone=True)
                for i in range(G):
                    last = pe.matmul(sum_p(g)[:, i, :], weighted[:, g.two, i, :], k.rows[:, g.at, i, 0:D],
                                     start=True, stop=True)
                last.then_inc(s.w_sum, 1)
            pipelined(pe, z, layer, [((1,), sums)])

        @block.vector
        def _(v):
            v.wait_ge(s.table_in, 16 * (layer + 1))

            def weigh(g):
                after(v, s.win_loaded[g.at], loaded(g))
                v.tensor_tensor(k.lo[:, g.two], k.win[:, g.at, :, 1], k.b128[:, ds(g.n * G, G)],
                                ALU.subtract).then_inc(s.w_lo, 1)
                after(v, s.w_lo, g.c + 1)
                after(v, s.w_sum, g.c - 1)
                for i in range(G):
                    last = v.tensor_scalar(weighted[:, g.two, i, :], k.iota[:], k.lo[:, g.two, i:i + 1],
                                           k.win[:, g.at, i, 2:3], ALU.is_equal, ALU.mult)
                last.then_inc(s.w_hot, 1)

            def add_sums(g):
                after(v, s.w_sum, g.c + 1)
                blocks = table_values(nc, mybir.EngineType.DVE, k.blks[SRC], g.n * G + 1, G, z.NB - 1)
                for i, b in enumerate(blocks):
                    node = k.acc[:, ds(b, 1), 0:D].rearrange("p a d -> p (a d)")
                    v.tensor_tensor(node, node, sum_p(g)[:, i, :], ALU.add).then_inc(s.w_acc1, 1)
                    v.wait_ge(s.w_acc1, g.c * G + i + 1)
                v.memset(k.pidx2[:], 0.0).then_inc(s.w_acc, 1)
            pipelined(v, z, layer, [((0,), weigh), ((2,), add_sums)])


def mlp_h0(a, k, z, two, m, z_kept=False):
    s = k.s
    if z_kept:
        after(a, s.z_kept, m - k.first + 1)
    after(a, s.hT_p_done[0], m - 1)
    a.activation(k.h0[:, two], z, ACT.Relu).then_inc(s.h0_done, 1)


def mlp_turn0(pe, k, two, m):
    s = k.s
    after(pe, s.h0_done, m + 1, alone=True)
    after(pe, s.hT_done[0], m, alone=True)
    for q in range(G // 2):
        last = pe.transpose(k.bank[4][:, q * P:(q + 1) * P], k.h0[:, two, 2 * q:2 * q + 2, :].rearrange("p g d -> p (g d)"),
                            k.ident[:])
    last.then_inc(s.hT_p_done[0], 1)


def mlp_copy(a, k, norm, m):
    s = k.s
    after(a, s.hT_p_done[norm], m + 1)
    after(a, (s.first_done, s.second_done)[norm], m)
    a.activation(k.hT[:, norm], k.bank[(4, 6)[norm]][:, 0:G // 2 * P], ACT.Copy).then_inc(s.hT_done[norm], 1)


def mlp_first(pe, k, m):
    s = k.s
    after(pe, s.hT_done[0], m + 1, alone=True)
    after(pe, s.t_done, m, alone=True)
    after(pe, s.sq_done[0], m, alone=True)
    for q in range(G // 2):
        last = pe.matmul(k.bank[5][:, q * 4 * D:(q + 1) * 4 * D], k.hT[:, 0, q * P:(q + 1) * P],
                         k.w1c[:].rearrange("p a d -> p (a d)"), start=True, stop=True)
    last.then_inc(s.first_done, 1)


def mlp_square0(a, k, m):
    s = k.s
    after(a, s.first_done, m + 1)
    after(a, s.ss_done[0], m)
    hc = k.bank[5].rearrange("p (g d) -> p g d", g=G)[:, :, D:2 * D]
    a.activation(k.sq[:, 0], hc, ACT.Square).then_inc(s.sq_done[0], 1)


def mlp_sums(v, k, norm, m):
    s = k.s
    after(v, s.sq_done[norm], m + 1)
    v.tensor_reduce(k.ss[:, norm], k.sq[:, norm], AX, ALU.add).then_inc(s.ss_done[norm], 1)


def mlp_rstd(v, k, n, sums):
    for norm in range(2):
        after(v, k.s.ss_done[norm], sums[norm])
    link = Links(v, k.s.newton_link, 12)
    link.run(n)
    r, rr, var = k.rstd[:], k.yy[:], k.var[:]
    link(v.tensor_scalar(var, k.ss[:], 1.0 / D, EPS_MLP, ALU.mult, ALU.add))
    link(v.tensor_scalar(rr.bitcast(I32), var.bitcast(I32), 1, None, ALU.logical_shift_right))
    link(v.tensor_scalar(r.bitcast(I32), rr.bitcast(I32), -1.0, float(0x5F3759DF), ALU.mult, ALU.add))
    for _ in range(3):
        link(v.tensor_tensor(rr, r, r, ALU.mult))
        link(v.scalar_tensor_tensor(rr, rr, -0.5, var, ALU.mult, ALU.mult))
        link(v.scalar_tensor_tensor(r, rr, 1.5, r, ALU.add, ALU.mult))
    link.end()


def mlp_t(v, k, m):
    s = k.s
    after(v, s.first_done, m + 1)
    after(v, s.h1_done, m)
    for g in range(G):
        last = v.scalar_tensor_tensor(k.t1[:, g, :], k.bank[5][:, g * P:g * P + D], k.rstd[:, 0, g:g + 1], k.w1b[:],
                                      ALU.mult, ALU.add)
    last.then_inc(s.t_done, 1)


def mlp_h1(a, k, m):
    s = k.s
    after(a, s.t_done, m + 1)
    after(a, s.hT_p_done[1], m)
    a.activation(k.h1[:], k.t1[:], ACT.Relu).then_inc(s.h1_done, 1)


def mlp_turn1(pe, k, m):
    s = k.s
    after(pe, s.h1_done, m + 1, alone=True)
    after(pe, s.hT_done[1], m, alone=True)
    for q in range(G // 2):
        last = pe.transpose(k.bank[6][:, q * P:(q + 1) * P], k.h1[:, 2 * q:2 * q + 2, :].rearrange("p g d -> p (g d)"),
                            k.ident[:])
    last.then_inc(s.hT_p_done[1], 1)


def mlp_second(pe, k, m):
    s = k.s
    after(pe, s.hT_done[1], m + 1, alone=True)
    after(pe, s.logit_done, m, alone=True)
    after(pe, s.sq_done[1], m, alone=True)
    for q in range(G // 2):
        last = pe.matmul(k.bank[7][:, 2 * q * (D + 1):2 * (q + 1) * (D + 1)], k.hT[:, 1, q * P:(q + 1) * P],
                         k.w2c[:].rearrange("p a d -> p (a d)"), start=True, stop=True)
    last.then_inc(s.second_done, 1)


def second_p(k):
    return k.bank[7][:, 0:G * (D + 1)].rearrange("p (g d) -> p g d", g=G)


def mlp_square1(a, k, m):
    s = k.s
    after(a, s.second_done, m + 1)
    after(a, s.ss_done[1], m)
    a.activation(k.sq[:, 1], second_p(k)[:, :, 0:D], ACT.Square).then_inc(s.sq_done[1], 1)


def mlp_logit(v, k, out, m):
    s = k.s
    after(v, s.second_done, m + 1)
    v.tensor_tensor(k.dot[:], second_p(k)[:, :, D], k.rstd[:, 1], ALU.mult).then_inc(s.dot_done, 1)
    after(v, s.dot_done, m + 1)
    v.tensor_scalar(out, k.dot[:], k.wfb[:], 0.0, ALU.add, ALU.max).then_inc(s.logit_done, 1)


def close_layer(nc, z, k, layer, table):
    s, n = k.s, layer
    with nc.Block() as block:
        @block.vector
        def _(v):
            link = Links(v, s.close_link[layer], {0: 10, 1: 1, 2: 10}[layer] + 6)
            link.run(0)
            if layer != 1:
                v.memset(k.top[:], NEG).then_inc(s.top_set, 1)
                v.wait_ge(s.top_set, layer // 2 + 1)
                some = max(m for m in range(1, 9) if z.NB % m == 0)
                with v.Fori(0, z.NB // some) as i:
                    lasts = table_values(nc, mybir.EngineType.DVE, k.lasts, i * some, some, z.STEPS)
                    for b, at in enumerate(lasts):
                        v.tensor_scalar(k.top[:, ds(i * some + b, 1)], k.peak[:, ds(at, 1)], 0.0, None,
                                        ALU.add).then_inc(s.top_done, 1)
                v.wait_ge(s.top_done, z.NB * (layer // 2 + 1))
                link(v.tensor_tensor(k.nstat[:, 2, :], k.top[:], k.eself[:], ALU.max))
                v.tensor_tensor(k.nstat[:, 0, :], k.top[:], k.nstat[:, 2, :], ALU.subtract)
                v.tensor_tensor(k.nstat[:, 1, :], k.eself[:], k.nstat[:, 2, :], ALU.subtract).then_inc(s.self_diff, 1)
                v.wait_ge(s.self_exp, layer // 2 + 1)
                c0, c1 = k.nstat[:, 0, :], k.nstat[:, 1, :]
                tmp, sums = k.tab[:, :, 0:D], k.acc[:, :, 0:D]
                link(v.tensor_tensor(k.acc[:], k.acc[:], over_features(c0, D + 1), ALU.mult))
                link(v.tensor_tensor(k.acc[:, :, D], k.acc[:, :, D], c1, ALU.add))
                v.wait_ge(s.own_in, 16 * (layer // 2 + 1))
                link(v.tensor_tensor(tmp, k.hbuf, over_features(c1), ALU.mult))
                link(v.tensor_tensor(sums, sums, tmp, ALU.add))
                link(v.reciprocal(k.nstat[:, 0, :], k.acc[:, :, D]))
                link(v.tensor_tensor(tmp, sums, over_features(k.nstat[:, 0, :]), ALU.mult))
            if layer == 0:
                link(v.tensor_tensor(k.x[:], k.x[:], tmp, ALU.add))
                link(v.tensor_tensor(k.x[:], k.x[:], rows_of(k.bias0[:], z.NBK), ALU.add))
            if layer == 1:
                link(v.tensor_tensor(k.x[:], k.x[:], k.acc[:, :, 0:D], ALU.add))
            if layer == 2:
                link(v.scalar_tensor_tensor(tmp, tmp, 0.01, tmp, ALU.mult, ALU.max))
                link(v.tensor_tensor(k.x[:], k.x[:], tmp, ALU.add))
            norm_vector(v, k, z, link, s, n)
            v.memset(k.acc[:], 0.0).then_inc(s.norm_done, 1)

        @block.scalar
        def _(a):
            if layer != 1:
                a.wait_ge(s.self_diff, layer // 2 + 1)
                a.activation(k.nstat[:, 0:2, :], k.nstat[:, 0:2, :], ACT.Exp).then_inc(s.self_exp, 1)
            norm_scalar(a, k, s, n)

        @block.sync
        def _(sp):
            if layer != 1:
                own = k.xl_dram if layer == 0 else k.q_dram
                sp.dma_start(k.hbuf, own.rearrange("(b p) d -> p b d", p=P)).then_inc(s.own_in, 16)
            if table is not None:
                sp.wait_ge(s.norm_done, n + 1)
                sp.dma_start(table.rearrange("(b p) d -> p b d", p=P), k.hbuf).then_inc(s.h_out, 16)
                sp.wait_ge(s.h_out, 16 if layer == 0 else 32)


def mlp_nodes(nc, z, k):
    s, groups, bank = k.s, z.NBK // G, k.bank
    dst = k.a2_dram.rearrange("(b p) d -> p b d", p=P)
    own = k.q_dram.rearrange("(b p) d -> p b d", p=P)
    a_st, b_st, zs = [k.rows[:, r, :, 0:2 * D] for r in range(3)]

    def grouped(b):
        return bank[b].rearrange("p (g d) -> p g d", g=G)

    with nc.Block() as block:
        @block.scalar
        def _(a):
            def group(i):
                a.activation(k.hs[:], k.hbuf[:, ds(i * G, G), :], ACT.Copy).then_inc(s.hs_done, 1)
                a.wait_ge(s.hsT_done, i + 1)
                a.activation(k.hTn[:], bank[3][0:D, :], ACT.Copy).then_inc(s.hTn_done, 1)
                a.wait_ge(s.ab_done, i + 1)
                after(a, s.a_out, 16 * i)
                a.activation(a_st, grouped(0), ACT.Copy).then_inc(s.a_done, 1)
                after(a, s.zs_done, i + 1, alone=True)
                a.activation(k.tab[:, ds(i * G, G), :], b_st, ACT.Copy).then_inc(s.b_kept, 1)
                mlp_h0(a, k, zs[:, :, 0:D], 0, i)
                mlp_copy(a, k, 0, i)
                mlp_square0(a, k, i)
                mlp_h1(a, k, i)
                mlp_copy(a, k, 1, i)
                mlp_square1(a, k, i)
            twice_counted(a, groups, group)

        @block.sync
        def _(sp):
            def group(i):
                sp.wait_ge(s.a_done, i + 1)
                sp.dma_start(dst[:, ds(i * G, G), :], a_st).then_inc(s.a_out, 16)
                sp.wait_ge(s.zs_done, i + 1)
                sp.dma_start(own[:, ds(i * G, G), :], zs[:, :, D:2 * D]).then_inc(s.q_out, 16)
            counted(sp, groups, group)
            sp.wait_ge(s.q_out, 16 * groups)
            sp.wait_ge(s.a_out, 16 * groups)

        @block.tensor
        def _(pe):
            def group(i):
                after(pe, s.hs_done, i + 1, alone=True)
                for g in range(G):
                    last = pe.transpose(bank[3][0:D, g * P:(g + 1) * P], k.hs[:, g, :], k.ident[:])
                last.then_inc(s.hsT_done, 1)
                after(pe, s.hTn_done, i + 1, alone=True)
                for b, w in ((0, k.wqa), (1, k.wqb)):
                    for g in range(G):
                        last = pe.matmul(bank[b][:, g * P:(g + 1) * P], k.hTn[:, g * P:(g + 1) * P], w[:],
                                         start=True, stop=True)
                last.then_inc(s.ab_done, 1)
                mlp_turn0(pe, k, 0, i)
                mlp_first(pe, k, i)
                mlp_turn1(pe, k, i)
                mlp_second(pe, k, i)
            counted(pe, groups, group)

        @block.vector
        def _(v):
            v.memset(k.ss[:], 1.0).then_inc(s.ss_set, 1)
            v.wait_ge(s.ss_set, 1)

            def group(i):
                v.wait_ge(s.a_done, i + 1)
                after(v, s.b_kept, i)
                v.tensor_tensor(b_st, grouped(1), rows_of(k.bq0[:], G), ALU.add).then_inc(s.b_done, 1)
                v.wait_ge(s.b_done, i + 1)
                after(v, s.q_out, 16 * i)
                v.tensor_tensor(zs, b_st, a_st, ALU.add).then_inc(s.zs_done, 1)
                for norm in range(2):
                    mlp_sums(v, k, norm, i)
                    mlp_rstd(v, k, 2 * i + norm, (i + 1, i + norm))
                    if norm == 0:
                        mlp_t(v, k, i)
                mlp_logit(v, k, k.eself[:, ds(i * G, G)], i)
            counted(v, groups, group)


def last_nodes(nc, io, z, k):
    s, groups = k.s, z.NBK // G
    full = z.N // P
    with nc.Block() as block:
        @block.scalar
        def _(a):
            a.wait_ge(s.own_in, 48)
            def group(i):
                for part, src in ((0, k.hbuf), (1, k.acc)):
                    n = 2 * i + part
                    a.activation(k.hs[:], src[:, ds(i * G, G), 0:D], ACT.Copy).then_inc(s.l_hs, 1)
                    a.wait_ge(s.l_hsT, n + 1)
                    a.activation(k.hTn[:], k.bank[6][0:D, :], ACT.Copy).then_inc(s.l_hT, 1)
                    a.wait_ge(s.l_y, n + 1)
            counted(a, groups, group)

        @block.tensor
        def _(pe):
            def group(i):
                for part in range(2):
                    n = 2 * i + part
                    after(pe, s.l_hs, n + 1, alone=True)
                    for g in range(G):
                        last = pe.transpose(k.bank[6][0:D, g * P:(g + 1) * P], k.hs[:, g, :], k.ident[:])
                    last.then_inc(s.l_hsT, 1)
                    after(pe, s.l_hT, n + 1, alone=True)
                    after(pe, s.l_x, i, alone=True)
                    for g in range(G):
                        last = pe.matmul(k.bank[part][:, g * D:(g + 1) * D], k.hTn[:, g * P:(g + 1) * P], k.w3[:, part, :],
                                         start=True, stop=True)
                    last.then_inc(s.l_y, 1)
            counted(pe, groups, group)

        @block.vector
        def _(v):
            link = Links(v, s.l_link, 2)
            def group(i):
                link.run(i)
                x = k.x[:, ds(i * G, G), :]
                y = [k.bank[b][:, 0:G * D].rearrange("p (g d) -> p g d", g=G) for b in range(2)]
                v.wait_ge(s.l_y, 2 * i + 2)
                link(v.tensor_tensor(x, x, y[0], ALU.add))
                link(v.tensor_tensor(x, x, y[1], ALU.add))
                v.tensor_tensor(x, x, rows_of(k.b3[:], G), ALU.add).then_inc(s.l_x, 1)
            counted(v, groups, group)

        @block.sync
        def _(sp):
            sp.dma_start(k.hbuf, k.h3_dram.rearrange("(b p) d -> p b d", p=P)).then_inc(s.own_in, 16)
            sp.wait_ge(s.l_x, groups)
            sp.dma_start(io.out[0:full * P, :].rearrange("(b p) d -> p b d", p=P), k.x[:, 0:full, :]).then_inc(s.out_done, 16)
            rest = z.N - full * P
            if rest:
                sp.dma_start(io.out[full * P:z.N, :], k.x[0:rest, full, :]).then_inc(s.out_done, 16)
            sp.wait_ge(s.out_done, 32 if rest else 16)


def build(nc, io, n, e):
    z = Sizes(n, e)
    NBK, NBUCK, C = z.NBK, z.NBUCK, z.C
    with ExitStack() as top:
        k = Place()
        k.first = NBK // G

        def sem(name):
            return top.enter_context(nc.semaphore(name))

        def sb(name, shape, dt=F32, ctx=top):
            return ctx.enter_context(nc.sbuf_tensor(name, shape, dt))

        def dram(name, shape, dt=F32):
            return nc.dram_tensor(name, shape, dt, kind="Internal").ap()

        k.xl_dram = dram("xl_dram", (NBK * P, D))
        k.h1_dram = dram("h1_dram", (NBK * P, D))
        k.q_dram = dram("q_dram", (NBK * P, D))
        k.h3_dram = dram("h3_dram", (NBK * P, D))
        k.a2_dram = dram("a2_dram", (NBK * P, 2 * D))
        k.recd_dram = dram("recd_dram", (z.EP, RECD))
        k.recs_dram = dram("recs_dram", (z.EP, RECS))
        k.off_dram = [dram(f"off{o}_dram", (P * z.SJ,), I32) for o in "ds"]
        k.blk_dram = [dram(f"blk{o}_dram", (P * z.SJ,), I32) for o in "ds"]
        k.b128_dram = [dram(f"b128{o}_dram", (P * z.SJ,), BF16) for o in "ds"]

        k.x = sb("x", [P, NBK, D])
        k.tab = sb("tab", [P, NBK, 2 * D])
        k.acc = sb("acc", [P, NBK, D + 1])
        k.top = sb("top", [P, NBK])
        k.eself = sb("eself", [P, NBK])
        half = R * G * P // 2
        shared = sb("shared", [P, max(NBK * D, 3 * half)])
        k.hbuf = shared[:, 0:NBK * D].rearrange("p (b d) -> p b d", d=D)
        k.neg = shared[:, 0:half].bitcast(BF16).rearrange("p (r g n) -> p r g n", r=R, g=G)
        k.hotT = shared[:, half:3 * half].rearrange("p (r g n) -> p r g n", r=R, g=G)
        k.nstat = sb("nstat", [P, 3, NBK])
        k.b128 = sb("b128", [P, P * z.SJ], BF16)
        k.fresh = sb("fresh", [P, z.STEPS], BF16)
        k.peak = sb("peak", [P, z.STEPS + 1])
        k.lasts = sb("lasts", [1, NBUCK], I32)
        k.steps = sb("steps", [4, P * z.SJ + 1], I32)
        k.offs = [k.steps[2 * o:2 * o + 1, 0:P * z.SJ] for o in (DST, SRC)]
        k.blks = [k.steps[2 * o + 1:2 * o + 2, :] for o in (DST, SRC)]
        k.ident = sb("ident", [P, P])
        k.identb = sb("identb", [P, P], BF16)
        k.iota = sb("iota", [P, P])
        k.pidx = sb("pidx", [P, 1])
        k.pidx2 = sb("pidx2", [P, 1])
        k.attw = sb("attw", [P, D])
        k.bias0 = sb("bias0", [P, D])
        k.wlr = sb("wlr", [D, 2 * D])
        k.wqa = sb("wqa", [D, 2 * D])
        k.wqb = sb("wqb", [D, 2 * D])
        k.wqe4 = sb("wqe4", [G * RECD, G, 2 * D])
        k.iotab = sb("iotab", [P, P], BF16)
        k.bq0 = sb("bq0", [P, 2 * D])
        k.w1c = sb("w1c", [P, 2, 2 * D])
        k.w2c = sb("w2c", [P, 2, D + 1])
        k.w1b = sb("w1b", [P, D])
        k.wfb = sb("wfb", [P, 1])
        k.w3 = sb("w3", [D, 2, D])
        k.b3 = sb("b3", [P, D])
        k.hs = sb("hs", [P, G, D])
        k.hTn = sb("hTn", [D, G * P])
        k.bank = [top.enter_context(nc.psum_tensor(f"bank{i}", [P, 512], F32)) for i in range(8)]

        with ExitStack() as early:
            k.w1 = sb("w1", [D, D], ctx=early)
            k.w1g = sb("w1g", [D, D], ctx=early)
            k.centre = sb("centre", [D, 2, D], ctx=early)
            k.g1 = sb("g1", [D, 1], ctx=early)
            k.wfcol = sb("wfcol", [D, 1], ctx=early)
            k.g0 = sb("g0", [D, 1], ctx=early)
            k.beta0 = sb("beta0", [D, 1], ctx=early)
            k.beta0w = sb("beta0w", [D, P], ctx=early)
            k.beta1 = sb("beta1", [P, D], ctx=early)
            k.wf = sb("wf", [P, D], ctx=early)
            k.b3n = sb("b3n", [P, D], ctx=early)
            k.before = sb("before", [P, P], ctx=early)
            k.ones = sb("ones", [P, P], ctx=early)
            k.csem = named(**{m: sem(m) for m in ("consts", "iota", "clink", "weights_scaled", "products", "wqe_clear", "wqe_in")})
            load_constants(nc, io, z, k)

            k.order = [named(
                key_int=sb(f"key_int{o}", [P, C], I32, early),
                pos_int=sb(f"pos_int{o}", [P, C], I32, early)) for o in "ds"]
            k.w = k.peak[:, 0:C]
            k.hi = sb("hi", [P, C], BF16, early)
            k.same = sb("same", [P, C], U8, early)
            k.run = sb("run", [P, C // CH], I32, early)
            (k.cnt, k.cnt2, k.tot, k.goff, k.base, k.nst, k.send, k.lead, k.jump, k.ended, k.ended2) = [
                sb(t, [P, NBUCK], ctx=early)
                for t in ("cnt", "cnt2", "tot", "goff", "base", "nst", "send", "lead", "jump", "ended", "ended2")]
            k.nst_int = sb("nst_int", [P, NBUCK], I32, early)
            k.step_no, k.blk, k.off, k.off2 = [
                sb(t, [P, z.SJ], ctx=early) for t in ("step_no", "blk", "off", "off2")]
            k.blk128 = sb("blk128", [P, z.SJ], BF16, early)
            k.off_int = sb("off_int", [P, z.SJ], I32, early)
            k.blk_int = sb("blk_int", [P, z.SJ], I32, early)
            k.attr_in = sb("attr_in", [P, 2, SC, EA], ctx=early)
            k.rec = sb("rec", [P, 2, SC, RECD], ctx=early)
            k.pos_st = sb("pos_st", [P, 2, SC], I32, early)
            k.s1 = named(
                rank_link=[sem("rank_link_dst"), sem("rank_link_src")],
                ranked=[sem("ranked_dst"), sem("ranked_src")], tables_out=[sem("tables_out_dst"), sem("tables_out_src")],
                attr_loaded=[sem("attr_loaded0"), sem("attr_loaded1")], scattered=[sem("scattered0"), sem("scattered1")],
                **{m: sem("first_" + m) for m in (
                    "counted", "count_sums", "off_sum", "tables_done", "tables_in", "x_loaded", "dst_loaded",
                    "src_loaded", "w_loaded", "xl_done", "xl_out", "staged", "norm_done", "hs_done", "hsT_done", "hT_done",
                    "proj_done", "nlink", "nvar_done", "nsqrt_done", "step_no_done")})
            sort_and_project(nc, io, z, k)

        k.win = sb("win", [P, R, G, RECD])
        k.rows = sb("rows", [P, R, G, 2 * D + 1])
        k.eh = sb("eh", [P, 4, G, P])
        k.ph = sb("ph", [P, 2, G, P])
        k.e = sb("e", [P, R, G])
        k.lo = sb("lo", [P, 2, G])
        k.tmp = sb("tmp", [P, G * D])
        k.lr = sb("lr", [P, G * D])
        k.ms = sb("ms", [P, 2, G])
        k.nme = sb("nme", [P, 2, G])
        k.dp = sb("dp", [P, G])
        k.dd = sb("dd", [P, 2, 2, G])
        k.cc = sb("cc", [P, 2, 2, G])
        k.ts = sb("ts", [P, G, D + 1])
        k.atT = sb("atT", [G * RECD, P])
        k.h0 = sb("h0", [P, 2, G, D])
        k.hT = sb("hT", [P, 2, G // 2 * P])
        k.sq = sb("sq", [P, 2, G, D])
        k.t1 = sb("t1", [P, G, D])
        k.h1 = sb("h1", [P, G, D])
        k.dot = sb("dot", [P, G])
        k.ss, k.var, k.yy, k.rstd = [sb(t, [P, 2, G]) for t in ("ss", "var", "yy", "rstd")]
        k.s = named(
            win_loaded=[sem(f"win_loaded{r}") for r in range(R)], gathered=[sem(f"gathered{r}") for r in range(R)],
            close_link=[sem(f"close_link{i}") for i in range(3)],
            **{m: [sem(m + "0"), sem(m + "1")] for m in (
                "hT_done", "hT_p_done", "sq_done", "ss_done")},
            **{m: sem(m) for m in (
                "table_in", "s_done", "eh_done", "ehT_done", "negT_done", "hotT_done", "z_done", "e_done", "z_added",
                "dd_done", "cc_done", "nme_done", "ph_done", "ts_done", "neg_done", "me_done", "ms_done", "ones_set",
                "start_link", "peak_link", "lo_done", "lr_done", "att_done", "sum_link",
                "w_sum", "w_hot", "w_acc", "w_acc1", "w_lo",
                "newton_link", "z_kept", "h0_done", "first_done", "t_done", "h1_done", "second_done", "dot_done", "logit_done",
                "own_in", "q_out", "ss_set", "top_set", "top_done", "self_diff", "self_exp", "nvar_done", "nsqrt_done", "norm_done", "h_out",
                "hs_done", "hsT_done", "hTn_done", "ab_done", "a_out", "a_done", "b_done", "zs_done", "b_kept",
                "l_hs", "l_hsT", "l_hT", "l_y", "l_x", "l_link", "out_done")})

        softmax_edges(nc, z, k, 0)
        close_layer(nc, z, k, 0, k.h1_dram)
        sum_edges(nc, z, k, 1, k.h1_dram)
        close_layer(nc, z, k, 1, None)
        mlp_nodes(nc, z, k)
        softmax_edges(nc, z, k, 2)
        close_layer(nc, z, k, 2, k.h3_dram)
        sum_edges(nc, z, k, 3, k.h3_dram)
        last_nodes(nc, io, z, k)


def kernel(**inputs):
    import numpy as _np
    import concourse.bacc as _bacc
    from concourse.bass_utils import run_bass_kernel_spmd as _run

    a = {name: _np.asarray(value) for name, value in inputs.items()}
    n, e = a["x"].shape[0], a["src"].shape[0]
    z = Sizes(n, e)
    nodes = (0, z.NBK * P - n)
    edges = (0, z.EP - e)
    laid = {
        "x": _np.pad(a["x"], (nodes, (0, 0))),
        "src": _np.pad(a["src"], edges, constant_values=z.PADKEY),
        "dst": _np.pad(a["dst"], edges, constant_values=z.PADKEY),
        "w": _np.pad(a["edge_weight"], edges),
        "attr": _np.pad(a["edge_attr_16"], (edges, (0, 0))),
        "W_l": a["L0_gnn_W_l"], "W_r": a["L0_gnn_W_r"], "att": a["L0_gnn_att"], "bias": a["L0_gnn_bias"],
        "Wq": a["L2_gnn_Wq"], "bq": a["L2_gnn_bq"], "W0": a["L2_gnn_W0"], "b0": a["L2_gnn_b0"],
        "g0": a["L2_gnn_g0"].reshape(D, 1), "beta0": a["L2_gnn_beta0"].reshape(D, 1),
        "W1": a["L2_gnn_W1"], "b1": a["L2_gnn_b1"], "g1": a["L2_gnn_g1"], "beta1": a["L2_gnn_beta1"],
        "Wf": a["L2_gnn_Wf"].reshape(D), "bf": a["L2_gnn_bf"],
        "W_selfT": a["L3_gnn_W_self"].T, "W_neighT": a["L3_gnn_W_neigh"].T,
        "b_self": a["L3_gnn_b_self"], "b_neigh": a["L3_gnn_b_neigh"],
    }
    nc = _bacc.Bacc("TRN2", target_bir_lowering=False, num_devices=1)
    arrays, tensors = {}, {}
    for name, value in laid.items():
        value = _np.ascontiguousarray(value)
        arrays[f"in_{name}"] = value
        t = nc.dram_tensor(f"in_{name}", value.shape, mybir.dt.from_np(value.dtype), kind="ExternalInput").ap()
        tensors[name] = t
    tensors["out"] = nc.dram_tensor("out", (n, D), F32, kind="ExternalOutput").ap()
    io = named(**tensors)
    build(nc, io, n, e)
    r = _run(nc, [arrays], core_ids=[0])
    return r.results[0]["out"]
```
